# Optimizing a Trainium2 kernel written in Bass

```python
import numpy as np
import jax
import jax.numpy as jnp

def _softmax(x, axis=-1):
    return jax.nn.softmax(x, axis=axis)

def _gelu(x):
    return jax.nn.gelu(x, approximate=True)

def _silu(x):
    return jax.nn.silu(x)

def _sigmoid(x):
    return jax.nn.sigmoid(x)

def _layernorm(x, axis=-1, eps=1e-05):
    m = jnp.mean(x, axis=axis, keepdims=True)
    v = jnp.var(x, axis=axis, keepdims=True)
    return (x - m) / jnp.sqrt(v + eps)

def _scatter_add(tgt, idx, src, axis=0):
    return tgt.at[idx].add(src)

def _segment_sum(src, seg, n):
    return jax.ops.segment_sum(src, seg, n)
kernel_name = 'mk_audio_tower_d1_tok_audfeat768_r4_255f29'

def setup_inputs(seed: int=0):
    np.random.seed(seed)
    _w = jnp.asarray

    def _rec_inputs():
        import jax
        import jax.numpy as jnp
        _rk = jax.random.key(seed)
        x = -0.000183583 + 0.999963 * jax.random.normal(jax.random.fold_in(_rk, 1), (16, 250, 192), jnp.float32)
        return x
    x = _rec_inputs()

    def _L0_tok_setup():
        import jax, jax.numpy as jnp
        import numpy as np
        KEEP_RATIO = 0.7
        LN_EPS = 1e-05
        key = jax.random.key(seed)
        k1, k2 = jax.random.split(key)
        B, N, D = (16, 2048, 192)
        x = jax.random.normal(k1, (B, N, D), dtype=jnp.float32)
        gamma = jnp.ones((D,), dtype=jnp.float32)
        beta = jnp.zeros((D,), dtype=jnp.float32)
        w = jax.random.normal(k2, (D,), dtype=jnp.float32) * (1.0 / np.sqrt(D))
        b = jnp.zeros((1,), dtype=jnp.float32)
        return {'x': x, 'gamma': gamma, 'beta': beta, 'w': w, 'b': b}
    _L0_tok_all = _L0_tok_setup()
    _L0_tok_in = {k: v for k, v in _L0_tok_all.items() if k in ('gamma', 'beta', 'w', 'b')}
    del _L0_tok_all

    def _L0_attn_setup():
        import jax, jax.numpy as jnp
        import numpy as np
        NH, DK, DV, D = (8, 64, 64, 192)
        DECAY = 0.95
        WRITE_STRENGTH = 0.1
        key = jax.random.key(seed)
        ks = jax.random.split(key, 6)
        s = 0.02
        return {'x': jax.random.normal(ks[0], (4, 1024, D), dtype=jnp.float32), 'w_key': jax.random.normal(ks[1], (NH * DK, D), dtype=jnp.float32) * s, 'w_value': jax.random.normal(ks[2], (NH * DV, D), dtype=jnp.float32) * s, 'w_query': jax.random.normal(ks[3], (NH * DK, D), dtype=jnp.float32) * s, 'w_gate': jax.random.normal(ks[4], (NH, D), dtype=jnp.float32) * s, 'w_out': jax.random.normal(ks[5], (D, NH * DV), dtype=jnp.float32) * s}
    _L0_attn_all = _L0_attn_setup()
    _L0_attn_in = {k: v for k, v in _L0_attn_all.items() if k in ('w_key', 'w_value', 'w_query', 'w_gate', 'w_out')}
    del _L0_attn_all

    def _L0_ffn_setup():
        import jax, jax.numpy as jnp
        import numpy as np
        HID = 192
        NQ = 12
        NKV = 3
        HD = 64
        REP = NQ // NKV
        E = 16
        TOPK = 2
        FF = 384
        EPS = 1e-06
        THETA = 10000.0

        def rms_norm(x, w):
            return x / jnp.sqrt(jnp.mean(x * x, axis=-1, keepdims=True) + EPS) * w

        def rope_tables(seq_len):
            inv = 1.0 / THETA ** (jnp.arange(0, HD, 2, dtype=jnp.float32) / HD)
            f = jnp.arange(seq_len, dtype=jnp.float32)[:, None] * inv[None, :]
            return (jnp.cos(f), jnp.sin(f))

        def apply_rope(t, cos, sin):
            B, S, H, _ = t.shape
            tr = t.reshape(B, S, H, HD // 2, 2)
            c = cos[None, :, None, :]
            s = sin[None, :, None, :]
            r0 = tr[..., 0] * c - tr[..., 1] * s
            r1 = tr[..., 0] * s + tr[..., 1] * c
            return jnp.stack([r0, r1], axis=-1).reshape(B, S, H, HD)

        def attention(x, w_qkv, w_out):
            B, S, _ = x.shape
            qkv = x @ w_qkv
            q, k, v = jnp.split(qkv, [NQ * HD, (NQ + NKV) * HD], axis=-1)
            q = q.reshape(B, S, NQ, HD)
            k = k.reshape(B, S, NKV, HD)
            v = v.reshape(B, S, NKV, HD)
            cos, sin = rope_tables(S)
            q = apply_rope(q, cos, sin)
            k = apply_rope(k, cos, sin)
            k = jnp.repeat(k, REP, axis=2)
            v = jnp.repeat(v, REP, axis=2)
            q = q.transpose(0, 2, 1, 3)
            k = k.transpose(0, 2, 1, 3)
            v = v.transpose(0, 2, 1, 3)
            scores = jnp.einsum('bhqd,bhkd->bhqk', q, k) / jnp.sqrt(jnp.float32(HD))
            causal = jnp.tril(jnp.ones((S, S), dtype=bool))
            scores = jnp.where(causal[None, None], scores, jnp.finfo(scores.dtype).min)
            attn = jax.nn.softmax(scores, axis=-1)
            out = jnp.einsum('bhqk,bhkd->bhqd', attn, v)
            out = out.transpose(0, 2, 1, 3).reshape(B, S, NQ * HD)
            return out @ w_out

        def moe_ffn(x2d, w_router, w_gate_up, w_down):
            logits = x2d @ w_router
            probs = jax.nn.softmax(logits, axis=-1)
            vals, idx = jax.lax.top_k(probs, TOPK)
            vals = vals / jnp.sum(vals, axis=-1, keepdims=True)
            combine = jnp.sum(jax.nn.one_hot(idx, E, dtype=x2d.dtype) * vals[..., None], axis=1)
            out = jnp.zeros_like(x2d)
            for e in range(E):
                gu = x2d @ w_gate_up[e]
                gate, up = jnp.split(gu, 2, axis=-1)
                h = jax.nn.silu(gate) * up
                out = out + combine[:, e:e + 1] * (h @ w_down[e])
            return out
        key = jax.random.key(seed)
        ks = jax.random.split(key, 6)
        B, S = (1, 512)
        return {'x': jax.random.normal(ks[0], (B, S, HID), dtype=jnp.float32), 'norm1_w': jnp.ones((HID,), dtype=jnp.float32), 'w_qkv': jax.random.normal(ks[1], (HID, (NQ + 2 * NKV) * HD), dtype=jnp.float32) * 0.02, 'w_out': jax.random.normal(ks[2], (NQ * HD, HID), dtype=jnp.float32) * 0.02, 'norm2_w': jnp.ones((HID,), dtype=jnp.float32), 'w_router': jax.random.normal(ks[3], (HID, E), dtype=jnp.float32) * 0.02, 'w_gate_up': jax.random.normal(ks[4], (E, HID, 2 * FF), dtype=jnp.float32) * 0.02, 'w_down': jax.random.normal(ks[5], (E, FF, HID), dtype=jnp.float32) * 0.02}
    _L0_ffn_all = _L0_ffn_setup()
    _L0_ffn_in = {k: v for k, v in _L0_ffn_all.items() if k in ('norm1_w', 'w_qkv', 'w_out', 'norm2_w', 'w_router', 'w_gate_up', 'w_down')}
    del _L0_ffn_all
    return {'x': x, 'L0_tok_gamma': _L0_tok_in['gamma'], 'L0_tok_beta': _L0_tok_in['beta'], 'L0_tok_w': _L0_tok_in['w'], 'L0_tok_b': _L0_tok_in['b'], 'L0_attn_w_key': _L0_attn_in['w_key'], 'L0_attn_w_value': _L0_attn_in['w_value'], 'L0_attn_w_query': _L0_attn_in['w_query'], 'L0_attn_w_gate': _L0_attn_in['w_gate'], 'L0_attn_w_out': _L0_attn_in['w_out'], 'L0_ffn_norm1_w': _L0_ffn_in['norm1_w'], 'L0_ffn_w_qkv': _L0_ffn_in['w_qkv'], 'L0_ffn_w_out': _L0_ffn_in['w_out'], 'L0_ffn_norm2_w': _L0_ffn_in['norm2_w'], 'L0_ffn_w_router': _L0_ffn_in['w_router'], 'L0_ffn_w_gate_up': _L0_ffn_in['w_gate_up'], 'L0_ffn_w_down': _L0_ffn_in['w_down']}

def reference(x, L0_tok_gamma, L0_tok_beta, L0_tok_w, L0_tok_b, L0_attn_w_key, L0_attn_w_value, L0_attn_w_query, L0_attn_w_gate, L0_attn_w_out, L0_ffn_norm1_w, L0_ffn_w_qkv, L0_ffn_w_out, L0_ffn_norm2_w, L0_ffn_w_router, L0_ffn_w_gate_up, L0_ffn_w_down):
    import jax
    import jax.numpy as jnp

    def _L0_tok_ref(x, gamma, beta, w, b):
        import jax, jax.numpy as jnp
        import numpy as np
        KEEP_RATIO = 0.7
        LN_EPS = 1e-05
        B, N, D = x.shape
        mu = jnp.mean(x, axis=-1, keepdims=True)
        var = jnp.mean(jnp.square(x - mu), axis=-1, keepdims=True)
        xn = (x - mu) * jax.lax.rsqrt(var + LN_EPS) * gamma + beta
        scores = jnp.einsum('bnd,d->bn', xn, w) + b[0]
        k = int(N * KEEP_RATIO)
        _, idx = jax.lax.top_k(scores, k)
        x_kept = jnp.take_along_axis(x, idx[..., None], axis=1)
        return x_kept

    def _L0_attn_ref(x, w_key, w_value, w_query, w_gate, w_out):
        import jax, jax.numpy as jnp
        import numpy as np
        NH, DK, DV, D = (8, 64, 64, 192)
        DECAY = 0.95
        WRITE_STRENGTH = 0.1
        B, S, _ = x.shape
        k = (x @ w_key.T).reshape(B, S, NH, DK)
        v = (x @ w_value.T).reshape(B, S, NH, DV)
        q = (x @ w_query.T).reshape(B, S, NH, DK)
        gate = jax.nn.sigmoid(x @ w_gate.T)
        k0 = k[0]
        v0 = v[0]
        g0 = gate[0]

        def step(fw, inp):
            q_t, k0_t, v0_t, g0_t = inp
            retrieved = jnp.einsum('bhk,hkv->bhv', q_t, fw)
            write = (WRITE_STRENGTH * g0_t)[:, None, None] * (k0_t[:, :, None] * v0_t[:, None, :])
            fw_new = DECAY * fw + jax.lax.stop_gradient(write)
            return (fw_new, retrieved)
        fw0 = jnp.zeros((NH, DK, DV), dtype=x.dtype)
        inputs = (q.transpose(1, 0, 2, 3), k0, v0, g0)
        _, retrieved = jax.lax.scan(step, fw0, inputs)
        retrieved = retrieved.transpose(1, 0, 2, 3).reshape(B, S, NH * DV)
        return x + retrieved @ w_out.T

    def _L0_ffn_ref(x, norm1_w, w_qkv, w_out, norm2_w, w_router, w_gate_up, w_down):
        import jax, jax.numpy as jnp
        import numpy as np
        HID = 192
        NQ = 12
        NKV = 3
        HD = 64
        REP = NQ // NKV
        E = 16
        TOPK = 2
        FF = 384
        EPS = 1e-06
        THETA = 10000.0

        def rms_norm(x, w):
            return x / jnp.sqrt(jnp.mean(x * x, axis=-1, keepdims=True) + EPS) * w

        def rope_tables(seq_len):
            inv = 1.0 / THETA ** (jnp.arange(0, HD, 2, dtype=jnp.float32) / HD)
            f = jnp.arange(seq_len, dtype=jnp.float32)[:, None] * inv[None, :]
            return (jnp.cos(f), jnp.sin(f))

        def apply_rope(t, cos, sin):
            B, S, H, _ = t.shape
            tr = t.reshape(B, S, H, HD // 2, 2)
            c = cos[None, :, None, :]
            s = sin[None, :, None, :]
            r0 = tr[..., 0] * c - tr[..., 1] * s
            r1 = tr[..., 0] * s + tr[..., 1] * c
            return jnp.stack([r0, r1], axis=-1).reshape(B, S, H, HD)

        def attention(x, w_qkv, w_out):
            B, S, _ = x.shape
            qkv = x @ w_qkv
            q, k, v = jnp.split(qkv, [NQ * HD, (NQ + NKV) * HD], axis=-1)
            q = q.reshape(B, S, NQ, HD)
            k = k.reshape(B, S, NKV, HD)
            v = v.reshape(B, S, NKV, HD)
            cos, sin = rope_tables(S)
            q = apply_rope(q, cos, sin)
            k = apply_rope(k, cos, sin)
            k = jnp.repeat(k, REP, axis=2)
            v = jnp.repeat(v, REP, axis=2)
            q = q.transpose(0, 2, 1, 3)
            k = k.transpose(0, 2, 1, 3)
            v = v.transpose(0, 2, 1, 3)
            scores = jnp.einsum('bhqd,bhkd->bhqk', q, k) / jnp.sqrt(jnp.float32(HD))
            causal = jnp.tril(jnp.ones((S, S), dtype=bool))
            scores = jnp.where(causal[None, None], scores, jnp.finfo(scores.dtype).min)
            attn = jax.nn.softmax(scores, axis=-1)
            out = jnp.einsum('bhqk,bhkd->bhqd', attn, v)
            out = out.transpose(0, 2, 1, 3).reshape(B, S, NQ * HD)
            return out @ w_out

        def moe_ffn(x2d, w_router, w_gate_up, w_down):
            logits = x2d @ w_router
            probs = jax.nn.softmax(logits, axis=-1)
            vals, idx = jax.lax.top_k(probs, TOPK)
            vals = vals / jnp.sum(vals, axis=-1, keepdims=True)
            combine = jnp.sum(jax.nn.one_hot(idx, E, dtype=x2d.dtype) * vals[..., None], axis=1)
            out = jnp.zeros_like(x2d)
            for e in range(E):
                gu = x2d @ w_gate_up[e]
                gate, up = jnp.split(gu, 2, axis=-1)
                h = jax.nn.silu(gate) * up
                out = out + combine[:, e:e + 1] * (h @ w_down[e])
            return out
        B, S, _ = x.shape
        h = x + attention(rms_norm(x, norm1_w), w_qkv, w_out)
        moe_in = rms_norm(h, norm2_w).reshape(B * S, HID)
        out = h + moe_ffn(moe_in, w_router, w_gate_up, w_down).reshape(B, S, HID)
        return out
    h = _L0_tok_ref(x, L0_tok_gamma, L0_tok_beta, L0_tok_w, L0_tok_b)
    h = h + _L0_attn_ref(_layernorm(h, axis=-1), L0_attn_w_key, L0_attn_w_value, L0_attn_w_query, L0_attn_w_gate, L0_attn_w_out)
    h = h + _L0_ffn_ref(_layernorm(h, axis=-1), L0_ffn_norm1_w, L0_ffn_w_qkv, L0_ffn_w_out, L0_ffn_norm2_w, L0_ffn_w_router, L0_ffn_w_gate_up, L0_ffn_w_down)
    return h

_drawn_inputs = setup_inputs


def setup_inputs(seed=0):
    import zlib

    import numpy as np

    out = dict(_drawn_inputs(seed))
    spreads = {'L0_tok_gamma': (1.0, 0.2),
     'L0_tok_beta': (0.0, 0.1),
     'L0_ffn_norm1_w': (1.0, 0.6),
     'L0_ffn_norm2_w': (1.0, 0.6)}
    factors = {'L0_attn_w_key': 7.832,
     'L0_attn_w_value': 7.2,
     'L0_attn_w_query': 7.167,
     'L0_attn_w_gate': 8.0,
     'L0_attn_w_out': 7.179,
     'L0_ffn_w_qkv': 5.502,
     'L0_ffn_w_out': 5.475,
     'L0_ffn_w_router': 8.0,
     'L0_ffn_w_gate_up': 8.0,
     'L0_ffn_w_down': 8.0}
    for name, (base, spread) in spreads.items():
        noise = np.random.default_rng([zlib.crc32(name.encode()), seed]).standard_normal(out[name].shape)
        drawn = base * np.exp(spread * noise) if base else spread * noise
        out[name] = jnp.asarray(drawn.astype(out[name].dtype))
    for name, factor in factors.items():
        out[name] = (out[name] * factor).astype(out[name].dtype)
    return out
```

```python
from contextlib import ExitStack

import numpy as np

import concourse.bass as bass
from concourse import mybir

F32 = mybir.dt.float32
BF16 = mybir.dt.bfloat16
I32 = mybir.dt.int32
ALU = mybir.AluOpType
ACT = mybir.ActivationFunctionType
AX = mybir.AxisListType.X

B, N0, D = 16, 250, 192
KEEP = int(N0 * 0.7)
HALF = N0 // 2
NT0 = 2 * B
T = (KEEP + 1) // 2
S = 2 * T
NT = 2 * B
NG = 4
GB = B // NG
C = D // 2
DEPTH = 1
LN_EPS = 1e-5
RMS_EPS = 1e-6
NH, DK = 8, 64
DECAY, WRITE = 0.95, 0.1
NQ, NKV, HD = 12, 3, 64
THETA = 10000.0
GW = (NQ // NKV + 2) * HD
QKW = (NQ // NKV + 1) * HD
E, FF = 16, 384
MT = 128
NMT = (2 * NT * T + E * (MT - 1)) // MT
NMT += NMT % 2
RW = D + 4
NSLOT = NMT * MT
MASKED = -1e30
NX = 4
NOROW = 1 << 20


def constants():
    t = np.arange(S)
    c = {}
    s_, t_ = np.arange(T)[:, None], t[None, :]
    c["decay"] = np.where(s_ < t_, WRITE * DECAY ** np.maximum(t_ - 1 - s_, 0), 0.0).astype(np.float32)
    c["ident"] = np.eye(128, dtype=np.float32)
    inv = 1.0 / THETA ** (np.arange(0, HD, 2, dtype=np.float32) / HD)
    f = t[:, None].astype(np.float32) * inv[None, :].astype(np.float32)
    cos, sin = np.cos(f).astype(np.float32), np.sin(f).astype(np.float32)
    tile = lambda a: np.ascontiguousarray(a.reshape(2, T, -1).transpose(1, 0, 2))
    c["cos"] = tile(np.concatenate([cos, cos], 1))
    c["sin"] = tile(np.concatenate([-sin, sin], 1))
    c["causal"] = np.where(np.arange(T)[None, :] <= np.arange(T)[:, None], 0.0, MASKED).astype(np.float32)
    j = np.arange(N0)[None, :]
    c["earlier"] = np.stack([(j < HALF * h + np.arange(HALF)[:, None]) for h in range(2)], 1).astype(np.float32)
    c["rowbase"] = np.broadcast_to((N0 * (np.arange(NT0) // 2)).astype(np.float32), (128, NT0)).copy()
    c["before"] = (np.arange(T)[:, None] < np.arange(T)[None, :]).astype(np.float32)
    c["erank"] = np.broadcast_to((E - np.arange(E)).astype(np.float32), (128, E)).copy()
    row = KEEP * (np.arange(NT) // 2)[None, :] + T * (np.arange(NT) % 2)[None, :] + np.arange(T)[:, None]
    kept = T * (np.arange(NT) % 2)[None, :] + np.arange(T)[:, None] < KEEP
    c["outrow"] = np.where(kept, row, NOROW).astype(np.int32).view(np.float32)
    blank = np.zeros((MT, RW), np.int32)
    blank[:, D] = NOROW
    c["blank"] = blank.view(np.float32)
    c["slotno"] = (np.arange(MT)[:, None] + MT * np.arange(NMT)[None, :]).astype(np.float32)
    c["tileno"] = np.arange(NMT, dtype=np.float32).reshape(1, NMT)
    return c


def build(nc, a, out, stage):
    scores_d = nc.dram_tensor("scores_d", (NT0, HALF), F32).ap()
    rows_d = nc.dram_tensor("rows_d", (NSLOT, RW), F32).ap()
    sorted_d = nc.dram_tensor("sorted_d", (B * N0, D), F32).ap()

    ctx = ExitStack()
    with ctx:
        def sb_in(stack, name, shape, dt=F32):
            return stack.enter_context(nc.sbuf_tensor(name, shape, dt))

        def sem(name):
            return ctx.enter_context(nc.semaphore(name))

        bank = [ctx.enter_context(nc.psum_tensor(f"bank{i}", [128, 512], F32)) for i in range(5)]
        proj = ctx.enter_context(nc.psum_tensor("proj", [128, 3, 512], F32))

        H = sb_in(ctx, "H", [T, NT, D])
        ident = sb_in(ctx, "ident", [128, 128])
        neg_half = sb_in(ctx, "neg_half", [128, NT])
        ln_eps = sb_in(ctx, "ln_eps", [128, 2])
        M = sb_in(ctx, "M", [T, NT, RW])
        ms = sb_in(ctx, "ms", [T, NT])

        before = sb_in(ctx, "before", [T, T])
        ones = sb_in(ctx, "ones", [T, T])
        erank = sb_in(ctx, "erank", [128, E])
        tileno = sb_in(ctx, "tileno", [1, NMT])
        slotno = sb_in(ctx, "slotno", [MT, NMT])
        outrow = sb_in(ctx, "outrow", [T, NT])
        blank = sb_in(ctx, "blank", [MT, RW])
        norm2w = sb_in(ctx, "norm2w", [T, D])
        wr = sb_in(ctx, "wr", [C, 2, E])
        rr3 = sb_in(ctx, "rr3", [T, NT])
        texp = sb_in(ctx, "texp", [1, NMT], I32)

        early, selection, attn = ExitStack(), ExitStack(), ExitStack()
        wq = sb_in(early, "wq", [C, 2, NH * DK])
        wk = sb_in(early, "wk", [C, 2, NH * DK])
        wv = sb_in(early, "wv", [C, 2, NH * DK])
        wg = sb_in(early, "wg", [C, 2, NH])
        wo = sb_in(early, "wo", [128, NH * DK // 128, D])
        decay = sb_in(early, "decay", [T, S])
        st1 = sb_in(early, "st1", [T, 2, 6])
        mv1 = sb_in(early, "mv1", [T, 2, 2, 2])
        rs1 = sb_in(early, "rs1", [T, 2, 2])
        xn1 = sb_in(early, "xn1", [T, 2, 2, D])
        hx1 = sb_in(early, "hx1", [T, 2, 2, D])
        xT1 = sb_in(early, "xT1", [C, 2, 2, S])
        qT1 = sb_in(early, "qT1", [128, 2, 4, S])
        kT1 = sb_in(early, "kT1", [128, 4, S])
        gate = sb_in(early, "gate", [T, 2, NH])
        vg = sb_in(early, "vg", [T, 2, NH, DK])
        p0 = sb_in(early, "p0", [T, 2, NH, S])
        p1 = sb_in(early, "p1", [T, 2, NH, T])
        rT1 = sb_in(early, "rT1", [128, 2, 4, S])

        X = sb_in(selection, "X", [HALF, NT0, D])
        GT = NT0 // NG
        Xc = sb_in(selection, "Xc", [HALF, 2, GT, D])
        Xsq = sb_in(selection, "Xsq", [HALF, 2, GT, D])
        Xgw = sb_in(selection, "Xgw", [HALF, 2, GT, D])
        gamma = sb_in(selection, "gamma", [128, D])
        beta = sb_in(selection, "beta", [128, D])
        tokw = sb_in(selection, "tokw", [128, D])
        tokb = sb_in(selection, "tokb", [128, 1])
        gw = sb_in(selection, "gw", [128, D])
        bw = sb_in(selection, "bw", [128, D])
        bsum = sb_in(selection, "bsum", [128, 1])
        mu = sb_in(selection, "mu", [HALF, NT0])
        var = sb_in(selection, "var", [HALF, NT0])
        dot = sb_in(selection, "dot", [HALF, NT0])
        rs0 = sb_in(selection, "rs0", [HALF, NT0])
        score = sb_in(selection, "score", [HALF, NT0])
        score_t = sb_in(selection, "score_t", [NT0, HALF])
        all_scores = sb_in(selection, "all_scores", [HALF, NT0 * HALF])
        earlier = sb_in(selection, "earlier", [HALF, 2, N0])
        rowbase = sb_in(selection, "rowbase", [128, NT0])
        above = sb_in(selection, "above", [HALF, NT0])
        tied = sb_in(selection, "tied", [HALF, NT0])
        flat = lambda t: t[:].rearrange("p a b d -> p (a b d)")[:, 0:GT * N0].rearrange("p (k n) -> p k n", k=GT)
        junk_a, junk_b = flat(Xsq), flat(Xgw)
        rank = sb_in(selection, "rank", [HALF, NT0], I32)

        selection.close()

        wqkv = sb_in(attn, "wqkv", [C, 2, NKV, GW])
        wout = sb_in(attn, "wout", [128, NQ * HD // 128, D])
        cos = sb_in(attn, "cos", [T, 2, HD])
        sin = sb_in(attn, "sin", [T, 2, HD])
        norm1w = sb_in(attn, "norm1w", [T, D])
        causal = sb_in(attn, "causal", [T, T])
        causal_b = sb_in(attn, "causal_b", [T, T], BF16)
        ident_b = sb_in(attn, "ident_b", [T, T], BF16)
        st2 = sb_in(attn, "st2", [T, 2, 6])
        mv2 = sb_in(attn, "mv2", [T, 2, 2])
        rs2 = sb_in(attn, "rs2", [T, 2, 2])
        rr2 = sb_in(attn, "rr2", [T, 2])
        ms2 = sb_in(attn, "ms2", [T, 2])
        x3 = sb_in(attn, "x3", [T, 2, 2, D])
        xr = sb_in(attn, "xr", [T, 2, D])
        xrT = sb_in(attn, "xrT", [C, 2, S])
        rope_c = sb_in(attn, "rope_c", [T, 2, NKV, QKW])
        rope_s = sb_in(attn, "rope_s", [T, 2, NKV, QKW])
        rot = sb_in(attn, "rot", [T, 2, NKV, QKW + HD])
        qkT = sb_in(attn, "qkT", [128, 2, NKV, 3, S])
        val = sb_in(attn, "val", [T, 2, 2, NKV, HD + 1])
        mx = sb_in(attn, "mx", [T, 2, 3])
        sx = sb_in(attn, "sx", [T, 2, 2 * S])
        pr = sb_in(attn, "pr", [T, 2, 2 * S])
        pT = sb_in(attn, "pT", [T, 2, 2 * S])
        rden = sb_in(attn, "rden", [T, 2, NQ // 2])
        oh = sb_in(attn, "oh", [T, 2, NQ * HD])
        oT = sb_in(attn, "oT", [128, 2, 6, T])
        sqj = sb_in(attn, "sqj", [T, 2, D])
        attn.close()
        early.close()

        wgu = sb_in(ctx, "wgu", [C, E * 4 * FF])
        wdn = sb_in(ctx, "wdn", [FF // 3, E * 3 * D])
        router, moe = ExitStack(), ctx
        EW = [T, NT, E]
        mrow = sb_in(router, "mrow", [T, 2, 2, D])
        mT = sb_in(router, "mT", [C, 2, 2, S])
        logit, sel1, sel2, sel = (sb_in(router, n, EW) for n in ("logit", "sel1", "sel2", "sel"))
        hit_pick = sb_in(router, "hit_pick", [T, 2, NT, E])
        hit, pick = hit_pick[:, 0], hit_pick[:, 1]
        run_a, run_b = hit, pick
        pos = sb_in(router, "pos", EW)
        top1, top2, cm, ex2, w1, w2, pos1, pos2 = (sb_in(router, n, [T, NT]) for n in
                                                   ("top1", "top2", "cm", "ex2", "w1", "w2", "pos1", "pos2"))
        pos1i, pos2i = (sb_in(router, n, [T, NT], I32) for n in ("pos1i", "pos2i"))
        cnt_i, til_i = (sb_in(router, n, [T, E], I32) for n in ("cnt_i", "til_i"))
        til, end_a, end_b, base = (sb_in(router, n, [T, E]) for n in ("til", "end_a", "end_b", "base"))
        past = hit_pick[0:1].rearrange("p a n e -> p (a n e)")[:, 0:NMT * E].rearrange("p (k e) -> p k e", e=E)
        texp_f = sb_in(router, "texp_f", [1, NMT])
        router.close()
        xg = sb_in(moe, "xg", [MT, NX, RW])
        xgT = sb_in(moe, "xgT", [C, 2, 2, MT])
        sg = sb_in(moe, "sg", [MT, 2, FF])
        hb = sb_in(moe, "hb", [MT, 2, FF])
        hT = sb_in(moe, "hT", [MT, 2, 3, MT])
        wv_ = sb_in(moe, "wv_", [MT, 2, 2])
        ys = sb_in(moe, "ys", [MT, 2, D])

        s_const = sem("s_const")
        s_tok_in = [sem(f"s_tok_in{g}") for g in range(NG)]
        s_tok_vec = sem("s_tok_vec")
        s_dve = sem("s_dve")
        s_apart = sem("s_apart")
        s_pool = sem("s_pool")
        s_centered = sem("s_centered")
        s_squared = sem("s_squared")
        s_weighted = sem("s_weighted")
        s_reduced = sem("s_reduced")
        s_stats = sem("s_stats")
        s_rs0 = sem("s_rs0")
        s_score = sem("s_score")
        s_score_tp = sem("s_score_tp")
        s_score_t = sem("s_score_t")
        s_score_out = sem("s_score_out")
        s_score_in = sem("s_score_in")
        s_rank = sem("s_rank")
        s_sorted = [sem(f"s_sorted{g}") for g in range(NG)]
        s_hzero = sem("s_hzero")
        s_h0 = [sem(f"s_h0{g}") for g in range(NG)]
        s_w1 = sem("s_w1")
        s_out = sem("s_out")

        SM = {n: sem("s_" + n) for n in ("c3 we blank base ms rr3 m back mTp mT logit gap ex sel cum slot dispatched texp").split()}
        s_xg = [sem(f"s_xg{i}") for i in range(NX)]
        s_xgTp, s_xgT, s_up, s_sg, s_h, s_hTp, s_hT, s_dn, s_y, s_add = (
            sem(n) for n in "s_xgTp s_xgT s_up s_sg s_h s_hTp s_hT s_dn s_y s_add".split())
        SEM = {}
        for n in ("s_w2 s_w2b s_h_stage s_mv2 s_rs2 s_xr s_xTp2 s_xrT s_proj s_rope s_rot s_val s_qkTp s_qkT s_sc2 s_sx s_pr s_tp s_pT "
                  "s_pv s_on s_oTp s_oT s_wo s_h2 s_hadd").split():
            SEM[n] = sem(n)
        (s_w2, s_w2b, s_h_stage, s_mv2, s_rs2, s_xr, s_xTp2, s_xrT, s_proj, s_rope, s_rot, s_val, s_qkTp, s_qkT, s_sc2, s_sx, s_pr,
         s_tp, s_pT, s_pv, s_on, s_oTp, s_oT, s_wo, s_h2, s_hadd) = SEM.values()
        s_mv1 = sem("s_mv1")
        s_rs1 = sem("s_rs1")
        s_xn1 = sem("s_xn1")
        s_hx1 = sem("s_hx1")
        s_xTp1 = sem("s_xTp1")
        s_xT1 = sem("s_xT1")
        s_qp1 = sem("s_qp1")
        s_q1 = sem("s_q1")
        s_kvg = sem("s_kvg")
        s_kv = sem("s_kv")
        s_gate = sem("s_gate")
        s_sc1 = sem("s_sc1")
        s_p1 = sem("s_p1")
        s_rp1 = sem("s_rp1")
        s_r1 = sem("s_r1")
        s_o1 = sem("s_o1")
        s_h1 = sem("s_h1")

        def wait(eng, s, v):
            if isinstance(v, int) and v <= 0:
                return
            eng.wait_ge(s, v)

        def wait_apart(eng, s, v):
            eng.wait_ge(s, v)
            eng.sem_inc(s_apart, 1)

        class Chain:

            def __init__(self, eng, s):
                self.eng, self.s, self.base, self.n = eng, s, 0, 0

            def link(self, ins, apart=False):
                ins.then_inc(self.s, 1)
                self.n += 1
                self.eng.wait_ge(self.s, self.base + self.n)
                if apart:
                    self.eng.sem_inc(s_apart, 1)

            def enter(self, i, per):
                self.start = self.n_done
                self.base, self.n, self.per = self.n_done + i * per, 0, per

            def leave(self, iterations):
                assert self.n == self.per, (self.n, self.per)
                self.n_done = self.start + iterations * self.per
                self.base, self.n = self.n_done, 0

            def settle(self):
                self.n_done = self.base + self.n

        block = ctx.enter_context(nc.Block())
        TX1, Q1A, Q1B, SC1A, SC1B = bank
        R1 = [proj[:, 0, :], proj[:, 1, :]]
        O1 = proj[:, 2, :]
        Q1 = [Q1A, Q1B]
        SC1 = [SC1A, SC1B]
        UNITS1 = [(1, (0, 2, 4, 6)), (1, (1, 3, 5, 7)), (0, (0, 2)), (0, (1, 3)), (0, (4, 6)), (0, (5, 7))]
        NU1 = len(UNITS1)
        UNITS2 = [(0, (0, 2, 4)), (0, (6, 8, 10)), (0, (1, 3, 5)), (0, (7, 9, 11)),
                  (1, (0, 2)), (1, (4, 6)), (1, (8, 10)), (1, (1, 3)), (1, (5, 7)), (1, (9, 11))]
        NU2 = len(UNITS2)
        HALF_END = {1: 0, 3: 1, 6: 2, 9: 3}
        PT2, O2, MISC, SC2A, SC2B = bank
        SC2 = [SC2A, SC2B]
        GATE = [bank[3], proj[:, 0, :]]
        UP = [bank[4], proj[:, 1, :]]

        @block.sync
        def _(sp):
            sp.dma_start(gamma[:], a["gamma"]).then_inc(s_tok_vec, 16)
            sp.dma_start(beta[:], a["beta"]).then_inc(s_tok_vec, 16)
            sp.dma_start(tokw[:], a["tokw"]).then_inc(s_tok_vec, 16)
            sp.dma_start(tokb[:], a["tokb"]).then_inc(s_tok_vec, 16)
            for g in range(NG):
                sp.dma_start(X[:, GT * g:GT * (g + 1), :],
                             a["x"][GB * g:GB * (g + 1)].rearrange("b (h p) d -> p (b h) d", h=2)).then_inc(s_tok_in[g], 16)
            sp.dma_start(ident[:], a["ident"]).then_inc(s_const, 16)
            sp.dma_start(earlier[:], a["earlier"]).then_inc(s_const, 16)
            sp.dma_start(rowbase[:], a["rowbase"]).then_inc(s_const, 16)
            for t_, n in ((wq, "wq"), (wk, "wk"), (wv, "wv"), (wg, "wg"), (wo, "wo"), (decay, "decay")):
                sp.dma_start(t_[:], a[n]).then_inc(s_w1, 16)
            sp.wait_ge(s_score_t, 1)
            sp.dma_start(scores_d, score_t[:]).then_inc(s_score_out, 16)
            sp.wait_ge(s_score_out, 16)
            sp.dma_start(all_scores[:], scores_d.rearrange("n p -> (n p)").partition_broadcast(HALF)).then_inc(s_score_in, 16)
            sp.wait_ge(s_hzero, 1)
            for g in range(NG):
                sp.wait_ge(s_sorted[g], 16 * GT)
                rows = sorted_d.rearrange("(b n) d -> n b d", n=N0)
                Hv = H[:].rearrange("p (b h) d -> p b h d", h=2)
                for h in range(2):
                    n = min(T, KEEP - T * h)
                    sp.dma_start(Hv[0:n, GB * g:GB * (g + 1), h, :],
                                 rows[T * h:T * h + n, GB * g:GB * (g + 1), :]).then_inc(s_h0[g], 16)
            for t_, n in ((wqkv, "wqkv"), (wout, "wout"), (cos, "cos"), (sin, "sin"), (norm1w, "norm1w"), (causal, "causal")):
                sp.dma_start(t_[:], a[n]).then_inc(s_w2, 16)
            for t_, n in ((before, "before"), (erank, "erank"), (tileno, "tileno"), (slotno, "slotno"), (outrow, "outrow"),
                          (norm2w, "norm2w"), (wr, "wr"), (blank, "blank")):
                sp.dma_start(t_[:], a[n]).then_inc(SM["c3"], 16)
            sp.wait_ge(SM["c3"], 16 * 8)
            sp.dma_start(rows_d.rearrange("(k p) r -> p k r", p=MT),
                         blank[:].unsqueeze(1).broadcast_to([MT, NMT, RW])).then_inc(SM["blank"], 16)
            sp.wait_ge(s_hadd, 2 * B)
            sp.wait_ge(s_h2, 2 * B)
            orow = out.rearrange("b t d -> t b d")
            for q in range(4):
                n = E // 4 * 4 * FF
                sp.dma_start(wgu[:, q * n:(q + 1) * n], a["wgu"][:, q * n:(q + 1) * n]).then_inc(SM["we"], 16)
            for q in range(4):
                n = E // 4 * 3 * D
                sp.dma_start(wdn[:, q * n:(q + 1) * n], a["wdn"][:, q * n:(q + 1) * n]).then_inc(SM["we"], 16)
            for h in range(2):
                n = min(T, KEEP - T * h)
                Hv = H[:].rearrange("p (b h) d -> p b h d", h=2)
                sp.dma_start(orow[T * h:T * h + n, :, :], Hv[0:n, :, h, :]).then_inc(SM["base"], 16)

            def load(k, slot, turn):
                wait(sp, s_add, 16 * (k - NX + 1))
                src = rows_d[bass.ds(k * MT, MT), :]
                sp.dma_start(xg[:, slot, :], src).then_inc(s_xg[slot], 16)

            sp.wait_ge(SM["dispatched"], 16 * 2 * NT)
            for k in range(NX):
                load(k, k, 0)
            with sp.Fori(1, NMT // NX) as i:
                for r in range(NX):
                    load(NX * i + r, r, i)

        @block.gpsimd
        def _(pool):
            ch = Chain(pool, s_pool)
            pool.memset(neg_half[:], -0.5)
            pool.memset(ln_eps[:], LN_EPS)
            ch.link(pool.memset(H[:], 0.0))
            pool.sem_inc(s_hzero, 1)
            for g in range(NG):
                pool.wait_ge(s_centered, g + 1)
                if g >= 2:
                    pool.wait_ge(s_reduced, g - 1)
                pool.tensor_tensor(Xgw[:, g % 2], Xc[:, g % 2], gw[0:HALF, :].unsqueeze(1).broadcast_to([HALF, GT, D]), ALU.mult).then_inc(s_weighted, 1)
            pool.wait_ge(s_stats, 1)
            pool.tensor_tensor(rs0[:], var[:], neg_half[0:HALF, :], ALU.pow).then_inc(s_rs0, 1)
            for g in range(NG):
                pool.wait_ge(s_rank, g + 1)
                for n in range(GT * g, GT * (g + 1)):
                    pool.indirect_dma_start(out=sorted_d, out_offset=bass.IndirectOffsetOnAxis(ap=rank[:, n:n + 1], axis=0),
                                            in_=X[:, n, :], in_offset=None).then_inc(s_sorted[g], 16)
            ch.settle()

            def norm1(b, u):
                wait_apart(pool, s_mv1, b + 1)
                ch.link(pool.tensor_scalar(rs1[:, u], mv1[:, u, :, 1], LN_EPS, None, ALU.add))
                pool.tensor_tensor(rs1[:, u], rs1[:, u], neg_half[0:T, 0:2], ALU.pow).then_inc(s_rs1, 1)

            def residual1(b, u):
                pool.wait_ge(s_xn1, b + 1)
                pool.tensor_tensor(hx1[:, u], H[:, bass.ds(2 * b, 2), :], xn1[:, u], ALU.add).then_inc(s_hx1, 1)

            norm1(0, 0)
            residual1(0, 0)
            ch.settle()
            with pool.Fori(0, B // 2 - 1) as i:
                ch.enter(i, 2)
                for u in range(2):
                    norm1(2 * i + u + 1, 1 - u)
                    residual1(2 * i + u + 1, 1 - u)
            ch.leave(B // 2 - 1)
            norm1(B - 1, 1)
            residual1(B - 1, 1)
            ch.settle()

            pool.wait_ge(s_w2, 16 * 6)
            pool.memset(val[:, :, :, :, HD:HD + 1], 1.0).then_inc(s_w2b, 1)

            def norm2(b, u):
                pool.wait_ge(s_mv2, b + 1)
                ch.link(pool.tensor_tensor(rs2[:, u], mv2[:, :, 1], ln_eps[0:T, :], ALU.add))
                ch.link(pool.tensor_tensor(rs2[:, u], rs2[:, u], neg_half[0:T, 0:2], ALU.pow))
                ch.link(pool.tensor_tensor(ms2[:], rs2[:, u], rs2[:, u], ALU.mult))
                ch.link(pool.tensor_tensor(ms2[:], ms2[:], mv2[:, :, 1], ALU.mult), apart=True)
                ch.link(pool.tensor_scalar(ms2[:], ms2[:], RMS_EPS, None, ALU.add))
                pool.tensor_tensor(rr2[:], ms2[:], neg_half[0:T, 0:2], ALU.pow).then_inc(s_rs2, 1)

            def rotate(b, j):
                pool.wait_ge(s_rope, 2 * b + j + 1)
                pool.tensor_tensor(rot[:, j, :, 0:QKW], rope_c[:, j], rope_s[:, j], ALU.add)
                pool.tensor_tensor(rot[:, j, :, QKW:QKW + HD], rope_c[:, j, :, QKW - HD:QKW], rope_s[:, j, :, QKW - HD:QKW],
                                   ALU.add).then_inc(s_rot, 1)

            def stream(b, j):
                n = bass.ds(2 * b + j, 1)
                pool.wait_ge(s_h2, 2 * b + j + 1)
                pool.tensor_tensor(H[:, n, :], H[:, n, :], M[:, n, 0:D], ALU.add).then_inc(s_hadd, 1)

            norm2(0, 0)
            rotate(0, 0)
            rotate(0, 1)

            def body(b, prev, nxt, nu):
                if nxt is not None:
                    norm2(nxt, nu)
                if prev is not None:
                    stream(prev, 1)
                if nxt is not None:
                    rotate(nxt, 0)
                stream(b, 0)
                if nxt is not None:
                    rotate(nxt, 1)

            body(0, None, 1, 1)
            ch.settle()
            with pool.Fori(0, B // 2 - 1) as i:
                ch.enter(i, 10)
                body(2 * i + 1, 2 * i, 2 * i + 2, 0)
                body(2 * i + 2, 2 * i + 1, 2 * i + 3, 1)
            ch.leave(B // 2 - 1)
            body(B - 1, B - 2, None, None)
            stream(B - 1, 1)

            pool.wait_ge(SM["ms"], 1)
            pool.memset(ones[:], 1.0)
            ch.link(pool.tensor_scalar(rr3[:], ms[:], RMS_EPS, None, ALU.add))
            pool.tensor_tensor(rr3[:], rr3[:], neg_half[0:T, :], ALU.pow).then_inc(SM["rr3"], 1)
            with pool.Fori(0, B // 2) as i:
                for u in range(2):
                    b = 2 * i + u
                    pool.wait_ge(SM["m"], b + 1)
                    pool.tensor_copy(M[:, bass.ds(2 * b, 2), 0:D], mrow[:, u]).then_inc(SM["back"], 1)
            pool.wait_ge(SM["back"], B)
            pool.wait_ge(SM["slot"], 1)
            pool.wait_ge(SM["blank"], 16)
            for p in (pos1i, pos2i):
                for n in range(NT):
                    pool.indirect_dma_start(out=rows_d, out_offset=bass.IndirectOffsetOnAxis(ap=p[:, n:n + 1], axis=0),
                                            in_=M[:, n, :], in_offset=None).then_inc(SM["dispatched"], 16)

            pool.wait_ge(SM["base"], 32)

            def add(k, u, slot):
                wait_apart(pool, s_y, k + 1)
                if not isinstance(k, int) or k:
                    wait_apart(pool, s_add, 16 * k)
                pool.indirect_dma_start(out=out.rearrange("b t d -> (b t) d"),
                                        out_offset=bass.IndirectOffsetOnAxis(ap=xg[:, slot, D:D + 1].bitcast(I32), axis=0),
                                        in_=ys[:, u, :], in_offset=None, bounds_check=B * KEEP - 1, oob_is_err=False,
                                        compute_op=ALU.add).then_inc(s_add, 16)

            for k in range(NX + 1):
                add(k, k % 2, k % NX)
            with pool.Fori(1, NMT // NX - 1) as i:
                for r in range(1, NX + 1):
                    add(NX * i + r, r % 2, r % NX)
            for k in range(NMT - NX + 1, NMT):
                add(k, k % 2, k % NX)
            pool.wait_ge(s_add, 16 * NMT)

        @block.scalar
        def _(act):
            for g in range(NG):
                act.wait_ge(s_centered, g + 1)
                if g >= 2:
                    act.wait_ge(s_reduced, g - 1)
                act.activation(Xsq[:, g % 2], Xc[:, g % 2], ACT.Square).then_inc(s_squared, 1)
            act.wait_ge(s_score_tp, 1)
            act.copy(score_t[:], TX1[0:NT0, 0:HALF]).then_inc(s_score_t, 1)

            def xT_copy(b, u):
                act.wait_ge(s_xTp1, b + 1)
                act.copy(xT1[:, u], TX1[0:C, 0:2 * S].rearrange("p (c t) -> p c t", c=2)).then_inc(s_xT1, 1)

            def q_copy(b, u, h):
                act.wait_ge(s_qp1, 2 * b + h + 1)
                act.copy(qT1[:, u, 2 * h:2 * h + 2, :], Q1[h][:, 0:2 * S].rearrange("p (m t) -> p m t", m=2)).then_inc(s_q1, 1)

            def r_copy(b, u, h):
                act.wait_ge(s_rp1, 2 * b + h + 1)
                if h == 0:
                    wait(act, s_o1, b)
                act.copy(rT1[:, u, 2 * h:2 * h + 2, :], R1[h][:, 0:2 * S].rearrange("p (m t) -> p m t", m=2)).then_inc(s_r1, 1)

            xT_copy(0, 0)
            for h in range(2):
                act.wait_ge(s_kvg, h + 1)
                act.copy(kT1[:, 2 * h:2 * h + 2, :], Q1[h][:, 0:2 * S].rearrange("p (m t) -> p m t", m=2)).then_inc(s_kv, 1)
            act.wait_ge(s_kvg, 3)
            act.activation(gate[:], O1[0:T, 0:2 * NH].rearrange("p (h e) -> p h e", h=2), ACT.Exp, scale=-1.0).then_inc(s_gate, 1)
            for h in range(2):
                q_copy(0, 0, h)

            def body(b, u, nxt):
                if nxt is not None:
                    xT_copy(nxt, 1 - u)
                r_copy(b, u, 0)
                if nxt is not None:
                    q_copy(nxt, 1 - u, 0)
                r_copy(b, u, 1)
                if nxt is not None:
                    q_copy(nxt, 1 - u, 1)

            body(0, 0, 1)
            with act.Fori(0, B // 2 - 1) as i:
                body(2 * i + 1, 1, 2 * i + 2)
                body(2 * i + 2, 0, 2 * i + 3)
            body(B - 1, 1, None)

            def xrT_copy(b):
                act.wait_ge(s_xTp2, b + 1)
                act.copy(xrT[:], MISC[0:C, 0:2 * S].rearrange("p (c t) -> p c t", c=2)).then_inc(s_xrT, 1)

            def val_copy(b, u, j):
                act.wait_ge(s_rope, 2 * b + j + 1)
                act.copy(val[:, u, j, :, 0:HD], proj[0:T, :, QKW:GW]).then_inc(s_val, 1)

            def qkT_copy(b, u, j):
                act.wait_ge(s_qkTp, 2 * b + j + 1)
                act.copy(qkT[:, u, :, :, j * T:(j + 1) * T], proj[:, :, 0:3 * T].rearrange("p g (k t) -> p g k t", k=3)).then_inc(s_qkT, 1)

            def exponent(b, k):
                w = (3 * T, 2 * S)[UNITS2[k][0]]
                act.wait_ge(s_sx, NU2 * b + k + 1)
                wait(act, s_tp, NU2 * b + k - 1)
                act.activation(pr[:, k % 2, 0:w], sx[:, k % 2, 0:w], ACT.Exp, scale=HD ** -0.5).then_inc(s_pr, 1)

            def pT_copy(b, k):
                w = (3 * T, 2 * S)[UNITS2[k][0]]
                act.wait_ge(s_tp, NU2 * b + k + 1)
                wait(act, s_pv, NU2 * b + k - 1)
                act.copy(pT[:, k % 2, 0:w], PT2[0:T, 0:w]).then_inc(s_pT, 1)

            def oT_copy(b, j, h):
                act.wait_ge(s_oTp, 4 * b + 2 * j + h + 1)
                act.copy(oT[:, j, 3 * h:3 * h + 3, :], MISC[:, 0:3 * T].rearrange("p (m t) -> p m t", m=3)).then_inc(s_oT, 1)

            act.wait_ge(s_w2b, 1)
            xrT_copy(0)
            val_copy(0, 0, 0)
            qkT_copy(0, 0, 0)
            val_copy(0, 0, 1)

            def body2(b, u, nxt):
                for k in range(NU2 + 2):
                    if k == 2:
                        qkT_copy(b, u, 1)
                    if k >= 2:
                        pT_copy(b, k - 2)
                    if k < NU2:
                        exponent(b, k)
                    if k == 3 and nxt is not None:
                        xrT_copy(nxt)
                    if k == 5 and nxt is not None:
                        val_copy(nxt, 1 - u, 0)
                    if k == 8 and nxt is not None:
                        qkT_copy(nxt, 1 - u, 0)
                    if k in (8, 9):
                        oT_copy(b, 0, k - 8)
                oT_copy(b, 1, 0)
                oT_copy(b, 1, 1)
                if nxt is not None:
                    val_copy(nxt, 1 - u, 1)

            body2(0, 0, 1)
            with act.Fori(0, B // 2 - 1) as i:
                body2(2 * i + 1, 1, 2 * i + 2)
                body2(2 * i + 2, 0, 2 * i + 3)
            body2(B - 1, 1, None)

            def mT_copy(b, u):
                act.wait_ge(SM["mTp"], b + 1)
                act.copy(mT[:, u], bank[u][0:C, 0:2 * S].rearrange("p (c t) -> p c t", c=2)).then_inc(SM["mT"], 1)

            act.wait_ge(s_hadd, 2 * B)
            with act.Fori(0, B // 2) as i:
                for u in range(2):
                    mT_copy(2 * i + u, u)
            act.wait_ge(SM["gap"], 1)
            act.activation(ex2[:], top2[:], ACT.Exp).then_inc(SM["ex"], 1)

            def xgT_copy(k, u):
                act.wait_ge(s_xgTp, k + 1)
                act.copy(xgT[:, u], bank[0][0:C, 0:2 * MT].rearrange("p (c t) -> p c t", c=2)).then_inc(s_xgT, 1)

            def silu(k, u):
                act.wait_ge(s_up, k + 1)
                act.activation(sg[:, u], GATE[u][:, 0:FF], ACT.Silu).then_inc(s_sg, 1)

            def hT_copy(k, u):
                act.wait_ge(s_hTp, k + 1)
                act.copy(hT[:, u], bank[1][:, 0:FF].rearrange("p (m t) -> p m t", m=3)).then_inc(s_hT, 1)

            def tile(k, u, last=False):
                if not last:
                    xgT_copy(k + 1, 1 - u)
                hT_copy(k, u)
                if not last:
                    silu(k + 1, 1 - u)

            act.wait_ge(SM["dispatched"], 16 * 2 * NT)
            xgT_copy(0, 0)
            silu(0, 0)
            for k in range(NX + 1):
                tile(k, k % 2)
            with act.Fori(1, NMT // NX - 1) as i:
                for r in range(1, NX + 1):
                    tile(NX * i + r, r % 2)
            for k in range(NMT - NX + 1, NMT):
                tile(k, k % 2, k == NMT - 1)

        @block.vector
        def _(dve):
            ch = Chain(dve, s_dve)
            dve.wait_ge(s_tok_vec, 64)
            dve.tensor_tensor(gw[:], gamma[:], tokw[:], ALU.mult)
            ch.link(dve.tensor_tensor(bw[:], beta[:], tokw[:], ALU.mult))
            ch.link(dve.tensor_reduce(bsum[:], bw[:], AX, ALU.add))
            ch.link(dve.tensor_tensor(bsum[:], bsum[:], tokb[:], ALU.add))

            def reduce_group(g):
                lo, hi = GT * g, GT * (g + 1)
                dve.wait_ge(s_squared, g + 1)
                dve.tensor_reduce(var[:, lo:hi], Xsq[:, g % 2], AX, ALU.add)
                dve.wait_ge(s_weighted, g + 1)
                ch.link(dve.tensor_reduce(dot[:, lo:hi], Xgw[:, g % 2], AX, ALU.add))
                dve.sem_inc(s_reduced, 1)

            for g in range(NG):
                lo, hi = GT * g, GT * (g + 1)
                dve.wait_ge(s_tok_in[g], 16)
                ch.link(dve.tensor_reduce(mu[:, lo:hi], X[:, lo:hi, :], AX, ALU.add))
                ch.link(dve.tensor_scalar(mu[:, lo:hi], mu[:, lo:hi], 1.0 / D, None, ALU.mult))
                dve.tensor_tensor(Xc[:, g % 2], X[:, lo:hi, :], mu[:, lo:hi].unsqueeze(2).broadcast_to([HALF, GT, D]),
                                  ALU.subtract).then_inc(s_centered, 1)
                if g:
                    reduce_group(g - 1)
            reduce_group(NG - 1)
            dve.tensor_scalar(var[:], var[:], 1.0 / D, LN_EPS, ALU.mult, ALU.add).then_inc(s_stats, 1)
            dve.wait_ge(s_rs0, 1)
            ch.link(dve.tensor_tensor(mu[:], rs0[:], rs0[:], ALU.mult))
            ch.link(dve.tensor_tensor(mu[:], mu[:], var[:], ALU.mult))
            ch.link(dve.tensor_scalar(mu[:], mu[:], -0.5, 1.5, ALU.mult, ALU.add))
            ch.link(dve.tensor_tensor(rs0[:], rs0[:], mu[:], ALU.mult))
            ch.link(dve.tensor_tensor(dot[:], dot[:], rs0[:], ALU.mult))
            dve.tensor_scalar(score[:], dot[:], bsum[0:HALF, :], None, ALU.add).then_inc(s_score, 1)
            dve.wait_ge(s_score_in, 16)
            dve.wait_ge(s_const, 48)
            ch.settle()
            with dve.Fori(0, NG) as g:
                ch.enter(g, 2)
                for k in range(GT):
                    row = all_scores[:, bass.ds(g * (GT * HALF) + N0 * (k // 2), N0)]
                    own = score[:, bass.ds(g * GT + k, 1)]
                    dve.tensor_scalar(junk_a[:, k], row, own, None, ALU.is_gt, ALU.add, accum_out=above[:, bass.ds(g * GT + k, 1)])
                    ins = dve.scalar_tensor_tensor(junk_b[:, k], row, own, earlier[:, k % 2, :], ALU.is_equal, ALU.mult,
                                                   accum_out=tied[:, bass.ds(g * GT + k, 1)])
                ch.link(ins)
                grp = bass.ds(g * GT, GT)
                ch.link(dve.tensor_tensor(above[:, grp], above[:, grp], tied[:, grp], ALU.add))
                dve.tensor_tensor(rank[:, grp], above[:, grp], rowbase[0:HALF, grp], ALU.add).then_inc(s_rank, 1)
            ch.leave(NG)

            def norm_rows(b, u):
                for h in range(2):
                    ins = dve.bn_stats(st1[:, h, :], H[:, bass.ds(2 * b + h, 1), :])
                ch.link(ins, apart=True)
                for h in range(2):
                    ins = dve.bn_aggr(mv1[:, u, h, :], st1[:, h, :])
                ins.then_inc(s_mv1, 1)

            def normalise(b, u):
                dve.wait_ge(s_rs1, b + 1)
                for h in range(2):
                    ins = dve.tensor_scalar(xn1[:, u, h, :], H[:, bass.ds(2 * b + h, 1), :], mv1[:, u, h, 0:1], rs1[:, u, h:h + 1],
                                            ALU.subtract, ALU.mult)
                ins.then_inc(s_xn1, 1)

            def decayed(b, u, k):
                tile, heads = UNITS1[k]
                dve.wait_ge(s_sc1, NU1 * b + k + 1)
                src = SC1[k % 2][0:T, 0:2 * S]
                if tile == 1:
                    o = p1[:, u].rearrange("p (m e) t -> p m e t", e=2)[:, :, heads[0] % 2, :]
                    dve.tensor_tensor(o, src.rearrange("p (m t) -> p m t", m=4), decay[:, 0:T].unsqueeze(1).broadcast_to([T, 4, T]),
                                      ALU.mult).then_inc(s_p1, 1)
                else:
                    o = p0[:, u].rearrange("p (m e) t -> p m e t", e=2)[:, heads[0] // 2:heads[0] // 2 + 2, heads[0] % 2, :]
                    dve.tensor_tensor(o, src.rearrange("p (m t) -> p m t", m=2), decay[:].unsqueeze(1).broadcast_to([T, 2, S]),
                                      ALU.mult).then_inc(s_p1, 1)

            def close1(b, u):
                dve.wait_ge(s_o1, b + 1)
                dve.wait_ge(s_hx1, b + 1)
                dve.tensor_tensor(H[:, bass.ds(2 * b, 2), :], O1[0:T, 0:2 * D].rearrange("p (h d) -> p h d", h=2), hx1[:, u],
                                  ALU.add).then_inc(s_h1, 1)

            dve.wait_ge(s_w1, 16 * 6)
            dve.wait_ge(s_h0[0], 32)
            norm_rows(0, 0)
            normalise(0, 0)
            dve.wait_ge(s_gate, 1)
            ch.link(dve.tensor_scalar(gate[:], gate[:], 1.0, None, ALU.add))
            ch.link(dve.reciprocal(gate[:], gate[:]))
            for h in range(2):
                ins = dve.tensor_tensor(vg[:, h], SC1[h][0:T, :].rearrange("p (e d) -> p e d", e=NH),
                                        gate[:, h, :].unsqueeze(2).broadcast_to([T, NH, DK]), ALU.mult)
            ins.then_inc(s_kv, 1)
            for g in range(1, NG):
                dve.wait_ge(s_h0[g], 32)
            ch.settle()

            def body(b, u, prev, nxt):
                if nxt is not None:
                    norm_rows(nxt, 1 - u)
                decayed(b, u, 0)
                decayed(b, u, 1)
                if prev is not None:
                    close1(prev, 1 - u)
                if nxt is not None:
                    normalise(nxt, 1 - u)
                for k in range(2, NU1):
                    decayed(b, u, k)

            body(0, 0, None, 1)
            ch.settle()
            with dve.Fori(0, B // 2 - 1) as i:
                ch.enter(i, 2)
                body(2 * i + 1, 1, 2 * i, 2 * i + 2)
                body(2 * i + 2, 0, 2 * i + 1, 2 * i + 3)
            ch.leave(B // 2 - 1)
            body(B - 1, 1, B - 2, None)
            close1(B - 1, 1)
            ch.settle()

            dve.wait_ge(s_w2, 16 * 6)
            dve.wait_ge(s_h1, B)
            dve.tensor_copy(causal_b[:], causal[:])
            dve.tensor_copy(ident_b[:], ident[0:T, 0:T]).then_inc(s_w2b, 1)

            def stats2(b):
                for h in range(2):
                    ins = dve.bn_stats(st2[:, h, :], H[:, bass.ds(2 * b + h, 1), :])
                ch.link(ins, apart=True)
                for h in range(2):
                    ins = dve.bn_aggr(mv2[:, h, :], st2[:, h, :])
                ins.then_inc(s_mv2, 1)

            def rows2(b, u):
                dve.wait_ge(s_rs2, b + 1)
                wait(dve, s_xTp2, b)
                for h in range(2):
                    ins = dve.tensor_scalar(x3[:, u, h, :], H[:, bass.ds(2 * b + h, 1), :], mv2[:, h, 0:1], rs2[:, u, h:h + 1],
                                            ALU.subtract, ALU.mult)
                ch.link(ins)
                for h in range(2):
                    ins = dve.scalar_tensor_tensor(xr[:, h, :], x3[:, u, h, :], rr2[:, h:h + 1], norm1w[:], ALU.mult, ALU.mult)
                ins.then_inc(s_xr, 1)

            def rope(b, j):
                dve.wait_ge(s_proj, 2 * b + j + 1)
                hw = HD // 2
                n = QKW // HD
                src = proj[0:T, :, 0:QKW].rearrange("p g (n d) -> p g n d", d=HD)
                tab = lambda t, lo, hi: t[:, j, lo:hi].unsqueeze(1).unsqueeze(1).broadcast_to([T, NKV, n, hi - lo])
                dst = lambda t: t[:, j].rearrange("p g (n d) -> p g n d", d=HD)
                dve.tensor_tensor(dst(rope_c), src, tab(cos, 0, HD), ALU.mult)
                dve.tensor_tensor(dst(rope_s)[:, :, :, 0:hw], src[:, :, :, hw:HD], tab(sin, 0, hw), ALU.mult)
                dve.tensor_tensor(dst(rope_s)[:, :, :, hw:HD], src[:, :, :, 0:hw], tab(sin, hw, HD), ALU.mult).then_inc(s_rope, 1)

            def centre(b, k):
                tile, heads = UNITS2[k]
                nh, w = len(heads), (T, S)[tile]
                dve.wait_ge(s_sc2, NU2 * b + k + 1)
                src = SC2[k % 2][0:T, 0:nh * w].rearrange("p (n t) -> p n t", n=nh)
                ch.link(dve.tensor_reduce(mx[:, k % 2, 0:nh], src, AX, ALU.max))
                wait(dve, s_pr, NU2 * b + k - 1)
                dve.tensor_tensor(sx[:, k % 2, 0:nh * w].rearrange("p (n t) -> p n t", n=nh), src,
                                  mx[:, k % 2, 0:nh].unsqueeze(2).broadcast_to([T, nh, w]), ALU.subtract).then_inc(s_sx, 1)

            def divide(b, q):
                dve.wait_ge(s_pv, NU2 * b + (2, 4, 7, 10)[q])
                o = O2[0:T, 0:6 * (HD + 1)].rearrange("p (n d) -> p n d", n=6)
                ch.link(dve.reciprocal(rden[:, q % 2, :], o[:, :, HD]))
                dst = oh[:, q // 2].rearrange("p (m e d) -> p m e d", m=6, e=2)[:, :, q % 2, :]
                dve.tensor_tensor(dst, o[:, :, 0:HD], rden[:, q % 2, :].unsqueeze(2).broadcast_to([T, 6, HD]), ALU.mult).then_inc(s_on, 1)

            def close2(b, u, j):
                n = bass.ds(2 * b + j, 1)
                dve.wait_ge(s_wo, 2 * b + j + 1)
                ch.link(dve.tensor_tensor(M[:, n, 0:D], MISC[0:T, 0:D], x3[:, u, j, :], ALU.add))
                dve.sem_inc(s_h2, 1)
                ch.link(dve.scalar_tensor_tensor(sqj[:, j, :], M[:, n, 0:D], 1.0 / D, M[:, n, 0:D], ALU.mult, ALU.mult, accum_out=ms[:, n]))

            stats2(0)
            rows2(0, 0)
            rope(0, 0)
            rope(0, 1)

            def body2(b, u, prev, nxt):
                for k in range(NU2):
                    centre(b, k)
                    if k == 0 and nxt is not None:
                        stats2(nxt)
                    if k == 1 and prev is not None:
                        close2(prev, 1 - u, 1)
                    if k == 2 and nxt is not None:
                        rows2(nxt, 1 - u)
                    if k == 4:
                        divide(b, 0)
                    if k == 5 and nxt is not None:
                        rope(nxt, 0)
                    if k == 6:
                        divide(b, 1)
                divide(b, 2)
                close2(b, u, 0)
                divide(b, 3)
                if nxt is not None:
                    rope(nxt, 1)

            body2(0, 0, None, 1)
            ch.settle()
            with dve.Fori(0, B // 2 - 1) as i:
                ch.enter(i, 2 * (NU2 + 4 + 2 + 4))
                body2(2 * i + 1, 1, 2 * i, 2 * i + 2)
                body2(2 * i + 2, 0, 2 * i + 1, 2 * i + 3)
            ch.leave(B // 2 - 1)
            body2(B - 1, 1, B - 2, None)
            close2(B - 1, 1, 1)
            dve.sem_inc(SM["ms"], 1)

            dve.wait_ge(SM["c3"], 16 * 8)
            dve.tensor_copy(M[:, :, D:D + 1], outrow[:].unsqueeze(2))
            dve.wait_ge(SM["rr3"], 1)
            dve.wait_ge(s_hadd, 2 * B)

            def rows3(b, u):
                wait(dve, SM["mTp"], b - 1)
                wait(dve, SM["back"], b - 1)
                for j in range(2):
                    n = bass.ds(2 * b + j, 1)
                    ins = dve.scalar_tensor_tensor(mrow[:, u, j, :], M[:, n, 0:D], rr3[:, n], norm2w[:], ALU.mult, ALU.mult)
                ins.then_inc(SM["m"], 1)

            for b in range(2):
                rows3(b, b)
            with dve.Fori(1, B // 2) as i:
                for u in range(2):
                    rows3(2 * i + u, u)

            wide = lambda t: t[:].unsqueeze(2).broadcast_to(EW)
            ranks = erank[0:T, :].unsqueeze(1).broadcast_to(EW)

            def choose(src, top, one):
                ch.link(dve.tensor_reduce(top[:], src, AX, ALU.max))
                ch.link(dve.tensor_tensor(hit, src, wide(top), ALU.is_equal))
                ch.link(dve.tensor_tensor(hit, hit, ranks, ALU.mult))
                ch.link(dve.tensor_reduce(cm[:], hit, AX, ALU.max))
                ch.link(dve.tensor_tensor(one[:], ranks, wide(cm), ALU.is_equal))

            dve.wait_ge(SM["logit"], B)
            ch.link(dve.tensor_copy(logit[:], bank[2][0:T, :].rearrange("p (n e) -> p n e", e=E)))
            choose(logit[:], top1, sel1)
            ch.link(dve.scalar_tensor_tensor(pick, sel1[:], MASKED, logit[:], ALU.mult, ALU.add))
            choose(pick, top2, sel2)
            dve.tensor_tensor(sel[:], sel1[:], sel2[:], ALU.add).then_inc(SM["sel"], 1)
            ch.link(dve.tensor_tensor(top2[:], top2[:], top1[:], ALU.subtract))
            dve.sem_inc(SM["gap"], 1)
            dve.wait_ge(SM["ex"], 1)
            ch.link(dve.tensor_scalar(w1[:], ex2[:], 1.0, None, ALU.add))
            ch.link(dve.reciprocal(w1[:], w1[:]))
            ch.link(dve.tensor_tensor(w2[:], ex2[:], w1[:], ALU.mult))
            dve.tensor_tensor(M[:, :, D + 2:D + 3], w1[:].unsqueeze(2), w2[:].unsqueeze(2), ALU.subtract)
            dve.tensor_copy(M[:, :, D + 3:D + 4], w2[:].unsqueeze(2))
            dve.wait_ge(SM["cum"], 1)
            tot = bank[4][0:T, :].rearrange("p (n e) -> p n e", e=E)
            ch.link(dve.tensor_copy(run_a, tot))
            cur, nxt, step = run_a, run_b, 1
            while step < NT:
                dve.tensor_copy(nxt[:, 0:step, :], cur[:, 0:step, :])
                ch.link(dve.tensor_tensor(nxt[:, step:NT, :], cur[:, step:NT, :], cur[:, 0:NT - step, :], ALU.add))
                cur, nxt, step = nxt, cur, 2 * step
            ch.link(dve.tensor_scalar(cnt_i[:], cur[:, NT - 1, :], float(MT - 1), None, ALU.add))
            ch.link(dve.tensor_scalar(til_i[:], cnt_i[:], MT.bit_length() - 1, None, ALU.arith_shift_right))
            ch.link(dve.tensor_copy(til[:], til_i[:]))
            ch.link(dve.tensor_tensor(nxt, cur, tot, ALU.subtract))
            ends, spare, step = til, end_a, 1
            while step < E:
                dve.tensor_copy(spare[:, 0:step], ends[:, 0:step])
                ch.link(dve.tensor_tensor(spare[:, step:E], ends[:, step:E], ends[:, 0:E - step], ALU.add))
                ends, spare, step = spare, (end_b if spare is end_a else end_a), 2 * step
            ch.link(dve.tensor_tensor(base[:], ends[:], til[:], ALU.subtract))
            ch.link(dve.tensor_scalar(base[:], base[:], float(MT), None, ALU.mult))
            ch.link(dve.tensor_tensor(pos[:], bank[3][0:T, :].rearrange("p (n e) -> p n e", e=E), nxt, ALU.add))
            ch.link(dve.tensor_tensor(pos[:], pos[:], base[:].unsqueeze(1).broadcast_to(EW), ALU.add))
            ch.link(dve.tensor_tensor(sel1[:], sel1[:], pos[:], ALU.mult))
            ch.link(dve.tensor_tensor(sel2[:], sel2[:], pos[:], ALU.mult))
            ch.link(dve.tensor_reduce(pos1[:], sel1[:], AX, ALU.add))
            ch.link(dve.tensor_reduce(pos2[:], sel2[:], AX, ALU.add))
            dve.tensor_copy(M[:, :, D + 1:D + 2], pos1[:].unsqueeze(2))
            dve.tensor_copy(pos1i[:], pos1[:])
            dve.tensor_copy(pos2i[:], pos2[:]).then_inc(SM["slot"], 1)
            ch.link(dve.tensor_tensor(past, tileno[:].unsqueeze(2).broadcast_to([1, NMT, E]),
                                      ends[0:1, :].unsqueeze(1).broadcast_to([1, NMT, E]), ALU.is_ge))
            ch.link(dve.tensor_reduce(texp_f[:], past, AX, ALU.add))
            dve.tensor_scalar(texp[:], texp_f[:], float(E - 1), None, ALU.min).then_inc(SM["texp"], 1)

            dve.wait_ge(SM["dispatched"], 16 * 2 * NT)

            def hidden(k, u):
                dve.wait_ge(s_sg, k + 1)
                dve.tensor_tensor(hb[:, u], UP[u][:, 0:FF], sg[:, u], ALU.mult).then_inc(s_h, 1)

            def result(k, u, slot):
                row = xg[:, slot]
                ch.link(dve.tensor_scalar(wv_[:, u, 0:1], row[:, D + 1:D + 2], slotno[:, bass.ds(k, 1)], row[:, D + 2:D + 3],
                                          ALU.is_equal, ALU.mult))
                ch.link(dve.tensor_tensor(wv_[:, u, 1:2], wv_[:, u, 0:1], row[:, D + 3:D + 4], ALU.add))
                wait(dve, s_add, 16 * (k - 1))
                dve.wait_ge(s_dn, k + 1)
                dve.tensor_scalar(ys[:, u], bank[2][:, 0:D], wv_[:, u, 1:2], None, ALU.mult).then_inc(s_y, 1)

            def tile(k, u, slot, last=False):
                result(k, u, slot)
                if not last:
                    hidden(k + 1, 1 - u)

            hidden(0, 0)
            for k in range(NX + 1):
                tile(k, k % 2, k % NX)
            ch.settle()
            with dve.Fori(1, NMT // NX - 1) as i:
                ch.enter(i - 1, 2 * NX)
                for r in range(1, NX + 1):
                    tile(NX * i + r, r % 2, r % NX)
            ch.leave(NMT // NX - 2)
            for k in range(NMT - NX + 1, NMT):
                tile(k, k % 2, k % NX, k == NMT - 1)

        @block.tensor
        def _(pe):
            pe.wait_ge(s_const, 48)
            pe.wait_ge(s_score, 1)
            pe.transpose(TX1[0:NT0, 0:HALF], score[:], ident[0:HALF, 0:HALF]).then_inc(s_score_tp, 1)
            pe.wait_ge(s_w1, 16 * 6)

            def transpose_x(b, u):
                pe.wait_ge(s_xn1, b + 1)
                wait(pe, s_xT1, b)
                for c in range(2):
                    for h in range(2):
                        ins = pe.transpose(TX1[0:C, c * S + h * T:c * S + h * T + T], xn1[:, u, h, c * C:(c + 1) * C], ident[0:T, 0:T])
                ins.then_inc(s_xTp1, 1)

            def project(w, x, dst, m0):
                for m in range(2):
                    for c in range(2):
                        ins = pe.matmul(dst[:, m * S:(m + 1) * S], w[:, c, 128 * (m0 + m):128 * (m0 + m + 1)], x[:, c, :],
                                        start=c == 0, stop=c == 1)
                return ins

            def queries(b, u, h):
                pe.wait_ge(s_xT1, b + 1)
                wait(pe, s_q1, 2 * b + h - 1 if isinstance(b, int) else 2 * (b - 1) + h + 1)
                if isinstance(b, int) and b == 0:
                    pe.wait_ge(s_kv, h + 1)
                project(wq, xT1[:, u], Q1[h], 2 * h).then_inc(s_qp1, 1)

            def scores(b, u, k):
                tile, heads = UNITS1[k]
                if k % 2 == 0 or True:
                    pe.wait_ge(s_q1, 2 * b + (2 if k < 2 or k >= 4 else 1))
                if isinstance(b, int) and b == 0 and k < 2:
                    pe.wait_ge(s_kv, 3)
                else:
                    pe.wait_ge(s_p1, NU1 * b + k - 1)
                w = S if tile == 0 else T
                for n, hd in enumerate(heads):
                    base = 64 * (hd % 2)
                    ins = pe.matmul(SC1[k % 2][0:T, n * w:(n + 1) * w], kT1[base:base + DK, hd // 2, tile * T:tile * T + T],
                                    qT1[base:base + DK, u, hd // 2, S - w:S], start=True, stop=True)
                ins.then_inc(s_sc1, 1)

            def retrieve(b, u, h):
                pe.wait_ge(s_p1, NU1 * b + (4 if h == 0 else 6))
                wait(pe, s_r1, 2 * b + h - 1 if isinstance(b, int) else 2 * (b - 1) + h + 1)
                for m in range(2):
                    for e in range(2):
                        hd = 4 * h + 2 * m + e
                        o = R1[h][64 * e:64 * e + DK, m * S:(m + 1) * S]
                        pe.matmul(o, vg[:, 0, hd, :], p0[:, u, hd, :], start=True, stop=False, skip_group_check=True)
                        ins = pe.matmul(o[:, T:S], vg[:, 1, hd, :], p1[:, u, hd, :], start=False, stop=True, skip_group_check=True)
                ins.then_inc(s_rp1, 1)

            def output(b, u):
                pe.wait_ge(s_r1, 2 * b + 2)
                wait(pe, s_h1, b)
                for h in range(2):
                    for m in range(4):
                        ins = pe.matmul(O1[0:T, h * D:(h + 1) * D], rT1[:, u, m, h * T:(h + 1) * T], wo[:, m, :],
                                        start=m == 0, stop=m == 3)
                ins.then_inc(s_o1, 1)

            transpose_x(0, 0)
            pe.wait_ge(s_xT1, 1)
            for h in range(2):
                project(wk, xT1[:, 0], Q1[h], 2 * h).then_inc(s_kvg, 1)
            for h in range(2):
                for c in range(2):
                    pe.matmul(SC1[h][0:T, :], xT1[:, 0, c, h * T:(h + 1) * T], wv[:, c, :], start=c == 0, stop=c == 1)
            for h in range(2):
                for c in range(2):
                    ins = pe.matmul(O1[0:T, h * NH:(h + 1) * NH], xT1[:, 0, c, h * T:(h + 1) * T], wg[:, c, :], start=c == 0, stop=c == 1)
            ins.then_inc(s_kvg, 1)
            for h in range(2):
                queries(0, 0, h)

            def body(b, u, nxt):
                for k in range(4):
                    scores(b, u, k)
                if nxt is not None:
                    transpose_x(nxt, 1 - u)
                scores(b, u, 4)
                scores(b, u, 5)
                retrieve(b, u, 0)
                if nxt is not None:
                    queries(nxt, 1 - u, 0)
                retrieve(b, u, 1)
                if nxt is not None:
                    queries(nxt, 1 - u, 1)
                output(b, u)

            body(0, 0, 1)
            with pe.Fori(0, B // 2 - 1) as i:
                body(2 * i + 1, 1, 2 * i + 2)
                body(2 * i + 2, 0, 2 * i + 3)
            body(B - 1, 1, None)

            pe.wait_ge(s_h1, B)
            pe.wait_ge(s_w2, 16 * 6)
            pe.wait_ge(s_w2b, 2)

            def transpose_xr(b):
                pe.wait_ge(s_xr, b + 1)
                wait(pe, s_h2, 2 * (b - 1))
                for c in range(2):
                    for h in range(2):
                        ins = pe.transpose(MISC[0:C, c * S + h * T:c * S + h * T + T], xr[:, h, c * C:(c + 1) * C], ident[0:T, 0:T])
                ins.then_inc(s_xTp2, 1)

            def project2(b, j, groups=range(NKV)):
                pe.wait_ge(s_xrT, b + 1)
                wait(pe, s_qkT, 2 * b + j)
                for g in groups:
                    for c in range(2):
                        ins = pe.matmul(proj[0:T, g, 0:GW], xrT[:, c, j * T:(j + 1) * T], wqkv[:, c, g, :], start=c == 0, stop=c == 1)
                if g == NKV - 1:
                    ins.then_inc(s_proj, 1)

            def transpose_qk(b, j):
                pe.wait_ge(s_rot, 2 * b + j + 1)
                pe.wait_ge(s_val, 2 * b + j + 1)
                for g in range(NKV):
                    for k in range(3):
                        ins = pe.transpose(proj[:, g, k * T:(k + 1) * T], rot[:, j, g, 128 * k:128 * (k + 1)], ident[0:T, 0:T])
                ins.then_inc(s_qkTp, 1)

            def scores2(b, u, k):
                tile, heads = UNITS2[k]
                nh, w = len(heads), (T, S)[tile]
                pe.wait_ge(s_qkT, 2 * b + tile + 1)
                wait(pe, s_sx, NU2 * b + k - 1)
                dst = SC2[k % 2][0:T, 0:nh * w].rearrange("p (n t) -> p n t", n=nh)
                pe.matmul(dst[:, :, w - T:w], ident_b[:], causal_b[:].unsqueeze(1).broadcast_to([T, nh, T]),
                          start=True, stop=False, skip_group_check=True)
                for n, hd in enumerate(heads):
                    base, g, m = HD * (hd % 2), hd // 4, (hd % 4) // 2
                    ins = pe.matmul(dst[:, n, :], qkT[base:base + HD, u, g, m, tile * T:tile * T + T], qkT[base:base + HD, u, g, 2, 0:w],
                                    start=False, stop=n == nh - 1, skip_group_check=True)
                ins.then_inc(s_sc2, 1)

            def transpose_p(b, k):
                tile, heads = UNITS2[k]
                pe.wait_ge(s_pr, NU2 * b + k + 1)
                wait(pe, s_pT, NU2 * b + k)
                for n in range(len(heads) * (tile + 1)):
                    ins = pe.transpose(PT2[0:T, n * T:(n + 1) * T], pr[:, k % 2, n * T:(n + 1) * T], ident[0:T, 0:T])
                ins.then_inc(s_tp, 1)

            def weigh(b, u, k):
                tile, heads = UNITS2[k]
                pe.wait_ge(s_pT, NU2 * b + k + 1)
                half = {0: 0, 2: 1, 4: 2, 7: 3}.get(k)
                if half is not None:
                    wait(pe, s_on, 4 * b + half)
                for n, hd in enumerate(heads):
                    o = O2[0:T, (hd // 2) * (HD + 1):(hd // 2 + 1) * (HD + 1)]
                    for blk in range(tile + 1):
                        q = n * (tile + 1) + blk
                        ins = pe.matmul(o, pT[:, k % 2, q * T:(q + 1) * T], val[:, u, blk, hd // 4, :], start=blk == 0, stop=blk == tile)
                ins.then_inc(s_pv, 1)

            def transpose_o(b, j, h, nxt):
                pe.wait_ge(s_on, 4 * b + 2 * j + 2)
                if h == 1:
                    pe.wait_ge(s_oT, 4 * b + 2 * j + 1)
                elif j == 1:
                    pe.wait_ge(s_h2, 2 * b + 1)
                elif nxt is not None:
                    pe.wait_ge(s_xrT, nxt + 1)
                else:
                    pe.wait_ge(s_h2, 2 * b)
                for m in range(3):
                    ins = pe.transpose(MISC[:, m * T:(m + 1) * T], oh[:, j, 128 * (3 * h + m):128 * (3 * h + m + 1)], ident[0:T, 0:T])
                ins.then_inc(s_oTp, 1)

            def output2(b, j):
                pe.wait_ge(s_oT, 4 * b + 2 * j + 2)
                for m in range(6):
                    ins = pe.matmul(MISC[0:T, 0:D], oT[:, j, m, :], wout[:, m, :], start=m == 0, stop=m == 5)
                ins.then_inc(s_wo, 1)

            transpose_xr(0)
            project2(0, 0)
            transpose_qk(0, 0)
            project2(0, 1)

            def body2(b, u, nxt):
                for k in range(NU2 + 3):
                    if k < NU2:
                        scores2(b, u, k)
                    if k == 2:
                        transpose_qk(b, 1)
                    if 2 <= k < NU2 + 2:
                        transpose_p(b, k - 2)
                    if k >= 3:
                        weigh(b, u, k - 3)
                    if k == 3 and nxt is not None:
                        transpose_xr(nxt)
                    if k == 4 and nxt is not None:
                        project2(nxt, 0)
                    if k == 8 and nxt is not None:
                        transpose_qk(nxt, 0)
                    if k in (8, 9):
                        transpose_o(b, 0, k - 8, nxt)
                    if k == 10:
                        output2(b, 0)
                if nxt is not None:
                    project2(nxt, 1, [0])
                transpose_o(b, 1, 0, nxt)
                if nxt is not None:
                    project2(nxt, 1, [1])
                transpose_o(b, 1, 1, nxt)
                if nxt is not None:
                    project2(nxt, 1, [2])
                output2(b, 1)

            body2(0, 0, 1)
            with pe.Fori(0, B // 2 - 1) as i:
                body2(2 * i + 1, 1, 2 * i + 2)
                body2(2 * i + 2, 0, 2 * i + 3)
            body2(B - 1, 1, None)

            def transpose_m(b, u):
                pe.wait_ge(SM["m"], b + 1)
                wait(pe, SM["mT"], b - 1)
                for c in range(2):
                    for h in range(2):
                        ins = pe.transpose(bank[u][0:C, c * S + h * T:c * S + h * T + T], mrow[:, u, h, c * C:(c + 1) * C],
                                           ident[0:T, 0:T])
                ins.then_inc(SM["mTp"], 1)

            def route(b, u):
                pe.wait_ge(SM["mT"], b + 1)
                for h in range(2):
                    for c in range(2):
                        ins = pe.matmul(bank[2][0:T, bass.ds((2 * b + h) * E, E)], mT[:, u, c, h * T:(h + 1) * T], wr[:, c, :],
                                        start=c == 0, stop=c == 1)
                ins.then_inc(SM["logit"], 1)

            pe.wait_ge(s_hadd, 2 * B)
            pe.wait_ge(SM["c3"], 16 * 8)
            for b in range(2):
                transpose_m(b, b)
                route(b, b)
            with pe.Fori(1, B // 2) as i:
                for u in range(2):
                    transpose_m(2 * i + u, u)
                    route(2 * i + u, u)
            pe.wait_ge(SM["sel"], 1)
            pe.wait_ge(SM["rr3"], 1)
            pe.matmul(bank[3][0:T, :], before[:], sel[:].rearrange("p n e -> p (n e)"), start=True, stop=True)
            pe.matmul(bank[4][0:T, :], ones[:], sel[:].rearrange("p n e -> p (n e)"), start=True, stop=True).then_inc(SM["cum"], 1)

            def transpose_rows(k, u, slot, turn):
                pe.wait_ge(s_xg[slot], 16 * (turn + 1))
                wait(pe, s_xgT, k)
                for c in range(2):
                    ins = pe.transpose(bank[0][0:C, c * MT:(c + 1) * MT], xg[:, slot, c * C:(c + 1) * C], ident[:])
                ins.then_inc(s_xgTp, 1)

            def expert_of(k):
                return pe.value_load(texp[0:1, bass.ds(k, 1)], min_val=0, max_val=E - 1)

            def up(k, u, e, part):
                pe.wait_ge(s_xgT, k + 1)
                dst = (GATE, UP)[part][u]
                for c in range(2):
                    ins = pe.matmul(dst[:, 0:FF], xgT[:, u, c, :], wgu[:, bass.ds(e * (4 * FF) + (2 * c + part) * FF, FF)],
                                    start=c == 0, stop=c == 1)
                if part:
                    ins.then_inc(s_up, 1)

            def transpose_h(k, u):
                pe.wait_ge(s_h, k + 1)
                for m in range(3):
                    ins = pe.transpose(bank[1][:, m * MT:(m + 1) * MT], hb[:, u, m * MT:(m + 1) * MT], ident[:])
                ins.then_inc(s_hTp, 1)

            def down(k, u, e):
                pe.wait_ge(s_hT, k + 1)
                wait(pe, s_y, k)
                for m in range(3):
                    ins = pe.matmul(bank[2][:, 0:D], hT[:, u, m, :], wdn[:, bass.ds(e * (3 * D) + m * D, D)], start=m == 0, stop=m == 2)
                ins.then_inc(s_dn, 1)

            def tile(k, u, slot, turn, last=False):
                if not last:
                    transpose_rows(k + 1, 1 - u, slot, turn)
                    e_next = expert_of(k + 1)
                    up(k + 1, 1 - u, e_next, 0)
                transpose_h(k, u)
                if not last:
                    up(k + 1, 1 - u, e_next, 1)
                down(k, u, expert_of(k))

            pe.wait_ge(SM["texp"], 1)
            pe.wait_ge(SM["we"], 16 * 8)
            transpose_rows(0, 0, 0, 0)
            e0 = expert_of(0)
            up(0, 0, e0, 0)
            up(0, 0, e0, 1)
            for k in range(NX + 1):
                tile(k, k % 2, (k + 1) % NX, (k + 1) // NX)
            with pe.Fori(1, NMT // NX - 1) as i:
                for r in range(1, NX + 1):
                    tile(NX * i + r, r % 2, (r + 1) % NX, i + (r + 1) // NX)
            for k in range(NMT - NX + 1, NMT):
                tile(k, k % 2, (k + 1) % NX, (k + 1) // NX, k == NMT - 1)


def host_layout(inputs):
    f = {k: np.asarray(v) for k, v in inputs.items()}
    rows = lambda v: np.ascontiguousarray(np.broadcast_to(v.reshape(1, -1), (128, v.size)))
    chunk = lambda w, k: np.ascontiguousarray(w.reshape(w.shape[0] // k, k, w.shape[1]).transpose(1, 0, 2))
    a = {"x": f["x"], "gamma": rows(f["L0_tok_gamma"]), "beta": rows(f["L0_tok_beta"]), "tokw": rows(f["L0_tok_w"]),
         "tokb": rows(f["L0_tok_b"]),
         "wq": chunk(f["L0_attn_w_query"].T, C), "wk": chunk(f["L0_attn_w_key"].T, C), "wv": chunk(f["L0_attn_w_value"].T, C),
         "wg": chunk(f["L0_attn_w_gate"].T, C), "wo": chunk(f["L0_attn_w_out"].T, 128)}
    w = f["L0_ffn_w_qkv"]
    split = lambda v: v.reshape(D, -1, HD // 2, 2).transpose(0, 1, 3, 2)
    q = split(w[:, :NQ * HD]).reshape(D, NKV, NQ // NKV * HD)
    k = split(w[:, NQ * HD:(NQ + NKV) * HD]).reshape(D, NKV, HD)
    v = w[:, (NQ + NKV) * HD:].reshape(D, NKV, HD)
    a["wqkv"] = chunk(np.concatenate([q, k, v], 2).reshape(D, NKV * GW), C).reshape(C, 2, NKV, GW)
    a["wout"] = chunk(f["L0_ffn_w_out"], 128)
    a["norm2w"] = rows(f["L0_ffn_norm2_w"])[:T]
    a["wr"] = chunk(f["L0_ffn_w_router"], C)
    a["wgu"] = f["L0_ffn_w_gate_up"].reshape(E, 2, C, 2 * FF).transpose(2, 0, 1, 3).reshape(C, E * 4 * FF)
    a["wdn"] = f["L0_ffn_w_down"].reshape(E, 3, FF // 3, D).transpose(2, 0, 1, 3).reshape(FF // 3, E * 3 * D)
    a["norm1w"] = rows(f["L0_ffn_norm1_w"])[:T]
    a.update(constants())
    return a


def kernel(**inputs):
    import concourse.bacc as _bacc
    from concourse import mybir as _mybir
    from concourse.bass_utils import run_bass_kernel_spmd as _run

    nc = _bacc.Bacc("TRN2", target_bir_lowering=False, num_devices=1)
    arrays, args = {}, {}
    for name, v in host_layout(inputs).items():
        v = np.ascontiguousarray(v)
        arrays[f"in_{name}"] = v
        args[name] = nc.dram_tensor(f"in_{name}", v.shape, _mybir.dt.from_np(v.dtype), kind="ExternalInput").ap()
    out = nc.dram_tensor("out_0", (B, KEEP, D), _mybir.dt.float32, kind="ExternalOutput").ap()
    build(nc, args, out, 1)
    r = _run(nc, [arrays], core_ids=[0])
    return r.results[0]["out_0"]
```

```python
from contextlib import ExitStack

import numpy as np

import concourse.bass as bass
from concourse import mybir

F32 = mybir.dt.float32
BF16 = mybir.dt.bfloat16
I32 = mybir.dt.int32
ALU = mybir.AluOpType
ACT = mybir.ActivationFunctionType
AX = mybir.AxisListType.X

B, N0, D = 16, 250, 192
KEEP = int(N0 * 0.7)
HALF = N0 // 2
NT0 = 2 * B
T = (KEEP + 1) // 2
S = 2 * T
NT = 2 * B
NG = 4
GB = B // NG
C = D // 2
LN_EPS = 1e-5
RMS_EPS = 1e-6
NH, DK = 8, 64
DECAY, WRITE = 0.95, 0.1
NQ, NKV, HD = 12, 3, 64
THETA = 10000.0
GW = (NQ // NKV + 2) * HD
QKW = (NQ // NKV + 1) * HD
E, FF = 16, 384
MT = 128
NMT = (2 * NT * T + E * (MT - 1)) // MT
NMT += NMT % 2
RW = D + 4
GR = 4
NEARLY = 6
CAP = NT * T + MT
MASKED = -1e30
NX = 4
NOROW = 1 << 20


def constants():
    t = np.arange(S)
    c = {}
    s_, t_ = np.arange(T)[:, None], t[None, :]
    c["decay"] = np.where(s_ < t_, WRITE * DECAY ** np.maximum(t_ - 1 - s_, 0), 0.0).astype(np.float32)
    c["ident"] = np.eye(128, dtype=np.float32)
    inv = 1.0 / THETA ** (np.arange(0, HD, 2, dtype=np.float32) / HD)
    f = t[:, None].astype(np.float32) * inv[None, :].astype(np.float32)
    cos, sin = np.cos(f).astype(np.float32), np.sin(f).astype(np.float32)
    tile = lambda a: np.ascontiguousarray(a.reshape(2, T, -1).transpose(1, 0, 2))
    c["cos"] = tile(np.concatenate([cos, cos], 1))
    c["sin"] = tile(np.concatenate([-sin, sin], 1))
    c["causal"] = np.where(np.arange(T)[None, :] <= np.arange(T)[:, None], 0.0, MASKED).astype(np.float32)
    j = np.arange(N0)[None, :]
    c["earlier"] = np.stack([(j < HALF * h + np.arange(HALF)[:, None]) for h in range(2)], 1).astype(np.float32)
    c["rowbase"] = np.broadcast_to((N0 * (np.arange(NT0) // 2)).astype(np.float32), (128, NT0)).copy()
    c["before"] = (np.arange(T)[:, None] < np.arange(T)[None, :]).astype(np.float32)
    c["erank"] = np.broadcast_to((E - np.arange(E)).astype(np.float32), (128, E)).copy()
    row = KEEP * (np.arange(NT) // 2)[None, :] + T * (np.arange(NT) % 2)[None, :] + np.arange(T)[:, None]
    kept = T * (np.arange(NT) % 2)[None, :] + np.arange(T)[:, None] < KEEP
    c["outrow"] = np.where(kept, row, NOROW).astype(np.int32).view(np.float32)
    blank = np.zeros((MT, RW), np.int32)
    blank[:, D] = NOROW
    c["blank"] = blank.view(np.float32)
    c["tileno"] = np.broadcast_to(np.arange(NMT, dtype=np.float32), (MT, NMT)).copy()
    c["region"] = np.broadcast_to((CAP * np.arange(E)).astype(np.float32), (MT, E)).copy()
    return c


def build(nc, a, out):
    scores_d = nc.dram_tensor("scores_d", (NT0, HALF), F32).ap()
    rows_d = nc.dram_tensor("rows_d", (E * CAP + MT, RW), F32).ap()
    sorted_d = nc.dram_tensor("sorted_d", (B * N0, D), F32).ap()

    ctx = ExitStack()
    with ctx:
        def sb_in(stack, name, shape, dt=F32, side="left"):
            return stack.enter_context(nc.sbuf_tensor(name, shape, dt, side=side))

        def right(stack, name, shape, dt=F32):
            return sb_in(stack, name, shape, dt, "right")

        def sem(name):
            return ctx.enter_context(nc.semaphore(name))

        bank = [ctx.enter_context(nc.psum_tensor(f"bank{i}", [128, 512], F32)) for i in range(5)]
        proj = ctx.enter_context(nc.psum_tensor("proj", [128, 3, 512], F32))

        H = sb_in(ctx, "H", [T, NT, D])
        ident = sb_in(ctx, "ident", [128, 128])
        neg_half = sb_in(ctx, "neg_half", [128, NT])
        ln_eps = sb_in(ctx, "ln_eps", [128, 2])
        rms_eps = sb_in(ctx, "rms_eps", [128, 2])
        M = sb_in(ctx, "M", [T, NT, D])
        ms = sb_in(ctx, "ms", [T, NT])

        before_b = sb_in(ctx, "before_b", [T, T], BF16)
        ones_b = sb_in(ctx, "ones_b", [T, MT], BF16)
        erank = sb_in(ctx, "erank", [128, E])
        tileno = sb_in(ctx, "tileno", [MT, NMT])
        run = sb_in(ctx, "run", [MT, E])
        region = sb_in(ctx, "region", [MT, E])
        outrow = sb_in(ctx, "outrow", [T, NT])
        blank = sb_in(ctx, "blank", [MT, RW])
        wr = sb_in(ctx, "wr", [C, 2, E])
        rr2 = sb_in(ctx, "rr2", [T, NT])
        rr3 = sb_in(ctx, "rr3", [T, NT])
        texp = sb_in(ctx, "texp", [1, NMT], I32)
        tstart = sb_in(ctx, "tstart", [1, NMT], I32)
        rexp = sb_in(ctx, "rexp", [MT, NMT])
        cnt_i = sb_in(ctx, "cnt_i", [MT, E], I32)
        logit, sel1, sel2, hit, pick, pos = (sb_in(ctx, n, [T, GR, E]) for n in "logit sel1 sel2 hit pick pos".split())
        sel_b = sb_in(ctx, "sel_b", [T, GR, E], BF16)
        top1, top2, cm, cm2, ex2, w1, w2 = (sb_in(ctx, n, [T, GR]) for n in "top1 top2 cm cm2 ex2 w1 w2".split())
        send = sb_in(ctx, "send", [T, 2, GR, RW])
        slot_f = sb_in(ctx, "slot_f", [T, 2, GR])
        slot = sb_in(ctx, "slot", [T, 2, 2, GR], I32)

        early, selection, attn = ExitStack(), ExitStack(), ExitStack()
        wq = sb_in(early, "wq", [C, 2, NH * DK])
        wk = sb_in(early, "wk", [C, 2, NH * DK])
        wv = sb_in(early, "wv", [C, 2, NH * DK])
        wg = sb_in(early, "wg", [C, 2, NH])
        wo = sb_in(early, "wo", [128, NH * DK // 128, D])
        decay = sb_in(early, "decay", [T, S])
        st1 = sb_in(early, "st1", [T, 2, 6])
        mv1 = sb_in(early, "mv1", [T, 2, 2, 2])
        rs1 = sb_in(early, "rs1", [T, 2, 2])
        xn1 = sb_in(early, "xn1", [T, 2, 2, D])
        hx1 = sb_in(early, "hx1", [T, 2, 2, D])
        xT1 = sb_in(early, "xT1", [C, 2, 2, S])
        qT1 = sb_in(early, "qT1", [128, 2, 4, S])
        kT1 = sb_in(early, "kT1", [128, 4, S])
        gate = sb_in(early, "gate", [T, 2, NH])
        vg = sb_in(early, "vg", [T, 2, NH, DK])
        p0 = sb_in(early, "p0", [T, 2, NH, S])
        p1 = sb_in(early, "p1", [T, 2, NH, T])
        rT1 = sb_in(early, "rT1", [128, 2, 4, S])
        mv2 = sb_in(early, "mv2", [T, 2, 2, 2])
        rs2 = sb_in(early, "rs2", [T, 2, 2])
        ms2 = sb_in(early, "ms2", [T, 2])
        st2 = sb_in(early, "st2", [T, 2, 6])

        X = right(selection, "X", [HALF, NT0, D])
        GT = NT0 // NG
        Xc = right(selection, "Xc", [HALF, 2, GT, D])
        Xsq = right(selection, "Xsq", [HALF, 2, GT, D])
        Xgw = right(selection, "Xgw", [HALF, 2, GT, D])
        gamma = right(selection, "gamma", [128, D])
        beta = right(selection, "beta", [128, D])
        tokw = right(selection, "tokw", [128, D])
        tokb = right(selection, "tokb", [128, 1])
        gw = right(selection, "gw", [128, D])
        bw = right(selection, "bw", [128, D])
        bsum = right(selection, "bsum", [128, 1])
        mu = right(selection, "mu", [HALF, NT0])
        var = right(selection, "var", [HALF, NT0])
        dot = right(selection, "dot", [HALF, NT0])
        rs0 = right(selection, "rs0", [HALF, NT0])
        score = right(selection, "score", [HALF, NT0])
        score_t = right(selection, "score_t", [NT0, HALF])
        all_scores = right(selection, "all_scores", [HALF, NT0 * HALF])
        earlier = right(selection, "earlier", [HALF, 2, N0])
        rowbase = right(selection, "rowbase", [128, NT0])
        above = right(selection, "above", [HALF, NT0])
        tied = right(selection, "tied", [HALF, NT0])
        flat = lambda t: t[:].rearrange("p a b d -> p (a b d)")[:, 0:GT * N0].rearrange("p (k n) -> p k n", k=GT)
        junk_a, junk_b = flat(Xsq), flat(Xgw)
        rank = right(selection, "rank", [HALF, NT0], I32)

        selection.close()

        early.close()

        wdn = right(ctx, "wdn", [FF // 3, E * 3 * D])
        wqkv = right(attn, "wqkv", [C, 2, NKV, GW])
        before = right(attn, "before", [T, T])
        norm2w = right(attn, "norm2w", [T, D])
        wout = right(attn, "wout", [128, NQ * HD // 128, D])
        cos = right(attn, "cos", [T, 2, HD])
        sin = right(attn, "sin", [T, 2, HD])
        norm1w = right(attn, "norm1w", [T, D])
        causal = right(attn, "causal", [T, T])
        causal_b = right(attn, "causal_b", [T, T], BF16)
        ident_b = right(attn, "ident_b", [T, T], BF16)
        xr = right(attn, "xr", [T, 2, D])
        xrT = right(attn, "xrT", [C, 2, 2, S])
        rope_c = right(attn, "rope_c", [T, 2, QKW])
        rope_s = right(attn, "rope_s", [T, 2, QKW])
        rot = right(attn, "rot", [T, 2, QKW + HD])
        qkT = right(attn, "qkT", [128, 2, NKV, 3, S])
        val = right(attn, "val", [T, 2, 2, NKV, HD + 1])
        mx = right(attn, "mx", [T, 2, 3])
        sx = right(attn, "sx", [T, 2, 2 * S])
        pr = right(attn, "pr", [T, 2, 2 * S])
        pT = right(attn, "pT", [T, 2, 2 * S])
        rden = right(attn, "rden", [T, 2, NQ // 2])
        oh = right(attn, "oh", [T, 2, NQ * HD])
        oT = right(attn, "oT", [128, 2, 6, T])
        sqj = right(attn, "sqj", [T, 2, D])
        mrow = right(attn, "mrow", [T, 2, D])
        mT = right(attn, "mT", [C, 2, S])
        attn.close()

        moe = ctx
        wgu = sb_in(ctx, "wgu", [C, E * 4 * FF])
        til, end_a, end_b, skip = (sb_in(ctx, n, [MT, E]) for n in ("til", "end_a", "end_b", "skip"))
        til_i = sb_in(ctx, "til_i", [MT, E], I32)
        table = ExitStack()
        past = sb_in(table, "past", [MT, NMT, E])
        jump = sb_in(table, "jump", [MT, NMT, E])
        texp_f = sb_in(table, "texp_f", [MT, NMT])
        tstart_f = sb_in(table, "tstart_f", [MT, NMT])
        table.close()
        xg = sb_in(moe, "xg", [MT, NX, RW])
        xgT = sb_in(moe, "xgT", [C, 2, 2, MT])
        sg = sb_in(moe, "sg", [MT, 2, FF])
        hb = sb_in(moe, "hb", [MT, 2, FF])
        hT = sb_in(moe, "hT", [MT, 2, 3, MT])
        wv_ = sb_in(moe, "wv_", [MT, 2, 2])
        ys = sb_in(moe, "ys", [MT, 2, D])

        s_const = sem("s_const")
        s_tok_in = [sem(f"s_tok_in{g}") for g in range(NG)]
        s_tok_vec = sem("s_tok_vec")
        s_dve = sem("s_dve")
        s_apart = sem("s_apart")
        s_pool = sem("s_pool")
        s_centered = sem("s_centered")
        s_squared = sem("s_squared")
        s_weighted = sem("s_weighted")
        s_reduced = sem("s_reduced")
        s_stats = sem("s_stats")
        s_rs0 = sem("s_rs0")
        s_score = sem("s_score")
        s_score_tp = sem("s_score_tp")
        s_score_t = sem("s_score_t")
        s_score_out = sem("s_score_out")
        s_score_in = sem("s_score_in")
        s_rank = sem("s_rank")
        s_sorted = [sem(f"s_sorted{g}") for g in range(NG)]
        s_hzero = sem("s_hzero")
        s_h0 = [sem(f"s_h0{g}") for g in range(NG)]
        s_w1 = sem("s_w1")

        SM = {n: sem("s_" + n) for n in ("c3 we blank base ms rr3 m back mTp mT logit logit_in gap ex sel sel_b cum cum_read bf slot texp count fill").split()}
        s_xg = [sem(f"s_xg{i}") for i in range(NX)]
        s_rows = [sem(f"s_rows{u}") for u in range(2)]
        s_xgTp, s_xgT, s_up, s_sg, s_h, s_hTp, s_hT, s_dn, s_y, s_add = (
            sem(n) for n in "s_xgTp s_xgT s_up s_sg s_h s_hTp s_hT s_dn s_y s_add".split())
        SEM = {}
        for n in ("s_w2 s_w2b s_mv2 s_rs2 s_x3 s_xr s_xTp2 s_xrT s_proj s_rope s_rot s_val s_qkTp s_qkT s_sc2 s_sx s_pr s_tp s_pT "
                  "s_pv s_on s_oTp s_oT s_wo s_h2 s_hadd").split():
            SEM[n] = sem(n)
        (s_w2, s_w2b, s_mv2, s_rs2, s_x3, s_xr, s_xTp2, s_xrT, s_proj, s_rope, s_rot, s_val, s_qkTp, s_qkT, s_sc2, s_sx, s_pr,
         s_tp, s_pT, s_pv, s_on, s_oTp, s_oT, s_wo, s_h2, s_hadd) = SEM.values()
        s_mv1 = sem("s_mv1")
        s_rs1 = sem("s_rs1")
        s_xn1 = sem("s_xn1")
        s_hx1 = sem("s_hx1")
        s_xTp1 = sem("s_xTp1")
        s_xT1 = sem("s_xT1")
        s_qp1 = sem("s_qp1")
        s_q1 = sem("s_q1")
        s_kvg = sem("s_kvg")
        s_kv = sem("s_kv")
        s_gate = sem("s_gate")
        s_sc1 = sem("s_sc1")
        s_p1 = sem("s_p1")
        s_rp1 = sem("s_rp1")
        s_r1 = sem("s_r1")
        s_o1 = sem("s_o1")
        s_h1 = sem("s_h1")

        def wait(eng, s, v):
            if isinstance(v, int) and v <= 0:
                return
            eng.wait_ge(s, v)

        def wait_apart(eng, s, v):
            eng.wait_ge(s, v)
            eng.sem_inc(s_apart, 1)

        class Chain:

            def __init__(self, eng, s):
                self.eng, self.s, self.base, self.n = eng, s, 0, 0

            def link(self, ins, apart=False):
                ins.then_inc(self.s, 1)
                self.n += 1
                self.eng.wait_ge(self.s, self.base + self.n)
                if apart:
                    self.eng.sem_inc(s_apart, 1)

            def enter(self, i, per):
                self.start = self.n_done
                self.base, self.n, self.per = self.n_done + i * per, 0, per

            def leave(self, iterations):
                assert self.n == self.per, (self.n, self.per)
                self.n_done = self.start + iterations * self.per
                self.base, self.n = self.n_done, 0

            def settle(self):
                self.n_done = self.base + self.n

        block = ctx.enter_context(nc.Block())
        TX1, Q1A, Q1B, SC1A, SC1B = bank
        R1 = [proj[:, 0, :], proj[:, 1, :]]
        O1 = proj[:, 2, :]
        Q1 = [Q1A, Q1B]
        SC1 = [SC1A, SC1B]
        UNITS1 = [(1, (0, 2, 4, 6)), (1, (1, 3, 5, 7)), (0, (0, 2)), (0, (1, 3)), (0, (4, 6)), (0, (5, 7))]
        NU1 = len(UNITS1)
        UNITS2 = [(0, (0, 2, 4)), (0, (6, 8, 10)), (0, (1, 3, 5)), (0, (7, 9, 11)),
                  (1, (0, 2)), (1, (4, 6)), (1, (8, 10)), (1, (1, 3)), (1, (5, 7)), (1, (9, 11))]
        NU2 = len(UNITS2)
        NCH = 2 * NKV
        NPAIR = B // 2
        PT2, O2, MISC, SC2A, SC2B = bank
        SC2 = [SC2A, SC2B]
        GATE = [bank[3], proj[:, 0, :]]
        UP = [bank[4], proj[:, 1, :]]

        @block.sync
        def _(sp):
            sp.dma_start(gamma[:], a["gamma"]).then_inc(s_tok_vec, 16)
            sp.dma_start(beta[:], a["beta"]).then_inc(s_tok_vec, 16)
            sp.dma_start(tokw[:], a["tokw"]).then_inc(s_tok_vec, 16)
            sp.dma_start(tokb[:], a["tokb"]).then_inc(s_tok_vec, 16)
            for g in range(NG):
                sp.dma_start(X[:, GT * g:GT * (g + 1), :],
                             a["x"][GB * g:GB * (g + 1)].rearrange("b (h p) d -> p (b h) d", h=2)).then_inc(s_tok_in[g], 16)
            sp.dma_start(ident[:], a["ident"]).then_inc(s_const, 16)
            sp.dma_start(earlier[:], a["earlier"]).then_inc(s_const, 16)
            sp.dma_start(rowbase[:], a["rowbase"]).then_inc(s_const, 16)
            for t_, n in ((wq, "wq"), (wk, "wk"), (wv, "wv"), (wg, "wg"), (wo, "wo"), (decay, "decay")):
                sp.dma_start(t_[:], a[n]).then_inc(s_w1, 16)
            sp.wait_ge(s_score_t, 1)
            sp.dma_start(scores_d, score_t[:]).then_inc(s_score_out, 16)
            sp.wait_ge(s_score_out, 16)
            sp.dma_start(all_scores[:], scores_d.rearrange("n p -> (n p)").partition_broadcast(HALF)).then_inc(s_score_in, 16)
            sp.wait_ge(s_hzero, 1)
            for g in range(NG):
                sp.wait_ge(s_sorted[g], 16 * GT)
                rows = sorted_d.rearrange("(b n) d -> n b d", n=N0)
                Hv = H[:].rearrange("p (b h) d -> p b h d", h=2)
                for h in range(2):
                    n = min(T, KEEP - T * h)
                    sp.dma_start(Hv[0:n, GB * g:GB * (g + 1), h, :],
                                 rows[T * h:T * h + n, GB * g:GB * (g + 1), :]).then_inc(s_h0[g], 16)
            for t_, n in ((wqkv, "wqkv"), (wout, "wout"), (cos, "cos"), (sin, "sin"), (norm1w, "norm1w"), (causal, "causal")):
                sp.dma_start(t_[:], a[n]).then_inc(s_w2, 16)
            for t_, n in ((before, "before"), (erank, "erank"), (tileno, "tileno"), (region, "region"), (outrow, "outrow"),
                          (norm2w, "norm2w"), (wr, "wr"), (blank, "blank")):
                sp.dma_start(t_[:], a[n]).then_inc(SM["c3"], 16)
            sp.wait_ge(SM["c3"], 16 * 8)
            sp.dma_start(rows_d[E * CAP:E * CAP + MT, :], blank[:]).then_inc(SM["fill"], 16)
            for q in range(2):
                n = E // 2 * 3 * D
                sp.dma_start(wdn[:, q * n:(q + 1) * n], a["wdn"][:, q * n:(q + 1) * n]).then_inc(SM["we"], 16)
            sp.wait_ge(s_x3, B)
            sp.wait_ge(s_rs2, B)
            for q in range(2):
                n = NEARLY // 2 * 4 * FF
                sp.dma_start(wgu[:, q * n:(q + 1) * n], a["wgu"][:, q * n:(q + 1) * n]).then_inc(SM["we"], 16)
            sp.wait_ge(s_hadd, 2 * B)
            orow = out.rearrange("b t d -> t b d")
            for h in range(2):
                n = min(T, KEEP - T * h)
                Hv = H[:].rearrange("p (b h) d -> p b h d", h=2)
                sp.dma_start(orow[T * h:T * h + n, :, :], Hv[0:n, :, h, :]).then_inc(SM["base"], 16)
            sp.wait_ge(SM["logit_in"], B)
            lo = NEARLY * 4 * FF
            for q in range(2):
                n = (E - NEARLY) // 2 * 4 * FF
                sp.dma_start(wgu[:, lo + q * n:lo + (q + 1) * n], a["wgu"][:, lo + q * n:lo + (q + 1) * n]).then_inc(SM["we"], 16)
            sp.wait_ge(SM["count"], 1)
            for e in range(E):
                end = sp.value_load(cnt_i[0:1, e:e + 1], min_val=0, max_val=E * CAP - MT)
                sp.dma_start(rows_d[bass.ds(end, MT), :], blank[:]).then_inc(SM["fill"], 16)

            def load(k, slot, turn):
                wait(sp, s_add, 16 * (k - NX + 1))
                start = sp.value_load(tstart[0:1, bass.ds(k, 1)], min_val=0, max_val=E * CAP)
                src = rows_d[bass.ds(start, MT), :]
                sp.dma_start(xg[:, slot, :], src).then_inc(s_xg[slot], 16)

            sp.wait_ge(SM["texp"], 1)
            sp.wait_ge(SM["fill"], 16 * (E + 1))
            sp.wait_ge(s_rows[0], 16 * NT)
            sp.wait_ge(s_rows[1], 16 * NT)
            for k in range(NX):
                load(k, k, 0)
            with sp.Fori(1, NMT // NX) as i:
                for r in range(NX):
                    load(NX * i + r, r, i)

        @block.gpsimd
        def _(pool):
            ch = Chain(pool, s_pool)
            pool.memset(neg_half[:], -0.5)
            pool.memset(ln_eps[:], LN_EPS)
            pool.memset(rms_eps[:], RMS_EPS)
            ch.link(pool.memset(H[:], 0.0))
            pool.sem_inc(s_hzero, 1)
            for g in range(NG):
                pool.wait_ge(s_centered, g + 1)
                if g >= 2:
                    pool.wait_ge(s_reduced, g - 1)
                pool.tensor_tensor(Xgw[:, g % 2], Xc[:, g % 2], gw[0:HALF, :].unsqueeze(1).broadcast_to([HALF, GT, D]), ALU.mult).then_inc(s_weighted, 1)
            pool.wait_ge(s_stats, 1)
            pool.tensor_tensor(rs0[:], var[:], neg_half[0:HALF, :], ALU.pow).then_inc(s_rs0, 1)
            for g in range(NG):
                pool.wait_ge(s_rank, g + 1)
                for n in range(GT * g, GT * (g + 1)):
                    pool.indirect_dma_start(out=sorted_d, out_offset=bass.IndirectOffsetOnAxis(ap=rank[:, n:n + 1], axis=0),
                                            in_=X[:, n, :], in_offset=None).then_inc(s_sorted[g], 16)
            ch.settle()

            def norm1(b, u):
                wait_apart(pool, s_mv1, b + 1)
                ch.link(pool.tensor_scalar(rs1[:, u], mv1[:, u, :, 1], LN_EPS, None, ALU.add))
                pool.tensor_tensor(rs1[:, u], rs1[:, u], neg_half[0:T, 0:2], ALU.pow).then_inc(s_rs1, 1)

            def residual1(b, u):
                pool.wait_ge(s_xn1, b + 1)
                pool.tensor_tensor(hx1[:, u], H[:, bass.ds(2 * b, 2), :], xn1[:, u], ALU.add).then_inc(s_hx1, 1)

            def norm2(b, u):
                pool.wait_ge(s_mv2, b + 1)
                ch.link(pool.tensor_tensor(rs2[:, u], mv2[:, u, :, 1], ln_eps[0:T, :], ALU.add))
                ch.link(pool.tensor_tensor(rs2[:, u], rs2[:, u], neg_half[0:T, 0:2], ALU.pow))
                ch.link(pool.tensor_tensor(ms2[:], rs2[:, u], rs2[:, u], ALU.mult))
                ch.link(pool.tensor_tensor(ms2[:], ms2[:], mv2[:, u, :, 1], ALU.mult), apart=True)
                ch.link(pool.tensor_scalar(ms2[:], ms2[:], RMS_EPS, None, ALU.add), apart=True)
                pool.tensor_tensor(rr2[:, bass.ds(2 * b, 2)], ms2[:], neg_half[0:T, 0:2], ALU.pow).then_inc(s_rs2, 1)

            def body(b, u, prev, nxt):
                if nxt is not None:
                    norm1(nxt, 1 - u)
                    residual1(nxt, 1 - u)
                if prev is not None:
                    norm2(prev, 1 - u)

            norm1(0, 0)
            residual1(0, 0)
            body(0, 0, None, 1)
            ch.settle()
            with pool.Fori(0, B // 2 - 1) as i:
                ch.enter(i, 12)
                body(2 * i + 1, 1, 2 * i, 2 * i + 2)
                body(2 * i + 2, 0, 2 * i + 1, 2 * i + 3)
            ch.leave(B // 2 - 1)
            body(B - 1, 1, B - 2, None)
            norm2(B - 1, 1)
            ch.settle()

            pool.wait_ge(s_w2, 16 * 6)
            pool.memset(ones_b[:], 1.0)
            pool.memset(val[:, :, :, :, HD:HD + 1], 1.0).then_inc(s_w2b, 1)

            def rotate(b, c):
                q = NCH * b + c
                pool.wait_ge(s_rope, q + 1)
                wait(pool, s_qkTp, q - 1)
                pool.tensor_tensor(rot[:, c % 2, 0:QKW], rope_c[:, c % 2], rope_s[:, c % 2], ALU.add)
                pool.tensor_tensor(rot[:, c % 2, QKW:QKW + HD], rope_c[:, c % 2, QKW - HD:QKW], rope_s[:, c % 2, QKW - HD:QKW],
                                   ALU.add).then_inc(s_rot, 1)

            def stream(b, j):
                n = bass.ds(2 * b + j, 1)
                pool.wait_ge(s_h2, 2 * b + j + 1)
                pool.tensor_tensor(H[:, n, :], H[:, n, :], M[:, n, 0:D], ALU.add).then_inc(s_hadd, 1)

            def norm3(b):
                n = bass.ds(2 * b, 2)
                wait_apart(pool, SM["ms"], b + 1)
                ch.link(pool.tensor_tensor(rr3[:, n], ms[:, n], rms_eps[0:T, :], ALU.add), apart=True)
                pool.tensor_tensor(rr3[:, n], rr3[:, n], neg_half[0:T, 0:2], ALU.pow).then_inc(SM["rr3"], 1)

            def dispatch(g, u, half):
                wait_apart(pool, SM["slot"], g + 1)
                for j in range(GR // 2 * half, GR // 2 * (half + 1)):
                    for p in range(2):
                        pool.indirect_dma_start(out=rows_d, out_offset=bass.IndirectOffsetOnAxis(ap=slot[:, u, p, j:j + 1], axis=0),
                                                in_=send[:, u, j, :],
                                                in_offset=None).then_inc(s_rows[u], 16)

            def batch(b, prev, nxt, group=None, gu=0, half=0):
                if prev is not None:
                    stream(prev, 0)
                rotate(b, 3)
                rotate(b, 4)
                rotate(b, 5)
                if group is not None:
                    dispatch(group, gu, half)
                if nxt is not None:
                    rotate(nxt, 0)
                if prev is not None:
                    stream(prev, 1)
                    norm3(prev)
                if nxt is not None:
                    rotate(nxt, 1)
                    rotate(nxt, 2)

            def pair(i, group=None, gu=0, first=False, last=False):
                batch(2 * i, None if first else 2 * i - 1, 2 * i + 1, group, gu, 0)
                batch(2 * i + 1, 2 * i, None if last else 2 * i + 2, group, gu, 1)

            for c in range(3):
                rotate(0, c)
            pair(0, first=True)
            pair(1)
            pair(2, 0, 0)
            ch.settle()
            with pool.Fori(1, NPAIR // 2 - 1) as i:
                ch.enter(i - 1, 4)
                pair(2 * i + 1, 2 * i - 1, 1)
                pair(2 * i + 2, 2 * i, 0)
            ch.leave(NPAIR // 2 - 2)
            pair(NPAIR - 1, NPAIR - 3, 1, last=True)
            stream(B - 1, 0)
            stream(B - 1, 1)
            norm3(B - 1)
            for g in (NPAIR - 2, NPAIR - 1):
                for half in range(2):
                    dispatch(g, g % 2, half)

            pool.wait_ge(SM["base"], 32)

            def add(k, u, slot):
                wait_apart(pool, s_y, k + 1)
                if not isinstance(k, int) or k:
                    wait_apart(pool, s_add, 16 * k)
                pool.indirect_dma_start(out=out.rearrange("b t d -> (b t) d"),
                                        out_offset=bass.IndirectOffsetOnAxis(ap=xg[:, slot, D:D + 1].bitcast(I32), axis=0),
                                        in_=ys[:, u, :], in_offset=None, bounds_check=B * KEEP - 1, oob_is_err=False,
                                        compute_op=ALU.add).then_inc(s_add, 16)

            for k in range(NX + 1):
                add(k, k % 2, k % NX)
            with pool.Fori(1, NMT // NX - 1) as i:
                for r in range(1, NX + 1):
                    add(NX * i + r, r % 2, r % NX)
            for k in range(NMT - NX + 1, NMT):
                add(k, k % 2, k % NX)
            pool.wait_ge(s_add, 16 * NMT)

        @block.scalar
        def _(act):
            for g in range(NG):
                act.wait_ge(s_centered, g + 1)
                if g >= 2:
                    act.wait_ge(s_reduced, g - 1)
                act.activation(Xsq[:, g % 2], Xc[:, g % 2], ACT.Square).then_inc(s_squared, 1)
            act.wait_ge(s_score_tp, 1)
            act.copy(score_t[:], TX1[0:NT0, 0:HALF]).then_inc(s_score_t, 1)

            def xT_copy(b, u):
                act.wait_ge(s_xTp1, b + 1)
                act.copy(xT1[:, u], TX1[0:C, 0:2 * S].rearrange("p (c t) -> p c t", c=2)).then_inc(s_xT1, 1)

            def q_copy(b, u, h):
                act.wait_ge(s_qp1, 2 * b + h + 1)
                act.copy(qT1[:, u, 2 * h:2 * h + 2, :], Q1[h][:, 0:2 * S].rearrange("p (m t) -> p m t", m=2)).then_inc(s_q1, 1)

            def r_copy(b, u, h):
                act.wait_ge(s_rp1, 2 * b + h + 1)
                if h == 0:
                    wait(act, s_o1, b)
                act.copy(rT1[:, u, 2 * h:2 * h + 2, :], R1[h][:, 0:2 * S].rearrange("p (m t) -> p m t", m=2)).then_inc(s_r1, 1)

            xT_copy(0, 0)
            for h in range(2):
                act.wait_ge(s_kvg, h + 1)
                act.copy(kT1[:, 2 * h:2 * h + 2, :], Q1[h][:, 0:2 * S].rearrange("p (m t) -> p m t", m=2)).then_inc(s_kv, 1)
            act.wait_ge(s_kvg, 3)
            act.activation(gate[:], O1[0:T, 0:2 * NH].rearrange("p (h e) -> p h e", h=2), ACT.Exp, scale=-1.0).then_inc(s_gate, 1)
            for h in range(2):
                q_copy(0, 0, h)

            def body(b, u, nxt):
                if nxt is not None:
                    xT_copy(nxt, 1 - u)
                r_copy(b, u, 0)
                if nxt is not None:
                    q_copy(nxt, 1 - u, 0)
                r_copy(b, u, 1)
                if nxt is not None:
                    q_copy(nxt, 1 - u, 1)

            body(0, 0, 1)
            with act.Fori(0, B // 2 - 1) as i:
                body(2 * i + 1, 1, 2 * i + 2)
                body(2 * i + 2, 0, 2 * i + 3)
            body(B - 1, 1, None)

            def xrT_copy(b, u):
                act.wait_ge(s_xTp2, b + 1)
                act.copy(xrT[:, u], MISC[0:C, 0:2 * S].rearrange("p (c t) -> p c t", c=2)).then_inc(s_xrT, 1)

            def val_copy(b, u, c):
                act.wait_ge(s_rope, NCH * b + c + 1)
                act.copy(val[:, u, c // NKV, c % NKV, 0:HD], proj[0:T, c % NKV, QKW:GW]).then_inc(s_val, 1)

            def qkT_copy(b, u, c):
                j, g = c // NKV, c % NKV
                act.wait_ge(s_qkTp, NCH * b + c + 1)
                act.copy(qkT[:, u, g, :, j * T:(j + 1) * T], proj[:, g, 0:3 * T].rearrange("p (k t) -> p k t", k=3)).then_inc(s_qkT, 1)

            def exponent(b, k):
                w = (3 * T, 2 * S)[UNITS2[k][0]]
                act.wait_ge(s_sx, NU2 * b + k + 1)
                wait(act, s_tp, NU2 * b + k - 1)
                act.activation(pr[:, k % 2, 0:w], sx[:, k % 2, 0:w], ACT.Exp, scale=HD ** -0.5).then_inc(s_pr, 1)

            def pT_copy(b, k):
                w = (3 * T, 2 * S)[UNITS2[k][0]]
                act.wait_ge(s_tp, NU2 * b + k + 1)
                wait(act, s_pv, NU2 * b + k - 1)
                act.copy(pT[:, k % 2, 0:w], PT2[0:T, 0:w]).then_inc(s_pT, 1)

            def oT_copy(b, j, h):
                act.wait_ge(s_oTp, 4 * b + 2 * j + h + 1)
                act.copy(oT[:, j, 3 * h:3 * h + 3, :], MISC[:, 0:3 * T].rearrange("p (m t) -> p m t", m=3)).then_inc(s_oT, 1)

            def mT_copy(b):
                act.wait_ge(SM["mTp"], b + 1)
                act.copy(mT[:], MISC[0:C, 0:2 * S].rearrange("p (c t) -> p c t", c=2)).then_inc(SM["mT"], 1)

            def put(b, u, gu, turn):
                act.wait_ge(SM["m"], b + 1)
                if u == 0:
                    wait(act, s_rows[gu], 16 * 2 * GR * turn)
                act.copy(send[:, gu, 2 * u:2 * u + 2, 0:D], mrow[:]).then_inc(SM["back"], 1)

            def weight_exp(g):
                act.wait_ge(SM["gap"], g + 1)
                act.activation(ex2[:], top2[:], ACT.Exp).then_inc(SM["ex"], 1)

            act.wait_ge(s_w2b, 1)
            xrT_copy(0, 0)
            for c in range(3):
                val_copy(0, 0, c)
                qkT_copy(0, 0, c)

            def batch(b, u, prev, prev2, nxt, group=None, g0=0, gu=0, turn=0, attend=True):
                for k in range(NU2):
                    if attend:
                        if k in (1, 3, 4):
                            val_copy(b, u, {1: 3, 3: 4, 4: 5}[k])
                        if k in (2, 4, 5):
                            qkT_copy(b, u, {2: 3, 4: 4, 5: 5}[k])
                    if nxt is not None:
                        if k in (5, 7, 8):
                            val_copy(nxt, 1 - u, {5: 0, 7: 1, 8: 2}[k])
                        if k in (6, 8, 9):
                            qkT_copy(nxt, 1 - u, {6: 0, 8: 1, 9: 2}[k])
                    if k == 0 and prev2 is not None:
                        put(prev2, u, gu, turn)
                        mT_copy(prev2)
                    if k == 1 and prev2 is not None:
                        logit_copy(prev2, u, g0)
                    if k == 2 and nxt is not None:
                        xrT_copy(nxt, 1 - u)
                    if k in (3, 4) and prev is not None:
                        oT_copy(prev, 1, k - 3)
                    if k in (7, 8) and attend:
                        oT_copy(b, 0, k - 7)
                    if k < 2:
                        if prev is not None:
                            pT_copy(prev, NU2 - 2 + k)
                    elif attend:
                        pT_copy(b, k - 2)
                    if k == 5 and group is not None:
                        weight_exp(group)
                    if attend:
                        exponent(b, k)

            def logit_copy(b, u, g):
                act.wait_ge(SM["logit"], b + 1)
                if u == 0:
                    wait(act, SM["sel"], g)
                act.copy(logit[:, 2 * u:2 * u + 2, :], MISC[0:T, 0:2 * E].rearrange("p (h e) -> p h e", h=2)).then_inc(SM["logit_in"], 1)

            def pair(i, gu=0, turn=0, first=False, last=False):
                batch(2 * i, 0, None if first else 2 * i - 1, None if first else 2 * i - 2, 2 * i + 1, None, i - 1, gu, turn)
                batch(2 * i + 1, 1, 2 * i, None if first else 2 * i - 1, None if last else 2 * i + 2, None if first else i - 1,
                      0, gu, turn)

            pair(0, first=True)
            pair(1, 0, 0)
            pair(2, 1, 0)
            with act.Fori(1, NPAIR // 2 - 1) as i:
                pair(2 * i + 1, 0, i)
                pair(2 * i + 2, 1, i)
            pair(NPAIR - 1, 0, NPAIR // 2 - 1, last=True)
            batch(B, 0, B - 1, B - 2, None, None, NPAIR - 1, 1, NPAIR // 2 - 1, attend=False)
            put(B - 1, 1, 1, NPAIR // 2 - 1)
            mT_copy(B - 1)
            logit_copy(B - 1, 1, NPAIR - 1)
            weight_exp(NPAIR - 1)

            def xgT_copy(k, u):
                act.wait_ge(s_xgTp, k + 1)
                act.copy(xgT[:, u], bank[0][0:C, 0:2 * MT].rearrange("p (c t) -> p c t", c=2)).then_inc(s_xgT, 1)

            def silu(k, u):
                act.wait_ge(s_up, k + 1)
                act.activation(sg[:, u], GATE[u][:, 0:FF], ACT.Silu).then_inc(s_sg, 1)

            def hT_copy(k, u):
                act.wait_ge(s_hTp, k + 1)
                act.copy(hT[:, u], bank[1][:, 0:FF].rearrange("p (m t) -> p m t", m=3)).then_inc(s_hT, 1)

            def tile(k, u, last=False):
                if not last:
                    xgT_copy(k + 1, 1 - u)
                hT_copy(k, u)
                if not last:
                    silu(k + 1, 1 - u)

            xgT_copy(0, 0)
            silu(0, 0)
            for k in range(NX + 1):
                tile(k, k % 2)
            with act.Fori(1, NMT // NX - 1) as i:
                for r in range(1, NX + 1):
                    tile(NX * i + r, r % 2)
            for k in range(NMT - NX + 1, NMT):
                tile(k, k % 2, k == NMT - 1)

        @block.vector
        def _(dve):
            ch = Chain(dve, s_dve)
            dve.wait_ge(s_tok_vec, 64)
            dve.tensor_tensor(gw[:], gamma[:], tokw[:], ALU.mult)
            ch.link(dve.tensor_tensor(bw[:], beta[:], tokw[:], ALU.mult))
            ch.link(dve.tensor_reduce(bsum[:], bw[:], AX, ALU.add))
            ch.link(dve.tensor_tensor(bsum[:], bsum[:], tokb[:], ALU.add))

            def reduce_group(g):
                lo, hi = GT * g, GT * (g + 1)
                dve.wait_ge(s_squared, g + 1)
                dve.tensor_reduce(var[:, lo:hi], Xsq[:, g % 2], AX, ALU.add)
                dve.wait_ge(s_weighted, g + 1)
                ch.link(dve.tensor_reduce(dot[:, lo:hi], Xgw[:, g % 2], AX, ALU.add))
                dve.sem_inc(s_reduced, 1)

            for g in range(NG):
                lo, hi = GT * g, GT * (g + 1)
                dve.wait_ge(s_tok_in[g], 16)
                ch.link(dve.tensor_reduce(mu[:, lo:hi], X[:, lo:hi, :], AX, ALU.add))
                ch.link(dve.tensor_scalar(mu[:, lo:hi], mu[:, lo:hi], 1.0 / D, None, ALU.mult))
                dve.tensor_tensor(Xc[:, g % 2], X[:, lo:hi, :], mu[:, lo:hi].unsqueeze(2).broadcast_to([HALF, GT, D]),
                                  ALU.subtract).then_inc(s_centered, 1)
                if g:
                    reduce_group(g - 1)
            reduce_group(NG - 1)
            dve.tensor_scalar(var[:], var[:], 1.0 / D, LN_EPS, ALU.mult, ALU.add).then_inc(s_stats, 1)
            dve.wait_ge(s_rs0, 1)
            ch.link(dve.tensor_tensor(mu[:], rs0[:], rs0[:], ALU.mult))
            ch.link(dve.tensor_tensor(mu[:], mu[:], var[:], ALU.mult))
            ch.link(dve.tensor_scalar(mu[:], mu[:], -0.5, 1.5, ALU.mult, ALU.add))
            ch.link(dve.tensor_tensor(rs0[:], rs0[:], mu[:], ALU.mult))
            ch.link(dve.tensor_tensor(dot[:], dot[:], rs0[:], ALU.mult))
            dve.tensor_scalar(score[:], dot[:], bsum[0:HALF, :], None, ALU.add).then_inc(s_score, 1)
            dve.wait_ge(s_score_in, 16)
            dve.wait_ge(s_const, 48)
            ch.settle()
            with dve.Fori(0, NG) as g:
                ch.enter(g, 2)
                for k in range(GT):
                    row = all_scores[:, bass.ds(g * (GT * HALF) + N0 * (k // 2), N0)]
                    own = score[:, bass.ds(g * GT + k, 1)]
                    dve.tensor_scalar(junk_a[:, k], row, own, None, ALU.is_gt, ALU.add, accum_out=above[:, bass.ds(g * GT + k, 1)])
                    ins = dve.scalar_tensor_tensor(junk_b[:, k], row, own, earlier[:, k % 2, :], ALU.is_equal, ALU.mult,
                                                   accum_out=tied[:, bass.ds(g * GT + k, 1)])
                ch.link(ins)
                grp = bass.ds(g * GT, GT)
                ch.link(dve.tensor_tensor(above[:, grp], above[:, grp], tied[:, grp], ALU.add))
                dve.tensor_tensor(rank[:, grp], above[:, grp], rowbase[0:HALF, grp], ALU.add).then_inc(s_rank, 1)
            ch.leave(NG)

            def norm_rows(b, u):
                for h in range(2):
                    ins = dve.bn_stats(st1[:, h, :], H[:, bass.ds(2 * b + h, 1), :])
                ch.link(ins, apart=True)
                for h in range(2):
                    ins = dve.bn_aggr(mv1[:, u, h, :], st1[:, h, :])
                ins.then_inc(s_mv1, 1)

            def normalise(b, u):
                dve.wait_ge(s_rs1, b + 1)
                for h in range(2):
                    ins = dve.tensor_scalar(xn1[:, u, h, :], H[:, bass.ds(2 * b + h, 1), :], mv1[:, u, h, 0:1], rs1[:, u, h:h + 1],
                                            ALU.subtract, ALU.mult)
                ins.then_inc(s_xn1, 1)

            def decayed(b, u, k):
                tile, heads = UNITS1[k]
                dve.wait_ge(s_sc1, NU1 * b + k + 1)
                src = SC1[k % 2][0:T, 0:2 * S]
                if tile == 1:
                    o = p1[:, u].rearrange("p (m e) t -> p m e t", e=2)[:, :, heads[0] % 2, :]
                    dve.tensor_tensor(o, src.rearrange("p (m t) -> p m t", m=4), decay[:, 0:T].unsqueeze(1).broadcast_to([T, 4, T]),
                                      ALU.mult).then_inc(s_p1, 1)
                else:
                    o = p0[:, u].rearrange("p (m e) t -> p m e t", e=2)[:, heads[0] // 2:heads[0] // 2 + 2, heads[0] % 2, :]
                    dve.tensor_tensor(o, src.rearrange("p (m t) -> p m t", m=2), decay[:].unsqueeze(1).broadcast_to([T, 2, S]),
                                      ALU.mult).then_inc(s_p1, 1)

            def close1(b, u):
                dve.wait_ge(s_o1, b + 1)
                dve.wait_ge(s_hx1, b + 1)
                dve.tensor_tensor(H[:, bass.ds(2 * b, 2), :], O1[0:T, 0:2 * D].rearrange("p (h d) -> p h d", h=2), hx1[:, u],
                                  ALU.add).then_inc(s_h1, 1)

            dve.wait_ge(s_w1, 16 * 6)
            dve.wait_ge(s_h0[0], 32)
            norm_rows(0, 0)
            normalise(0, 0)
            dve.wait_ge(s_gate, 1)
            ch.link(dve.tensor_scalar(gate[:], gate[:], 1.0, None, ALU.add))
            ch.link(dve.reciprocal(gate[:], gate[:]))
            for h in range(2):
                ins = dve.tensor_tensor(vg[:, h], SC1[h][0:T, :].rearrange("p (e d) -> p e d", e=NH),
                                        gate[:, h, :].unsqueeze(2).broadcast_to([T, NH, DK]), ALU.mult)
            ins.then_inc(s_kv, 1)
            for g in range(1, NG):
                dve.wait_ge(s_h0[g], 32)
            ch.settle()

            def stats2(b, u):
                wait_apart(dve, s_h1, b + 1)
                for h in range(2):
                    ins = dve.bn_stats(st2[:, h, :], H[:, bass.ds(2 * b + h, 1), :])
                ch.link(ins, apart=True)
                for h in range(2):
                    ins = dve.bn_aggr(mv2[:, u, h, :], st2[:, h, :])
                ins.then_inc(s_mv2, 1)

            def rows2(b, u):
                dve.wait_ge(s_rs2, b + 1)
                for h in range(2):
                    ins = dve.tensor_scalar(M[:, bass.ds(2 * b + h, 1), 0:D], H[:, bass.ds(2 * b + h, 1), :], mv2[:, u, h, 0:1],
                                            rs2[:, u, h:h + 1], ALU.subtract, ALU.mult)
                ins.then_inc(s_x3, 1)

            def body(b, u, prev, prev2, nxt):
                if nxt is not None:
                    norm_rows(nxt, 1 - u)
                decayed(b, u, 0)
                decayed(b, u, 1)
                if prev is not None:
                    close1(prev, 1 - u)
                if nxt is not None:
                    normalise(nxt, 1 - u)
                decayed(b, u, 2)
                decayed(b, u, 3)
                if prev is not None:
                    stats2(prev, 1 - u)
                decayed(b, u, 4)
                if prev2 is not None:
                    rows2(prev2, u)
                decayed(b, u, 5)

            body(0, 0, None, None, 1)
            body(1, 1, 0, None, 2)
            ch.settle()
            with dve.Fori(1, B // 2 - 1) as i:
                ch.enter(i - 1, 4)
                body(2 * i, 0, 2 * i - 1, 2 * i - 2, 2 * i + 1)
                body(2 * i + 1, 1, 2 * i, 2 * i - 1, 2 * i + 2)
            ch.leave(B // 2 - 2)
            body(B - 2, 0, B - 3, B - 4, B - 1)
            body(B - 1, 1, B - 2, B - 3, None)
            close1(B - 1, 1)
            stats2(B - 1, 1)
            rows2(B - 2, 0)
            rows2(B - 1, 1)
            ch.settle()

            dve.wait_ge(s_w2, 16 * 6)
            dve.wait_ge(s_h1, B)
            dve.tensor_copy(causal_b[:], causal[:])
            dve.tensor_copy(ident_b[:], ident[0:T, 0:T]).then_inc(s_w2b, 1)
            dve.wait_ge(SM["c3"], 16 * 8)
            dve.tensor_copy(run[:], region[:])
            dve.tensor_copy(before_b[:], before[:]).then_inc(SM["bf"], 1)

            def rms_rows(b):
                dve.wait_ge(s_x3, b + 1)
                wait(dve, s_xTp2, b)
                for h in range(2):
                    n = bass.ds(2 * b + h, 1)
                    ins = dve.scalar_tensor_tensor(xr[:, h, :], M[:, n, 0:D], rr2[:, n], norm1w[:], ALU.mult, ALU.mult)
                ins.then_inc(s_xr, 1)

            def rope(b, c):
                j, g = c // NKV, c % NKV
                dve.wait_ge(s_proj, NCH * b + c + 1)
                wait(dve, s_rot, NCH * b + c - 1)
                hw = HD // 2
                n = QKW // HD
                src = proj[0:T, g, 0:QKW].rearrange("p (n d) -> p n d", d=HD)
                tab = lambda t, lo, hi: t[:, j, lo:hi].unsqueeze(1).broadcast_to([T, n, hi - lo])
                dst = lambda t: t[:, c % 2].rearrange("p (n d) -> p n d", d=HD)
                dve.tensor_tensor(dst(rope_c), src, tab(cos, 0, HD), ALU.mult)
                dve.tensor_tensor(dst(rope_s)[:, :, 0:hw], src[:, :, hw:HD], tab(sin, 0, hw), ALU.mult)
                dve.tensor_tensor(dst(rope_s)[:, :, hw:HD], src[:, :, 0:hw], tab(sin, hw, HD), ALU.mult).then_inc(s_rope, 1)

            def centre(b, k):
                tile, heads = UNITS2[k]
                nh, w = len(heads), (T, S)[tile]
                dve.wait_ge(s_sc2, NU2 * b + k + 1)
                src = SC2[k % 2][0:T, 0:nh * w].rearrange("p (n t) -> p n t", n=nh)
                ch.link(dve.tensor_reduce(mx[:, k % 2, 0:nh], src, AX, ALU.max))
                wait(dve, s_pr, NU2 * b + k - 1)
                dve.tensor_tensor(sx[:, k % 2, 0:nh * w].rearrange("p (n t) -> p n t", n=nh), src,
                                  mx[:, k % 2, 0:nh].unsqueeze(2).broadcast_to([T, nh, w]), ALU.subtract).then_inc(s_sx, 1)

            def divide(b, q):
                dve.wait_ge(s_pv, NU2 * b + (2, 4, 7, 10)[q])
                o = O2[0:T, 0:6 * (HD + 1)].rearrange("p (n d) -> p n d", n=6)
                ch.link(dve.reciprocal(rden[:, q % 2, :], o[:, :, HD]))
                dst = oh[:, q // 2].rearrange("p (m e d) -> p m e d", m=6, e=2)[:, :, q % 2, :]
                dve.tensor_tensor(dst, o[:, :, 0:HD], rden[:, q % 2, :].unsqueeze(2).broadcast_to([T, 6, HD]), ALU.mult).then_inc(s_on, 1)

            def close2(b, j):
                n = bass.ds(2 * b + j, 1)
                dve.wait_ge(s_wo, 2 * b + j + 1)
                ch.link(dve.tensor_tensor(M[:, n, 0:D], MISC[0:T, 0:D], M[:, n, 0:D], ALU.add))
                dve.sem_inc(s_h2, 1)
                ch.link(dve.scalar_tensor_tensor(sqj[:, j, :], M[:, n, 0:D], 1.0 / D, M[:, n, 0:D], ALU.mult, ALU.mult, accum_out=ms[:, n]))
                if j:
                    dve.sem_inc(SM["ms"], 1)

            def rows3(b):
                wait_apart(dve, SM["rr3"], b + 1)
                wait_apart(dve, s_hadd, 2 * b + 2)
                wait(dve, SM["back"], b)
                wait(dve, SM["mTp"], b)
                for j in range(2):
                    n = bass.ds(2 * b + j, 1)
                    ins = dve.scalar_tensor_tensor(mrow[:, j, :], M[:, n, 0:D], rr3[:, n], norm2w[:], ALU.mult, ALU.mult)
                ins.then_inc(SM["m"], 1)

            EW = [T, GR, E]
            wide = lambda t: t[:].unsqueeze(2).broadcast_to(EW)
            ranks = erank[0:T, :].unsqueeze(1).broadcast_to(EW)

            def choose(src, top, c_, one):
                ch.link(dve.tensor_reduce(top[:], src, AX, ALU.max))
                ch.link(dve.tensor_tensor(hit[:], src, wide(top), ALU.is_equal))
                ch.link(dve.tensor_tensor(hit[:], hit[:], ranks, ALU.mult))
                ch.link(dve.tensor_reduce(c_[:], hit[:], AX, ALU.max))
                ch.link(dve.tensor_tensor(one[:], ranks, wide(c_), ALU.is_equal))

            def router(g, gu, part):
                rows = lambda col: send[:, gu, :, col:col + 1]
                if part == 0:
                    dve.wait_ge(SM["logit_in"], 2 * g + 2)
                    choose(logit[:], top1, cm, sel1)
                if part == 1:
                    ch.link(dve.scalar_tensor_tensor(pick[:], sel1[:], MASKED, logit[:], ALU.mult, ALU.add))
                    dve.sem_inc(SM["sel"], 1)
                    choose(pick[:], top2, cm2, sel2)
                if part == 2:
                    dve.tensor_tensor(sel_b[:], sel1[:], sel2[:], ALU.add).then_inc(SM["sel_b"], 1)
                    dve.tensor_tensor(top2[:], top2[:], top1[:], ALU.subtract).then_inc(SM["gap"], 1)
                if part == 3:
                    dve.wait_ge(SM["ex"], g + 1)
                    ch.link(dve.tensor_scalar(w1[:], ex2[:], 1.0, None, ALU.add))
                    ch.link(dve.reciprocal(w1[:], w1[:]))
                    ch.link(dve.tensor_tensor(w2[:], ex2[:], w1[:], ALU.mult))
                    dve.tensor_tensor(rows(D + 2), w1[:].unsqueeze(2), w2[:].unsqueeze(2), ALU.subtract)
                    dve.tensor_copy(rows(D + 3), w2[:].unsqueeze(2))
                    dve.tensor_copy(rows(D + 1), cm[:].unsqueeze(2))
                    dve.tensor_copy(rows(D), outrow[:, bass.ds(GR * g, GR)].unsqueeze(2))
                if part == 4:
                    dve.wait_ge(SM["cum"], g + 1)
                    ch.link(dve.tensor_tensor(pos[:], MISC[0:T, 0:GR * E].rearrange("p (n e) -> p n e", e=E),
                                              run[0:T, :].unsqueeze(1).broadcast_to(EW), ALU.add))
                    ch.link(dve.tensor_tensor(run[:], MISC[:, GR * E:(GR + 1) * E], run[:], ALU.add))
                    dve.sem_inc(SM["cum_read"], 1)
                    ch.link(dve.tensor_tensor(sel1[:], sel1[:], pos[:], ALU.mult))
                    ch.link(dve.tensor_tensor(sel2[:], sel2[:], pos[:], ALU.mult))
                if part == 5:
                    ch.link(dve.tensor_reduce(slot_f[:, 0], sel1[:], AX, ALU.add))
                    ch.link(dve.tensor_reduce(slot_f[:, 1], sel2[:], AX, ALU.add))
                    dve.tensor_copy(slot[:, gu], slot_f[:]).then_inc(SM["slot"], 1)

            rms_rows(0)
            for c in range(3):
                rope(0, c)

            def batch(b, u, prev, nxt, group=None, gu=0):
                if prev is not None:
                    close2(prev, 0)
                for k in range(NU2):
                    if k == 3 and prev is not None:
                        divide(prev, 3)
                    if k == 5:
                        divide(b, 0)
                    if k == 7:
                        divide(b, 1)
                    centre(b, k)
                    if k in (0, 2, 3):
                        rope(b, {0: 3, 2: 4, 3: 5}[k])
                    if k in (4, 6, 7) and nxt is not None:
                        rope(nxt, {4: 0, 6: 1, 7: 2}[k])
                    if k == 1 and nxt is not None:
                        rms_rows(nxt)
                    if k == 5 and prev is not None:
                        close2(prev, 1)
                    if k == 8 and prev is not None:
                        rows3(prev)
                    if group is not None and k in (2, 3, 4, 6, 7, 8):
                        router(group, gu, {2: 0, 3: 1, 4: 2, 6: 4, 7: 3, 8: 5}[k])
                divide(b, 2)

            def pair(i, gu=0, first=False, last=False):
                batch(2 * i, 0, None if first else 2 * i - 1, 2 * i + 1)
                batch(2 * i + 1, 1, 2 * i, None if last else 2 * i + 2, None if first else i - 1, gu)

            pair(0, first=True)
            pair(1, 0)
            pair(2, 1)
            ch.settle()
            with dve.Fori(1, NPAIR // 2 - 1) as i:
                ch.enter(i - 1, 4 * (NU2 + 8) + 2 * 20)
                pair(2 * i + 1, 0)
                pair(2 * i + 2, 1)
            ch.leave(NPAIR // 2 - 2)
            pair(NPAIR - 1, 0, last=True)
            close2(B - 1, 0)
            divide(B - 1, 3)
            close2(B - 1, 1)
            rows3(B - 1)
            for part in (0, 1, 2, 4, 3, 5):
                router(NPAIR - 1, 1, part)

            ch.link(dve.tensor_copy(cnt_i[:], run[:]))
            dve.sem_inc(SM["count"], 1)
            ch.link(dve.tensor_tensor(til[:], run[:], region[:], ALU.subtract))
            ch.link(dve.tensor_scalar(til_i[:], til[:], float(MT - 1), None, ALU.add))
            ch.link(dve.tensor_scalar(til_i[:], til_i[:], MT.bit_length() - 1, None, ALU.arith_shift_right))
            ch.link(dve.tensor_copy(til[:], til_i[:]))
            ends, spare, step = til, end_a, 1
            while step < E:
                dve.tensor_copy(spare[:, 0:step], ends[:, 0:step])
                ch.link(dve.tensor_tensor(spare[:, step:E], ends[:, step:E], ends[:, 0:E - step], ALU.add))
                ends, spare, step = spare, (end_b if spare is end_a else end_a), 2 * step
            TW = [MT, NMT, E]
            ch.link(dve.tensor_tensor(past[:], tileno[:].unsqueeze(2).broadcast_to(TW), ends[:].unsqueeze(1).broadcast_to(TW), ALU.is_ge))
            ch.link(dve.tensor_reduce(texp_f[:], past[:], AX, ALU.add))
            dve.tensor_scalar(rexp[:], texp_f[:], -1.0, float(E), ALU.mult, ALU.add)
            dve.tensor_scalar(texp[:], texp_f[0:1, :], float(E - 1), None, ALU.min)
            ch.link(dve.tensor_scalar(skip[:], til[:], -float(MT), float(CAP), ALU.mult, ALU.add))
            ch.link(dve.tensor_tensor(jump[:], past[:], skip[:].unsqueeze(1).broadcast_to(TW), ALU.mult))
            ch.link(dve.tensor_reduce(tstart_f[:], jump[:], AX, ALU.add))
            ch.link(dve.scalar_tensor_tensor(tstart_f[:], tileno[:], float(MT), tstart_f[:], ALU.mult, ALU.add))
            dve.tensor_scalar(tstart[:], tstart_f[0:1, :], float(E * CAP), None, ALU.min).then_inc(SM["texp"], 1)


            def hidden(k, u):
                dve.wait_ge(s_sg, k + 1)
                dve.tensor_tensor(hb[:, u], UP[u][:, 0:FF], sg[:, u], ALU.mult).then_inc(s_h, 1)

            def result(k, u, slot):
                row = xg[:, slot]
                ch.link(dve.tensor_scalar(wv_[:, u, 0:1], row[:, D + 1:D + 2], rexp[:, bass.ds(k, 1)], row[:, D + 2:D + 3],
                                          ALU.is_equal, ALU.mult))
                ch.link(dve.tensor_tensor(wv_[:, u, 1:2], wv_[:, u, 0:1], row[:, D + 3:D + 4], ALU.add))
                wait(dve, s_add, 16 * (k - 1))
                dve.wait_ge(s_dn, k + 1)
                dve.tensor_scalar(ys[:, u], bank[2][:, 0:D], wv_[:, u, 1:2], None, ALU.mult).then_inc(s_y, 1)

            def tile(k, u, slot, last=False):
                result(k, u, slot)
                if not last:
                    hidden(k + 1, 1 - u)

            hidden(0, 0)
            for k in range(NX + 1):
                tile(k, k % 2, k % NX)
            ch.settle()
            with dve.Fori(1, NMT // NX - 1) as i:
                ch.enter(i - 1, 2 * NX)
                for r in range(1, NX + 1):
                    tile(NX * i + r, r % 2, r % NX)
            ch.leave(NMT // NX - 2)
            for k in range(NMT - NX + 1, NMT):
                tile(k, k % 2, k % NX, k == NMT - 1)

        @block.tensor
        def _(pe):
            pe.wait_ge(s_const, 48)
            pe.wait_ge(s_score, 1)
            pe.transpose(TX1[0:NT0, 0:HALF], score[:], ident[0:HALF, 0:HALF]).then_inc(s_score_tp, 1)
            pe.wait_ge(s_w1, 16 * 6)

            def transpose_x(b, u):
                pe.wait_ge(s_xn1, b + 1)
                wait(pe, s_xT1, b)
                for c in range(2):
                    for h in range(2):
                        ins = pe.transpose(TX1[0:C, c * S + h * T:c * S + h * T + T], xn1[:, u, h, c * C:(c + 1) * C], ident[0:T, 0:T])
                ins.then_inc(s_xTp1, 1)

            def project(w, x, dst, m0):
                for m in range(2):
                    for c in range(2):
                        ins = pe.matmul(dst[:, m * S:(m + 1) * S], w[:, c, 128 * (m0 + m):128 * (m0 + m + 1)], x[:, c, :],
                                        start=c == 0, stop=c == 1)
                return ins

            def queries(b, u, h):
                pe.wait_ge(s_xT1, b + 1)
                wait(pe, s_q1, 2 * b + h - 1 if isinstance(b, int) else 2 * (b - 1) + h + 1)
                if isinstance(b, int) and b == 0:
                    pe.wait_ge(s_kv, h + 1)
                project(wq, xT1[:, u], Q1[h], 2 * h).then_inc(s_qp1, 1)

            def scores(b, u, k):
                tile, heads = UNITS1[k]
                if k % 2 == 0 or True:
                    pe.wait_ge(s_q1, 2 * b + (2 if k < 2 or k >= 4 else 1))
                if isinstance(b, int) and b == 0 and k < 2:
                    pe.wait_ge(s_kv, 3)
                else:
                    pe.wait_ge(s_p1, NU1 * b + k - 1)
                w = S if tile == 0 else T
                for n, hd in enumerate(heads):
                    base = 64 * (hd % 2)
                    ins = pe.matmul(SC1[k % 2][0:T, n * w:(n + 1) * w], kT1[base:base + DK, hd // 2, tile * T:tile * T + T],
                                    qT1[base:base + DK, u, hd // 2, S - w:S], start=True, stop=True)
                ins.then_inc(s_sc1, 1)

            def retrieve(b, u, h):
                pe.wait_ge(s_p1, NU1 * b + (4 if h == 0 else 6))
                wait(pe, s_r1, 2 * b + h - 1 if isinstance(b, int) else 2 * (b - 1) + h + 1)
                for m in range(2):
                    for e in range(2):
                        hd = 4 * h + 2 * m + e
                        o = R1[h][64 * e:64 * e + DK, m * S:(m + 1) * S]
                        pe.matmul(o, vg[:, 0, hd, :], p0[:, u, hd, :], start=True, stop=False, skip_group_check=True)
                        ins = pe.matmul(o[:, T:S], vg[:, 1, hd, :], p1[:, u, hd, :], start=False, stop=True, skip_group_check=True)
                ins.then_inc(s_rp1, 1)

            def output(b, u):
                pe.wait_ge(s_r1, 2 * b + 2)
                wait(pe, s_h1, b)
                for h in range(2):
                    for m in range(4):
                        ins = pe.matmul(O1[0:T, h * D:(h + 1) * D], rT1[:, u, m, h * T:(h + 1) * T], wo[:, m, :],
                                        start=m == 0, stop=m == 3)
                ins.then_inc(s_o1, 1)

            transpose_x(0, 0)
            pe.wait_ge(s_xT1, 1)
            for h in range(2):
                project(wk, xT1[:, 0], Q1[h], 2 * h).then_inc(s_kvg, 1)
            for h in range(2):
                for c in range(2):
                    pe.matmul(SC1[h][0:T, :], xT1[:, 0, c, h * T:(h + 1) * T], wv[:, c, :], start=c == 0, stop=c == 1)
            for h in range(2):
                for c in range(2):
                    ins = pe.matmul(O1[0:T, h * NH:(h + 1) * NH], xT1[:, 0, c, h * T:(h + 1) * T], wg[:, c, :], start=c == 0, stop=c == 1)
            ins.then_inc(s_kvg, 1)
            for h in range(2):
                queries(0, 0, h)

            def body(b, u, nxt):
                for k in range(4):
                    scores(b, u, k)
                if nxt is not None:
                    transpose_x(nxt, 1 - u)
                scores(b, u, 4)
                scores(b, u, 5)
                retrieve(b, u, 0)
                if nxt is not None:
                    queries(nxt, 1 - u, 0)
                retrieve(b, u, 1)
                if nxt is not None:
                    queries(nxt, 1 - u, 1)
                output(b, u)

            body(0, 0, 1)
            with pe.Fori(0, B // 2 - 1) as i:
                body(2 * i + 1, 1, 2 * i + 2)
                body(2 * i + 2, 0, 2 * i + 3)
            body(B - 1, 1, None)

            pe.wait_ge(s_h1, B)
            pe.wait_ge(s_w2, 16 * 6)
            pe.wait_ge(s_w2b, 2)

            def transpose_xr(b):
                pe.wait_ge(s_xr, b + 1)
                if not isinstance(b, int) or b >= 3:
                    pe.wait_ge(SM["logit_in"], b - 2)
                elif b == 2:
                    pe.wait_ge(s_h2, 1)
                for c in range(2):
                    for h in range(2):
                        ins = pe.transpose(MISC[0:C, c * S + h * T:c * S + h * T + T], xr[:, h, c * C:(c + 1) * C], ident[0:T, 0:T])
                ins.then_inc(s_xTp2, 1)

            def project2(b, u, c):
                j, g = c // NKV, c % NKV
                pe.wait_ge(s_xrT, b + 1)
                wait(pe, s_qkT, NCH * b + c - 2)
                for k in range(2):
                    ins = pe.matmul(proj[0:T, g, 0:GW], xrT[:, u, k, j * T:(j + 1) * T], wqkv[:, k, g, :], start=k == 0, stop=k == 1)
                ins.then_inc(s_proj, 1)

            def transpose_qk(b, c):
                pe.wait_ge(s_rot, NCH * b + c + 1)
                pe.wait_ge(s_val, NCH * b + c + 1)
                for k in range(3):
                    ins = pe.transpose(proj[:, c % NKV, k * T:(k + 1) * T], rot[:, c % 2, 128 * k:128 * (k + 1)], ident[0:T, 0:T])
                ins.then_inc(s_qkTp, 1)

            def scores2(b, u, k):
                tile, heads = UNITS2[k]
                nh, w = len(heads), (T, S)[tile]
                pe.wait_ge(s_qkT, NCH * b + NKV * tile + heads[-1] // 4 + 1)
                wait(pe, s_sx, NU2 * b + k - 1)
                dst = SC2[k % 2][0:T, 0:nh * w].rearrange("p (n t) -> p n t", n=nh)
                pe.matmul(dst[:, :, w - T:w], ident_b[:], causal_b[:].unsqueeze(1).broadcast_to([T, nh, T]),
                          start=True, stop=False, skip_group_check=True)
                for n, hd in enumerate(heads):
                    base, g, m = HD * (hd % 2), hd // 4, (hd % 4) // 2
                    ins = pe.matmul(dst[:, n, :], qkT[base:base + HD, u, g, m, tile * T:tile * T + T], qkT[base:base + HD, u, g, 2, 0:w],
                                    start=False, stop=n == nh - 1, skip_group_check=True)
                ins.then_inc(s_sc2, 1)

            def transpose_p(b, k):
                tile, heads = UNITS2[k]
                pe.wait_ge(s_pr, NU2 * b + k + 1)
                wait(pe, s_pT, NU2 * b + k)
                for n in range(len(heads) * (tile + 1)):
                    ins = pe.transpose(PT2[0:T, n * T:(n + 1) * T], pr[:, k % 2, n * T:(n + 1) * T], ident[0:T, 0:T])
                ins.then_inc(s_tp, 1)

            def weigh(b, u, k):
                tile, heads = UNITS2[k]
                pe.wait_ge(s_pT, NU2 * b + k + 1)
                half = {0: 0, 2: 1, 4: 2, 7: 3}.get(k)
                if half is not None:
                    wait(pe, s_on, 4 * b + half)
                for n, hd in enumerate(heads):
                    o = O2[0:T, (hd // 2) * (HD + 1):(hd // 2 + 1) * (HD + 1)]
                    for blk in range(tile + 1):
                        q = n * (tile + 1) + blk
                        ins = pe.matmul(o, pT[:, k % 2, q * T:(q + 1) * T], val[:, u, blk, hd // 4, :], start=blk == 0, stop=blk == tile)
                ins.then_inc(s_pv, 1)

            def transpose_o(b, j, h, group=None):
                pe.wait_ge(s_on, 4 * b + 2 * j + 2)
                if h == 1:
                    pe.wait_ge(s_oT, 4 * b + 2 * j + 1)
                elif group is not None:
                    pe.wait_ge(SM["cum_read"], group + 1)
                elif j == 0:
                    if not isinstance(b, int) or b:
                        pe.wait_ge(s_h2, 2 * b)
                    else:
                        pe.wait_ge(s_xrT, 2)
                elif isinstance(b, int) and b >= B - 2:
                    pe.wait_ge(SM["logit_in"], b)
                else:
                    pe.wait_ge(s_xrT, b + 3)
                for m in range(3):
                    ins = pe.transpose(MISC[:, m * T:(m + 1) * T], oh[:, j, 128 * (3 * h + m):128 * (3 * h + m + 1)], ident[0:T, 0:T])
                ins.then_inc(s_oTp, 1)

            def output2(b, j):
                pe.wait_ge(s_oT, 4 * b + 2 * j + 2)
                for m in range(6):
                    ins = pe.matmul(MISC[0:T, 0:D], oT[:, j, m, :], wout[:, m, :], start=m == 0, stop=m == 5)
                ins.then_inc(s_wo, 1)

            def transpose_m(b):
                pe.wait_ge(SM["m"], b + 1)
                pe.wait_ge(s_h2, 2 * b + 3 if not isinstance(b, int) or b < B - 1 else 2 * B)
                wait(pe, SM["mT"], b)
                for c in range(2):
                    for h in range(2):
                        ins = pe.transpose(MISC[0:C, c * S + h * T:c * S + h * T + T], mrow[:, h, c * C:(c + 1) * C], ident[0:T, 0:T])
                ins.then_inc(SM["mTp"], 1)

            def route(b):
                pe.wait_ge(SM["mT"], b + 1)
                for h in range(2):
                    for c in range(2):
                        ins = pe.matmul(MISC[0:T, h * E:(h + 1) * E], mT[:, c, h * T:(h + 1) * T], wr[:, c, :], start=c == 0, stop=c == 1)
                ins.then_inc(SM["logit"], 1)

            def count(g):
                pe.wait_ge(SM["sel_b"], g + 1)
                pe.wait_ge(s_h2, 4 * g + 6 if not isinstance(g, int) or g < NPAIR - 1 else 2 * B)
                cum, tot, flat_sel = MISC[0:T, 0:GR * E], MISC[:, GR * E:(GR + 1) * E], sel_b[:].rearrange("p n e -> p (n e)")
                pe.matmul(cum, before_b[:], flat_sel, start=True, stop=False, skip_group_check=True)
                for j in range(1, GR):
                    pe.matmul(cum[:, j * E:GR * E], ones_b[:, 0:T], flat_sel[:, 0:(GR - j) * E], start=False, stop=j == GR - 1,
                              skip_group_check=True)
                for j in range(GR):
                    ins = pe.matmul(tot, ones_b[:], flat_sel[:, j * E:(j + 1) * E], start=j == 0, stop=j == GR - 1, skip_group_check=True)
                ins.then_inc(SM["cum"], 1)

            def batch(b, u, prev, prev2, nxt, group=None):
                for k in range(NU2):
                    scores2(b, u, k)
                    if k in (2, 4, 5):
                        transpose_qk(b, {2: 3, 4: 4, 5: 5}[k])
                    if k in (6, 8, 9) and nxt is not None:
                        transpose_qk(nxt, {6: 0, 8: 1, 9: 2}[k])
                    if k in (0, 2, 3):
                        project2(b, u, {0: 3, 2: 4, 3: 5}[k])
                    if k in (4, 6, 7) and nxt is not None:
                        project2(nxt, 1 - u, {4: 0, 6: 1, 7: 2}[k])
                    if k == 0 and prev2 is not None:
                        transpose_m(prev2)
                    if k == 1 and prev2 is not None:
                        route(prev2)
                    if k == 2 and nxt is not None:
                        transpose_xr(nxt)
                    if k in (3, 4) and prev is not None:
                        transpose_o(prev, 1, k - 3)
                    if k == 5 and prev is not None:
                        output2(prev, 1)
                    if k == 6 and group is not None:
                        count(group)
                    if k in (7, 8):
                        transpose_o(b, 0, k - 7, group)
                    if k == 9:
                        output2(b, 0)
                    if k < 2:
                        if prev is not None:
                            transpose_p(prev, NU2 - 2 + k)
                    else:
                        transpose_p(b, k - 2)
                    if k < 3:
                        if prev is not None:
                            weigh(prev, 1 - u, NU2 - 3 + k)
                    else:
                        weigh(b, u, k - 3)

            def pair(i, first=False, last=False):
                batch(2 * i, 0, None if first else 2 * i - 1, None if first else 2 * i - 2, 2 * i + 1)
                batch(2 * i + 1, 1, 2 * i, None if first else 2 * i - 1, None if last else 2 * i + 2, None if first else i - 1)

            pe.wait_ge(SM["bf"], 1)
            transpose_xr(0)
            for c in range(3):
                project2(0, 0, c)
                transpose_qk(0, c)
            pair(0, first=True)
            pair(1)
            with pe.Fori(2, NPAIR - 1) as i:
                pair(i)
            pair(NPAIR - 1, last=True)
            transpose_m(B - 2)
            transpose_p(B - 1, NU2 - 2)
            weigh(B - 1, 1, NU2 - 3)
            route(B - 2)
            transpose_p(B - 1, NU2 - 1)
            weigh(B - 1, 1, NU2 - 2)
            weigh(B - 1, 1, NU2 - 1)
            for h in range(2):
                transpose_o(B - 1, 1, h)
            output2(B - 1, 1)
            transpose_m(B - 1)
            route(B - 1)
            count(NPAIR - 1)

            def transpose_rows(k, u, slot, turn):
                pe.wait_ge(s_xg[slot], 16 * (turn + 1))
                wait(pe, s_xgT, k)
                for c in range(2):
                    ins = pe.transpose(bank[0][0:C, c * MT:(c + 1) * MT], xg[:, slot, c * C:(c + 1) * C], ident[:])
                ins.then_inc(s_xgTp, 1)

            def expert_of(k):
                return pe.value_load(texp[0:1, bass.ds(k, 1)], min_val=0, max_val=E - 1)

            def up(k, u, e, part):
                pe.wait_ge(s_xgT, k + 1)
                dst = (GATE, UP)[part][u]
                for c in range(2):
                    ins = pe.matmul(dst[:, 0:FF], xgT[:, u, c, :], wgu[:, bass.ds(e * (4 * FF) + (2 * c + part) * FF, FF)],
                                    start=c == 0, stop=c == 1)
                if part:
                    ins.then_inc(s_up, 1)

            def transpose_h(k, u):
                pe.wait_ge(s_h, k + 1)
                for m in range(3):
                    ins = pe.transpose(bank[1][:, m * MT:(m + 1) * MT], hb[:, u, m * MT:(m + 1) * MT], ident[:])
                ins.then_inc(s_hTp, 1)

            def down(k, u, e):
                pe.wait_ge(s_hT, k + 1)
                wait(pe, s_y, k)
                for m in range(3):
                    ins = pe.matmul(bank[2][:, 0:D], hT[:, u, m, :], wdn[:, bass.ds(e * (3 * D) + m * D, D)], start=m == 0, stop=m == 2)
                ins.then_inc(s_dn, 1)

            def tile(k, u, slot, turn, last=False):
                if not last:
                    transpose_rows(k + 1, 1 - u, slot, turn)
                    e_next = expert_of(k + 1)
                    up(k + 1, 1 - u, e_next, 0)
                transpose_h(k, u)
                if not last:
                    up(k + 1, 1 - u, e_next, 1)
                down(k, u, expert_of(k))

            pe.wait_ge(SM["texp"], 1)
            pe.wait_ge(SM["we"], 16 * 6)
            transpose_rows(0, 0, 0, 0)
            e0 = expert_of(0)
            up(0, 0, e0, 0)
            up(0, 0, e0, 1)
            for k in range(NX + 1):
                tile(k, k % 2, (k + 1) % NX, (k + 1) // NX)
            with pe.Fori(1, NMT // NX - 1) as i:
                for r in range(1, NX + 1):
                    tile(NX * i + r, r % 2, (r + 1) % NX, i + (r + 1) // NX)
            for k in range(NMT - NX + 1, NMT):
                tile(k, k % 2, (k + 1) % NX, (k + 1) // NX, k == NMT - 1)


def host_layout(inputs):
    f = {k: np.asarray(v) for k, v in inputs.items()}
    rows = lambda v: np.ascontiguousarray(np.broadcast_to(v.reshape(1, -1), (128, v.size)))
    chunk = lambda w, k: np.ascontiguousarray(w.reshape(w.shape[0] // k, k, w.shape[1]).transpose(1, 0, 2))
    a = {"x": f["x"], "gamma": rows(f["L0_tok_gamma"]), "beta": rows(f["L0_tok_beta"]), "tokw": rows(f["L0_tok_w"]),
         "tokb": rows(f["L0_tok_b"]),
         "wq": chunk(f["L0_attn_w_query"].T, C), "wk": chunk(f["L0_attn_w_key"].T, C), "wv": chunk(f["L0_attn_w_value"].T, C),
         "wg": chunk(f["L0_attn_w_gate"].T, C), "wo": chunk(f["L0_attn_w_out"].T, 128)}
    w = f["L0_ffn_w_qkv"]
    split = lambda v: v.reshape(D, -1, HD // 2, 2).transpose(0, 1, 3, 2)
    q = split(w[:, :NQ * HD]).reshape(D, NKV, NQ // NKV * HD)
    k = split(w[:, NQ * HD:(NQ + NKV) * HD]).reshape(D, NKV, HD)
    v = w[:, (NQ + NKV) * HD:].reshape(D, NKV, HD)
    a["wqkv"] = chunk(np.concatenate([q, k, v], 2).reshape(D, NKV * GW), C).reshape(C, 2, NKV, GW)
    a["wout"] = chunk(f["L0_ffn_w_out"], 128)
    a["norm2w"] = rows(f["L0_ffn_norm2_w"])[:T]
    a["wr"] = chunk(f["L0_ffn_w_router"], C)
    a["wgu"] = f["L0_ffn_w_gate_up"].reshape(E, 2, C, 2 * FF).transpose(2, 0, 1, 3).reshape(C, E * 4 * FF)
    a["wdn"] = f["L0_ffn_w_down"].reshape(E, 3, FF // 3, D).transpose(2, 0, 1, 3).reshape(FF // 3, E * 3 * D)
    a["norm1w"] = rows(f["L0_ffn_norm1_w"])[:T]
    a.update(constants())
    return a


def kernel(**inputs):
    import concourse.bacc as _bacc
    from concourse import mybir as _mybir
    from concourse.bass_utils import run_bass_kernel_spmd as _run

    nc = _bacc.Bacc("TRN2", target_bir_lowering=False, num_devices=1)
    arrays, args = {}, {}
    for name, v in host_layout(inputs).items():
        v = np.ascontiguousarray(v)
        arrays[f"in_{name}"] = v
        args[name] = nc.dram_tensor(f"in_{name}", v.shape, _mybir.dt.from_np(v.dtype), kind="ExternalInput").ap()
    out = nc.dram_tensor("out_0", (B, KEEP, D), _mybir.dt.float32, kind="ExternalOutput").ap()
    build(nc, args, out)
    r = _run(nc, [arrays], core_ids=[0])
    return r.results[0]["out_0"]
```

```python
from contextlib import ExitStack

import numpy as np

import concourse.bass as bass
from concourse import mybir

F32 = mybir.dt.float32
BF16 = mybir.dt.bfloat16
I32 = mybir.dt.int32
ALU = mybir.AluOpType
ACT = mybir.ActivationFunctionType
AX = mybir.AxisListType.X

B, N0, D = 16, 250, 192
KEEP = int(N0 * 0.7)
HALF = N0 // 2
NT0 = 2 * B
T = (KEEP + 1) // 2
S = 2 * T
NT = 2 * B
NG = 4
GB = B // NG
C = D // 2
LN_EPS = 1e-5
RMS_EPS = 1e-6
NH, DK = 8, 64
DECAY, WRITE = 0.95, 0.1
NQ, NKV, HD = 12, 3, 64
THETA = 10000.0
GW = (NQ // NKV + 2) * HD
QKW = (NQ // NKV + 1) * HD
E, FF = 16, 384
MT = 128
NMT = (2 * NT * T + E * (MT - 1)) // MT
NMT += NMT % 2
RW = D + 4
GR = 4
NEARLY = 6
CAP = NT * T + MT
MASKED = -1e30
NX = 6
NOROW = 1 << 20


def constants():
    t = np.arange(S)
    c = {}
    s_, t_ = np.arange(T)[:, None], t[None, :]
    c["decay"] = np.where(s_ < t_, WRITE * DECAY ** np.maximum(t_ - 1 - s_, 0), 0.0).astype(np.float32)
    c["ident"] = np.eye(128, dtype=np.float32)
    inv = 1.0 / THETA ** (np.arange(0, HD, 2, dtype=np.float32) / HD)
    f = t[:, None].astype(np.float32) * inv[None, :].astype(np.float32)
    cos, sin = np.cos(f).astype(np.float32), np.sin(f).astype(np.float32)
    tile = lambda a: np.ascontiguousarray(a.reshape(2, T, -1).transpose(1, 0, 2))
    c["cos"] = tile(np.concatenate([cos, cos], 1))
    c["sin"] = tile(np.concatenate([-sin, sin], 1))
    c["causal"] = np.where(np.arange(T)[None, :] <= np.arange(T)[:, None], 0.0, MASKED).astype(np.float32)
    j = np.arange(N0)[None, :]
    c["earlier"] = np.stack([(j < HALF * h + np.arange(HALF)[:, None]) for h in range(2)], 1).astype(np.float32)
    c["rowbase"] = np.broadcast_to((N0 * (np.arange(NT0) // 2)).astype(np.float32), (128, NT0)).copy()
    c["before"] = (np.arange(T)[:, None] < np.arange(T)[None, :]).astype(np.float32)
    c["erank"] = np.broadcast_to((E - np.arange(E)).astype(np.float32), (128, E)).copy()
    row = KEEP * (np.arange(NT) // 2)[None, :] + T * (np.arange(NT) % 2)[None, :] + np.arange(T)[:, None]
    kept = T * (np.arange(NT) % 2)[None, :] + np.arange(T)[:, None] < KEEP
    c["outrow"] = np.where(kept, row, NOROW).astype(np.int32).view(np.float32)
    blank = np.zeros((MT, RW), np.int32)
    blank[:, D] = NOROW
    c["blank"] = blank.view(np.float32)
    c["tileno"] = np.broadcast_to(np.arange(NMT, dtype=np.float32), (MT, NMT)).copy()
    c["region"] = np.broadcast_to((CAP * np.arange(E)).astype(np.float32), (MT, E)).copy()
    return c


def build(nc, a, out):
    scores_d = nc.dram_tensor("scores_d", (NT0, HALF), F32).ap()
    rows_d = nc.dram_tensor("rows_d", (E * CAP + MT, RW), F32).ap()
    sorted_d = nc.dram_tensor("sorted_d", (B * N0, D), F32).ap()

    ctx = ExitStack()
    with ctx:
        def sb_in(stack, name, shape, dt=F32, side="left"):
            return stack.enter_context(nc.sbuf_tensor(name, shape, dt, side=side))

        def right(stack, name, shape, dt=F32):
            return sb_in(stack, name, shape, dt, "right")

        def sem(name):
            return ctx.enter_context(nc.semaphore(name))

        bank = [ctx.enter_context(nc.psum_tensor(f"bank{i}", [128, 512], F32)) for i in range(5)]
        proj = ctx.enter_context(nc.psum_tensor("proj", [128, 3, 512], F32))

        H = sb_in(ctx, "H", [T, NT, D])
        ident = sb_in(ctx, "ident", [128, 128])
        neg_half = sb_in(ctx, "neg_half", [128, NT])
        ln_eps = sb_in(ctx, "ln_eps", [128, 2])
        rms_eps = sb_in(ctx, "rms_eps", [128, 2])
        stream_rows = sb_in(ctx, "stream_rows", [128, NT * D])
        M = stream_rows[0:T].rearrange("p (n d) -> p n d", d=D)
        xg = stream_rows[:, 0:NX * RW].rearrange("p (x r) -> p x r", r=RW)
        ms = sb_in(ctx, "ms", [T, NT])

        mv2 = sb_in(ctx, "mv2", [T, 2, 2, 2])
        rs2 = sb_in(ctx, "rs2", [T, 2, 2])
        ms2 = sb_in(ctx, "ms2", [T, 2])
        st2 = sb_in(ctx, "st2", [T, 2, 6])
        before_b = sb_in(ctx, "before_b", [T, T], BF16)
        ones_b = sb_in(ctx, "ones_b", [T, MT], BF16)
        erank = sb_in(ctx, "erank", [128, E])
        tileno = sb_in(ctx, "tileno", [MT, NMT])
        run = sb_in(ctx, "run", [MT, E])
        region = sb_in(ctx, "region", [MT, E])
        outrow = sb_in(ctx, "outrow", [T, NT])
        blank = sb_in(ctx, "blank", [MT, RW])
        wr = sb_in(ctx, "wr", [C, 2, E])
        rr2 = sb_in(ctx, "rr2", [T, NT])
        rr3 = sb_in(ctx, "rr3", [T, NT])
        texp = sb_in(ctx, "texp", [1, NMT], I32)
        tneed = sb_in(ctx, "tneed", [1, NX], I32)
        tstart = sb_in(ctx, "tstart", [1, NMT], I32)
        rexp = sb_in(ctx, "rexp", [MT, NMT])
        cnt_i = sb_in(ctx, "cnt_i", [MT, E], I32)
        logit, sel1, sel2, hit, pick, pos = (sb_in(ctx, n, [T, GR, E]) for n in "logit sel1 sel2 hit pick pos".split())
        sel_b = sb_in(ctx, "sel_b", [T, GR, E], BF16)
        top1, top2, cm, cm2, ex2, w1, w2 = (sb_in(ctx, n, [T, GR]) for n in "top1 top2 cm cm2 ex2 w1 w2".split())
        send = sb_in(ctx, "send", [T, 2, GR, RW])
        slot_f = sb_in(ctx, "slot_f", [T, 2, GR])
        slot = sb_in(ctx, "slot", [T, 2, 2, GR], I32)

        early, selection, attn = ExitStack(), ExitStack(), ExitStack()
        wq = sb_in(early, "wq", [C, 2, NH * DK])
        wk = sb_in(early, "wk", [C, 2, NH * DK])
        wv = sb_in(early, "wv", [C, 2, NH * DK])
        wg = sb_in(early, "wg", [C, 2, NH])
        wo = sb_in(early, "wo", [128, NH * DK // 128, D])
        decay = sb_in(early, "decay", [T, S])
        st1 = sb_in(early, "st1", [T, 2, 6])
        mv1 = sb_in(early, "mv1", [T, 2, 2, 2])
        rs1 = sb_in(early, "rs1", [T, 2, 2])
        xn1 = sb_in(early, "xn1", [T, 2, 2, D])
        hx1 = sb_in(early, "hx1", [T, 2, 2, D])
        xT1 = sb_in(early, "xT1", [C, 2, 2, S])
        qT1 = sb_in(early, "qT1", [128, 2, 4, S])
        kT1 = sb_in(early, "kT1", [128, 4, S])
        gate = sb_in(early, "gate", [T, 2, NH])
        vg = sb_in(early, "vg", [T, 2, NH, DK])
        p0 = sb_in(early, "p0", [T, 2, NH, S])
        p1 = sb_in(early, "p1", [T, 2, NH, T])
        rT1 = sb_in(early, "rT1", [128, 2, 4, S])

        X = right(selection, "X", [HALF, NT0, D])
        GT = NT0 // NG
        junk_sq = right(selection, "junk_sq", [HALF, 2, GT, D])
        junk_dot = right(selection, "junk_dot", [HALF, 2, GT, D])
        junk_above = right(selection, "junk_above", [HALF, GT, N0])
        junk_tied = right(selection, "junk_tied", [HALF, GT, N0])
        gamma = right(selection, "gamma", [128, D])
        beta = right(selection, "beta", [128, D])
        tokw = right(selection, "tokw", [128, D])
        tokb = right(selection, "tokb", [128, 1])
        gw = right(selection, "gw", [128, D])
        bw = right(selection, "bw", [128, D])
        bsum = right(selection, "bsum", [128, 1])
        mu = right(selection, "mu", [HALF, NT0])
        minus_mu = right(selection, "minus_mu", [HALF, NT0])
        var = right(selection, "var", [HALF, NT0])
        dot = right(selection, "dot", [HALF, NT0])
        rs0 = right(selection, "rs0", [HALF, NT0])
        score = right(selection, "score", [HALF, NT0])
        score_t = right(selection, "score_t", [GT, NG, HALF])
        all_scores = right(selection, "all_scores", [HALF, NT0 * HALF])
        earlier = right(selection, "earlier", [HALF, 2, N0])
        rowbase = right(selection, "rowbase", [128, NT0])
        above = right(selection, "above", [HALF, NT0])
        tied = right(selection, "tied", [HALF, NT0])
        rank = right(selection, "rank", [HALF, NT0], I32)

        selection.close()

        early.close()

        wdn = right(ctx, "wdn", [FF // 3, E * 3 * D])
        wqkv = right(attn, "wqkv", [C, 2, NKV, GW])
        before = right(attn, "before", [T, T])
        norm2w = right(attn, "norm2w", [T, D])
        wout = right(attn, "wout", [128, NQ * HD // 128, D])
        cos = right(attn, "cos", [T, 2, HD])
        sin = right(attn, "sin", [T, 2, HD])
        norm1w = right(attn, "norm1w", [T, D])
        causal = right(attn, "causal", [T, T])
        causal_b = right(attn, "causal_b", [T, T], BF16)
        ident_b = right(attn, "ident_b", [T, T], BF16)
        xr = right(attn, "xr", [T, 2, D])
        xrT = right(attn, "xrT", [C, 2, 2, S])
        rope_c = right(attn, "rope_c", [T, 2, QKW])
        rope_s = right(attn, "rope_s", [T, 2, QKW])
        rot = right(attn, "rot", [T, 2, QKW + HD])
        qkT = right(attn, "qkT", [128, 2, NKV, 3, S])
        val = right(attn, "val", [T, 2, 2, NKV, HD])
        mx = right(attn, "mx", [T, 2, 3])
        shift = right(attn, "shift", [T, 2, 3])
        pr = right(attn, "pr", [T, 2, 2 * S])
        pT = right(attn, "pT", [T, 4, 2 * S])
        den = right(attn, "den", [T, 2, 3])
        rden = right(attn, "rden", [T, 2, 3])
        oT = right(attn, "oT", [128, 2, 6, T])
        sqj = right(attn, "sqj", [T, 2, D])
        mrow = right(attn, "mrow", [T, 2, D])
        mT = right(attn, "mT", [C, 2, S])
        attn.close()

        wgu = sb_in(ctx, "wgu", [C, E * 4 * FF])
        til, end_a, end_b, skip = (sb_in(ctx, n, [MT, E]) for n in ("til", "end_a", "end_b", "skip"))
        til_i = sb_in(ctx, "til_i", [MT, E], I32)
        table = ExitStack()
        past = sb_in(table, "past", [MT, NMT, E])
        jump = sb_in(table, "jump", [MT, NMT, E])
        texp_f = sb_in(table, "texp_f", [MT, NMT])
        need_f = sb_in(table, "need_f", [1, NX])
        tstart_f = sb_in(table, "tstart_f", [MT, NMT])
        table.close()
        xgT = sb_in(ctx, "xgT", [C, 2, 2, MT])
        sg = sb_in(ctx, "sg", [MT, 2, FF])
        hb = sb_in(ctx, "hb", [MT, 2, FF])
        hT = sb_in(ctx, "hT", [MT, 2, 3, MT])
        wv_ = sb_in(ctx, "wv_", [MT, 2, 2])
        ys = sb_in(ctx, "ys", [MT, 2, D])

        s_dve = sem("s_dve")
        s_pool = sem("s_pool")
        s_apart = sem("s_apart")
        s_const = sem("s_const")
        s_tok_in = [sem(f"s_tok_in{i}") for i in range(NG)]
        s_tok_vec = sem("s_tok_vec")
        s_centered = sem("s_centered")
        s_squared = sem("s_squared")
        s_stats = sem("s_stats")
        s_rs0 = sem("s_rs0")
        s_score = sem("s_score")
        s_score_tp = sem("s_score_tp")
        s_score_t = sem("s_score_t")
        s_score_out = [sem(f"s_score_out{i}") for i in range(NG)]
        s_score_in = [sem(f"s_score_in{i}") for i in range(NG)]
        s_rank = sem("s_rank")
        s_sorted = [sem(f"s_sorted{i}") for i in range(2 * NG)]
        s_hzero = sem("s_hzero")
        s_h0 = [sem(f"s_h0{i}") for i in range(2 * NG)]
        s_w1 = sem("s_w1")
        s_mv1 = sem("s_mv1")
        s_rs1 = sem("s_rs1")
        s_xn1 = sem("s_xn1")
        s_hx1 = sem("s_hx1")
        s_xTp1 = sem("s_xTp1")
        s_xT1 = sem("s_xT1")
        s_qp1 = sem("s_qp1")
        s_q1 = sem("s_q1")
        s_kvg = sem("s_kvg")
        s_kv = sem("s_kv")
        s_gate = sem("s_gate")
        s_sc1 = sem("s_sc1")
        s_p1 = sem("s_p1")
        s_rp1 = sem("s_rp1")
        s_r1 = sem("s_r1")
        s_o1 = sem("s_o1")
        s_h1 = sem("s_h1")
        s_mv2 = sem("s_mv2")
        s_rs2 = sem("s_rs2")
        s_x3 = sem("s_x3")
        s_w2 = sem("s_w2")
        s_w2b = sem("s_w2b")
        s_xr = sem("s_xr")
        s_xTp2 = sem("s_xTp2")
        s_xrT = sem("s_xrT")
        s_proj = sem("s_proj")
        s_rope = sem("s_rope")
        s_rot = sem("s_rot")
        s_val = sem("s_val")
        s_qkTp = sem("s_qkTp")
        s_qkT = sem("s_qkT")
        s_sc2 = sem("s_sc2")
        s_shift = sem("s_shift")
        s_pr = sem("s_pr")
        s_pn = sem("s_pn")
        s_tp = sem("s_tp")
        s_pT = sem("s_pT")
        s_pv = sem("s_pv")
        s_oT = sem("s_oT")
        s_wo = sem("s_wo")
        s_h2 = sem("s_h2")
        s_hadd = sem("s_hadd")
        s_const2 = sem("s_const2")
        s_ms = sem("s_ms")
        s_rr3 = sem("s_rr3")
        s_mrow = sem("s_mrow")
        s_send = sem("s_send")
        s_mTp = sem("s_mTp")
        s_mT = sem("s_mT")
        s_logit = sem("s_logit")
        s_logit_in = sem("s_logit_in")
        s_logit_used = sem("s_logit_used")
        s_sel = sem("s_sel")
        s_gap = sem("s_gap")
        s_exp = sem("s_exp")
        s_cum = sem("s_cum")
        s_cum_read = sem("s_cum_read")
        s_slot = sem("s_slot")
        s_rows = [sem(f"s_rows{i}") for i in range(2)]
        s_count = sem("s_count")
        s_fill = sem("s_fill")
        s_fill_b = sem("s_fill_b")
        s_tables = sem("s_tables")
        s_expert_w = sem("s_expert_w")
        s_base = sem("s_base")
        s_xg = [sem(f"s_xg{i}") for i in range(NX)]
        s_xgTp = sem("s_xgTp")
        s_xgT = sem("s_xgT")
        s_gated = sem("s_gated")
        s_up = sem("s_up")
        s_sg = sem("s_sg")
        s_h = sem("s_h")
        s_hTp = sem("s_hTp")
        s_hT = sem("s_hT")
        s_dn = sem("s_dn")
        s_y = sem("s_y")
        s_add = sem("s_add")

        def wait(eng, s, v):
            if isinstance(v, int) and v <= 0:
                return
            eng.wait_ge(s, v)

        def wait_apart(eng, s, v):
            eng.wait_ge(s, v)
            eng.sem_inc(s_apart, 1)

        class Chain:

            def __init__(self, eng, s):
                self.eng, self.s, self.base, self.n = eng, s, 0, 0

            def link(self, ins, apart=False):
                ins.then_inc(self.s, 1)
                self.n += 1
                self.eng.wait_ge(self.s, self.base + self.n)
                if apart:
                    self.eng.sem_inc(s_apart, 1)

            def enter(self, i, per):
                self.start = self.n_done
                self.base, self.n, self.per = self.n_done + i * per, 0, per

            def leave(self, iterations):
                assert self.n == self.per, (self.n, self.per)
                self.n_done = self.start + iterations * self.per
                self.base, self.n = self.n_done, 0

            def settle(self):
                self.n_done = self.base + self.n

        block = ctx.enter_context(nc.Block())
        TX1, Q1A, Q1B, SC1A, SC1B = bank
        R1 = [proj[:, 0, :], proj[:, 1, :]]
        O1 = proj[:, 2, :]
        Q1 = [Q1A, Q1B]
        SC1 = [SC1A, SC1B]
        UNITS1 = [(1, (0, 2, 4, 6)), (1, (1, 3, 5, 7)), (0, (0, 2)), (0, (1, 3)), (0, (4, 6)), (0, (5, 7))]
        NU1 = len(UNITS1)
        UNITS2 = [(0, (0, 2, 4)), (0, (1, 3, 5)), (0, (6, 8, 10)), (0, (7, 9, 11)),
                  (1, (0, 2)), (1, (1, 3)), (1, (4, 6)), (1, (5, 7)), (1, (8, 10)), (1, (9, 11))]
        NU2 = len(UNITS2)
        NPU = NU2 // 2
        unit_width = lambda k: len(UNITS2[k][1]) * (UNITS2[k][0] + 1) * T
        buffer4 = lambda u, k: (2 * u + k) % 4
        NCH = 2 * NKV
        NPAIR = B // 2
        WE_EARLY, WE_ALL = 16 * 4, 16 * 6
        PT2, O2, MISC, SC2A, SC2B = bank
        SC2 = [SC2A, SC2B]
        GATE = [bank[3], proj[:, 0, :]]
        UP = [bank[4], proj[:, 1, :]]

        @block.sync
        def _(sp):
            sp.dma_start(gamma[:], a["gamma"]).then_inc(s_tok_vec, 16)
            sp.dma_start(beta[:], a["beta"]).then_inc(s_tok_vec, 16)
            sp.dma_start(tokw[:], a["tokw"]).then_inc(s_tok_vec, 16)
            sp.dma_start(tokb[:], a["tokb"]).then_inc(s_tok_vec, 16)
            for g in range(NG):
                sp.dma_start(X[:, GT * g:GT * (g + 1), :],
                             a["x"][GB * g:GB * (g + 1)].rearrange("b (h p) d -> p (b h) d", h=2)).then_inc(s_tok_in[g], 16)
            sp.dma_start(ident[:], a["ident"]).then_inc(s_const, 16)
            sp.dma_start(earlier[:], a["earlier"]).then_inc(s_const, 16)
            sp.dma_start(rowbase[:], a["rowbase"]).then_inc(s_const, 16)
            for t_, n in ((wq, "wq"), (wk, "wk"), (wv, "wv"), (wg, "wg"), (wo, "wo"), (decay, "decay")):
                sp.dma_start(t_[:], a[n]).then_inc(s_w1, 16)
            def broadcast(g):
                rows = scores_d[GT * g:GT * (g + 1), :]
                sp.wait_ge(s_score_t, g + 1)
                sp.dma_start(rows, score_t[:, g, :]).then_inc(s_score_out[g], 16)
                sp.wait_ge(s_score_out[g], 16)
                sp.dma_start(all_scores[:, GT * HALF * g:GT * HALF * (g + 1)],
                             rows.rearrange("n p -> (n p)").partition_broadcast(HALF)).then_inc(s_score_in[g], 16)

            def load_sorted(q):
                sp.wait_ge(s_sorted[q], 16 * 4)
                rows = sorted_d.rearrange("(b n) d -> n b d", n=N0)
                Hv = H[:].rearrange("p (b h) d -> p b h d", h=2)
                for h in range(2):
                    n = min(T, KEEP - T * h)
                    sp.dma_start(Hv[0:n, 2 * q:2 * q + 2, h, :], rows[T * h:T * h + n, 2 * q:2 * q + 2, :]).then_inc(s_h0[q], 16)

            broadcast(0)
            broadcast(1)
            sp.wait_ge(s_hzero, 1)
            load_sorted(0)
            load_sorted(1)
            broadcast(2)
            broadcast(3)
            for q in range(2, 2 * NG):
                load_sorted(q)
            for t_, n in ((wqkv, "wqkv"), (wout, "wout"), (cos, "cos"), (sin, "sin"), (norm1w, "norm1w"), (causal, "causal")):
                sp.dma_start(t_[:], a[n]).then_inc(s_w2, 16)
            for t_, n in ((before, "before"), (erank, "erank"), (tileno, "tileno"), (region, "region"), (outrow, "outrow"),
                          (norm2w, "norm2w"), (wr, "wr"), (blank, "blank")):
                sp.dma_start(t_[:], a[n]).then_inc(s_const2, 16)
            sp.wait_ge(s_const2, 16 * 8)
            sp.dma_start(rows_d[E * CAP:E * CAP + MT, :], blank[:]).then_inc(s_fill, 16)
            for q in range(2):
                n = E // 2 * 3 * D
                sp.dma_start(wdn[:, q * n:(q + 1) * n], a["wdn"][:, q * n:(q + 1) * n]).then_inc(s_expert_w, 16)
            sp.wait_ge(s_x3, B)
            sp.wait_ge(s_rs2, B)
            for q in range(2):
                n = NEARLY // 2 * 4 * FF
                sp.dma_start(wgu[:, q * n:(q + 1) * n], a["wgu"][:, q * n:(q + 1) * n]).then_inc(s_expert_w, 16)
            sp.wait_ge(s_hadd, 2 * B)
            orow = out.rearrange("b t d -> t b d")
            for h in range(2):
                n = min(T, KEEP - T * h)
                Hv = H[:].rearrange("p (b h) d -> p b h d", h=2)
                sp.dma_start(orow[T * h:T * h + n, :, :], Hv[0:n, :, h, :]).then_inc(s_base, 16)
            sp.wait_ge(s_count, 1)
            for e in range(0, E, 2):
                end = sp.value_load(cnt_i[0:1, e:e + 1], min_val=0, max_val=E * CAP - MT)
                sp.dma_start(rows_d[bass.ds(end, MT), :], blank[:]).then_inc(s_fill, 16)

            def load(k, slot, turn):
                wait(sp, s_add, 16 * (k - NX + 1))
                start = sp.value_load(tstart[0:1, bass.ds(k, 1)], min_val=0, max_val=E * CAP)
                src = rows_d[bass.ds(start, MT), :]
                sp.dma_start(xg[:, slot, :], src).then_inc(s_xg[slot], 16)

            sp.wait_ge(s_tables, 1)
            sp.wait_ge(s_fill, 16 * (E // 2 + 1))
            sp.wait_ge(s_fill_b, 16 * (E // 2))
            sp.wait_ge(s_rows[0], 16 * NT)
            sp.wait_ge(s_rows[1], 16 * NT)
            for k in range(NX):
                load(k, k, 0)
            lo = NEARLY * 4 * FF
            for q in range(2):
                n = (E - NEARLY) // 2 * 4 * FF
                sp.dma_start(wgu[:, lo + q * n:lo + (q + 1) * n], a["wgu"][:, lo + q * n:lo + (q + 1) * n]).then_inc(s_expert_w, 16)
            with sp.Fori(1, NMT // NX) as i:
                for r in range(NX):
                    load(NX * i + r, r, i)

        @block.gpsimd
        def _(pool):
            ch = Chain(pool, s_pool)
            pool.memset(neg_half[:], -0.5)
            pool.memset(ln_eps[:], LN_EPS)
            pool.memset(rms_eps[:], RMS_EPS)
            ch.link(pool.memset(H[:], 0.0))
            pool.sem_inc(s_hzero, 1)
            def token_rs(g):
                grp = slice(GT * g, GT * (g + 1))
                pool.wait_ge(s_stats, g + 1)
                pool.tensor_tensor(rs0[:, grp], var[:, grp], neg_half[0:HALF, grp], ALU.pow).then_inc(s_rs0, 1)

            def sort(g, half):
                pool.wait_ge(s_rank, 2 * g + half + 1)
                for n in range(GT * g + GT // 2 * half, GT * g + GT // 2 * (half + 1)):
                    pool.indirect_dma_start(out=sorted_d, out_offset=bass.IndirectOffsetOnAxis(ap=rank[:, n:n + 1], axis=0),
                                            in_=X[:, n, :], in_offset=None).then_inc(s_sorted[2 * g + half], 16)

            token_rs(0)
            token_rs(1)
            token_rs(2)
            sort(0, 0)
            sort(0, 1)
            token_rs(3)
            ch.settle()

            def norm1(b, u):
                wait_apart(pool, s_mv1, b + 1)
                ch.link(pool.tensor_scalar(rs1[:, u], mv1[:, u, :, 1], LN_EPS, None, ALU.add))
                pool.tensor_tensor(rs1[:, u], rs1[:, u], neg_half[0:T, 0:2], ALU.pow).then_inc(s_rs1, 1)

            def residual1(b, u):
                if not isinstance(b, int) or b >= 2:
                    wait_apart(pool, s_h1, b - 1)
                pool.wait_ge(s_xn1, b + 1)
                pool.tensor_tensor(hx1[:, u], H[:, bass.ds(2 * b, 2), :], xn1[:, u], ALU.add).then_inc(s_hx1, 1)

            def norm2(b, u):
                pool.wait_ge(s_mv2, b + 1)
                ch.link(pool.tensor_tensor(rs2[:, u], mv2[:, u, :, 1], ln_eps[0:T, :], ALU.add))
                ch.link(pool.tensor_tensor(rs2[:, u], rs2[:, u], neg_half[0:T, 0:2], ALU.pow))
                ch.link(pool.tensor_tensor(ms2[:], rs2[:, u], rs2[:, u], ALU.mult))
                ch.link(pool.tensor_tensor(ms2[:], ms2[:], mv2[:, u, :, 1], ALU.mult), apart=True)
                ch.link(pool.tensor_scalar(ms2[:], ms2[:], RMS_EPS, None, ALU.add), apart=True)
                pool.tensor_tensor(rr2[:, bass.ds(2 * b, 2)], ms2[:], neg_half[0:T, 0:2], ALU.pow).then_inc(s_rs2, 1)

            def body(b, u, prev, nxt, nxt2, *parts):
                if nxt2 is not None:
                    norm1(nxt2, u)
                if nxt is not None:
                    residual1(nxt, 1 - u)
                if prev is not None:
                    norm2(prev, 1 - u)
                for part in parts:
                    sort(*part)

            norm1(0, 0)
            residual1(0, 0)
            norm1(1, 1)
            body(0, 0, None, 1, 2, (1, 0), (1, 1))
            body(1, 1, 0, 2, 3, (2, 0))
            body(2, 0, 1, 3, 4, (2, 1))
            body(3, 1, 2, 4, 5, (3, 0))
            body(4, 0, 3, 5, 6, (3, 1))
            body(5, 1, 4, 6, 7)
            ch.settle()
            with pool.Fori(3, B // 2 - 1) as i:
                ch.enter(i - 3, 12)
                body(2 * i, 0, 2 * i - 1, 2 * i + 1, 2 * i + 2)
                body(2 * i + 1, 1, 2 * i, 2 * i + 2, 2 * i + 3)
            ch.leave(B // 2 - 4)
            body(B - 2, 0, B - 3, B - 1, None)
            pool.memset(ones_b[:], 1.0).then_inc(s_w2b, 1)
            body(B - 1, 1, B - 2, None, None)
            ch.settle()


            def rotate(b, c):
                q = NCH * b + c
                pool.wait_ge(s_rope, q + 1)
                wait(pool, s_qkTp, q - 1)
                pool.tensor_tensor(rot[:, c % 2, 0:QKW], rope_c[:, c % 2], rope_s[:, c % 2], ALU.add)
                pool.tensor_tensor(rot[:, c % 2, QKW:QKW + HD], rope_c[:, c % 2, QKW - HD:QKW], rope_s[:, c % 2, QKW - HD:QKW],
                                   ALU.add).then_inc(s_rot, 1)

            def stream(b, j):
                n = bass.ds(2 * b + j, 1)
                pool.wait_ge(s_h2, 2 * b + j + 1)
                pool.tensor_tensor(H[:, n, :], H[:, n, :], M[:, n, :], ALU.add).then_inc(s_hadd, 1)

            def norm3(b):
                n = bass.ds(2 * b, 2)
                wait_apart(pool, s_ms, b + 1)
                ch.link(pool.tensor_tensor(rr3[:, n], ms[:, n], rms_eps[0:T, :], ALU.add), apart=True)
                pool.tensor_tensor(rr3[:, n], rr3[:, n], neg_half[0:T, 0:2], ALU.pow).then_inc(s_rr3, 1)

            def dispatch(g, u, *tiles):
                wait_apart(pool, s_slot, g + 1)
                for j in tiles:
                    for p in range(2):
                        pool.indirect_dma_start(out=rows_d, out_offset=bass.IndirectOffsetOnAxis(ap=slot[:, u, p, j:j + 1], axis=0),
                                                in_=send[:, u, j, :],
                                                in_offset=None).then_inc(s_rows[u], 16)

            def batch(b, prev, nxt, group=None, gu=0, half=0):
                if prev is not None:
                    stream(prev, 0)
                rotate(b, 3)
                if group is not None:
                    dispatch(group, gu, 2 * half)
                rotate(b, 4)
                rotate(b, 5)
                if nxt is not None:
                    rotate(nxt, 0)
                if group is not None:
                    dispatch(group, gu, 2 * half + 1)
                if prev is not None:
                    stream(prev, 1)
                    norm3(prev)
                if nxt is not None:
                    rotate(nxt, 1)
                    rotate(nxt, 2)

            def pair(i, group=None, gu=0, first=False, last=False):
                batch(2 * i, None if first else 2 * i - 1, 2 * i + 1, group, gu, 0)
                batch(2 * i + 1, 2 * i, None if last else 2 * i + 2, group, gu, 1)

            for c in range(NKV):
                rotate(0, c)
            norm2(B - 1, 1)
            pair(0, first=True)
            pair(1)
            pair(2, 0, 0)
            ch.settle()
            with pool.Fori(1, NPAIR // 2 - 1) as i:
                ch.enter(i - 1, 4)
                pair(2 * i + 1, 2 * i - 1, 1)
                pair(2 * i + 2, 2 * i, 0)
            ch.leave(NPAIR // 2 - 2)
            pair(NPAIR - 1, NPAIR - 3, 1, last=True)
            stream(B - 1, 0)
            stream(B - 1, 1)
            norm3(B - 1)
            for g in (NPAIR - 2, NPAIR - 1):
                dispatch(g, g % 2, *range(GR))

            pool.wait_ge(s_base, 32)

            def add(k, u, slot):
                wait_apart(pool, s_y, k + 1)
                if not isinstance(k, int) or k:
                    wait_apart(pool, s_add, 16 * k)
                pool.indirect_dma_start(out=out.rearrange("b t d -> (b t) d"),
                                        out_offset=bass.IndirectOffsetOnAxis(ap=xg[:, slot, D:D + 1].bitcast(I32), axis=0),
                                        in_=ys[:, u, :], in_offset=None, bounds_check=B * KEEP - 1, oob_is_err=False,
                                        compute_op=ALU.add).then_inc(s_add, 16)

            for k in range(NX):
                add(k, k % 2, k)
            with pool.Fori(1, NMT // NX) as i:
                for r in range(NX):
                    add(NX * i + r, r % 2, r)
            pool.wait_ge(s_add, 16 * NMT)

        @block.scalar
        def _(act):
            def squares(g):
                act.wait_ge(s_centered, g + 1)
                wait(act, s_squared, g - 1)
                for k in range(GT):
                    n = GT * g + k
                    ins = act.activation(junk_sq[:, g % 2, k, :], X[:, n, :], ACT.Square, bias=minus_mu[:, n:n + 1],
                                         accum_out=var[:, n:n + 1])
                ins.then_inc(s_squared, 1)

            def score_copy(g):
                act.wait_ge(s_score_tp, g + 1)
                act.copy(score_t[:, g, :], bank[g][0:GT, 0:HALF]).then_inc(s_score_t, 1)

            squares(0)
            squares(1)
            for g in range(2, NG):
                score_copy(g - 2)
                squares(g)
            for g in range(NG - 2, NG):
                score_copy(g)

            def xT_copy(b, u):
                act.wait_ge(s_xTp1, b + 1)
                act.copy(xT1[:, u], TX1[0:C, 0:2 * S].rearrange("p (c t) -> p c t", c=2)).then_inc(s_xT1, 1)

            def q_copy(b, u, h):
                act.wait_ge(s_qp1, 2 * b + h + 1)
                act.copy(qT1[:, u, 2 * h:2 * h + 2, :], Q1[h][:, 0:2 * S].rearrange("p (m t) -> p m t", m=2)).then_inc(s_q1, 1)

            def r_copy(b, u, h):
                act.wait_ge(s_rp1, 2 * b + h + 1)
                if h == 0:
                    wait(act, s_o1, b)
                act.copy(rT1[:, u, 2 * h:2 * h + 2, :], R1[h][:, 0:2 * S].rearrange("p (m t) -> p m t", m=2)).then_inc(s_r1, 1)

            xT_copy(0, 0)
            for h in range(2):
                act.wait_ge(s_kvg, h + 1)
                act.copy(kT1[:, 2 * h:2 * h + 2, :], Q1[h][:, 0:2 * S].rearrange("p (m t) -> p m t", m=2)).then_inc(s_kv, 1)
            act.wait_ge(s_kvg, 3)
            act.activation(gate[:], O1[0:T, 0:2 * NH].rearrange("p (h e) -> p h e", h=2), ACT.Exp, scale=-1.0).then_inc(s_gate, 1)
            for h in range(2):
                q_copy(0, 0, h)

            def body(b, u, nxt):
                if nxt is not None:
                    xT_copy(nxt, 1 - u)
                r_copy(b, u, 0)
                if nxt is not None:
                    q_copy(nxt, 1 - u, 0)
                r_copy(b, u, 1)
                if nxt is not None:
                    q_copy(nxt, 1 - u, 1)

            body(0, 0, 1)
            with act.Fori(0, B // 2 - 1) as i:
                body(2 * i + 1, 1, 2 * i + 2)
                body(2 * i + 2, 0, 2 * i + 3)
            body(B - 1, 1, None)

            def xrT_copy(b, u):
                act.wait_ge(s_xTp2, b + 1)
                act.copy(xrT[:, u], MISC[0:C, 0:2 * S].rearrange("p (c t) -> p c t", c=2)).then_inc(s_xrT, 1)

            def val_copy(b, u, c):
                act.wait_ge(s_rope, NCH * b + c + 1)
                act.copy(val[:, u, c // NKV, c % NKV, :], proj[0:T, c % NKV, QKW:GW]).then_inc(s_val, 1)

            def qkT_copy(b, u, c):
                j, g = c // NKV, c % NKV
                act.wait_ge(s_qkTp, NCH * b + c + 1)
                act.copy(qkT[:, u, g, :, j * T:(j + 1) * T], proj[:, g, 0:3 * T].rearrange("p (k t) -> p k t", k=3)).then_inc(s_qkT, 1)

            def exponent(b, k):
                tile, heads = UNITS2[k]
                w = (T, S)[tile]
                wait_apart(act, s_shift, NU2 * b + k + 1)
                if not isinstance(b, int) or NU2 * b + k >= 2:
                    wait_apart(act, s_tp, NU2 * b + k - 1)
                for n in range(len(heads)):
                    ins = act.activation(pr[:, k % 2, n * w:(n + 1) * w], SC2[k % 2][0:T, n * w:(n + 1) * w], ACT.Exp,
                                         bias=shift[:, k % 2, n:n + 1], scale=HD ** -0.5, accum_out=den[:, k % 2, n:n + 1])
                ins.then_inc(s_pr, 1)

            def pT_copy(b, u, k):
                w = unit_width(k)
                act.wait_ge(s_tp, NU2 * b + k + 1)
                wait(act, s_pv, NPU * b + k // 2 - 1)
                act.copy(pT[:, buffer4(u, k), 0:w], PT2[0:T, 0:w]).then_inc(s_pT, 1)

            def oT_copy(b, p):
                tile, heads = UNITS2[2 * p]
                m = heads[0] // 2
                if p in (0, 2):
                    wait(act, s_wo, 2 * b - 1 + tile)
                act.wait_ge(s_pv, NPU * b + p + 1)
                act.copy(oT[:, tile, m:m + len(heads), :], O2[:, 0:len(heads) * T].rearrange("p (m t) -> p m t", t=T)).then_inc(s_oT, 1)

            def mT_copy(b):
                act.wait_ge(s_mTp, b + 1)
                act.copy(mT[:], MISC[0:C, 0:2 * S].rearrange("p (c t) -> p c t", c=2)).then_inc(s_mT, 1)

            def put(b, u, gu, turn):
                act.wait_ge(s_mrow, b + 1)
                if u == 0:
                    wait(act, s_rows[gu], 16 * 2 * GR * turn)
                act.copy(send[:, gu, 2 * u:2 * u + 2, 0:D], mrow[:]).then_inc(s_send, 1)

            def weight_exp(g):
                act.wait_ge(s_gap, g + 1)
                act.activation(ex2[:], top2[:], ACT.Exp).then_inc(s_exp, 1)

            act.wait_ge(s_w2b, 1)
            xrT_copy(0, 0)
            val_copy(0, 0, 0)
            val_copy(0, 0, 1)
            qkT_copy(0, 0, 0)
            val_copy(0, 0, 2)
            qkT_copy(0, 0, 1)
            qkT_copy(0, 0, 2)

            def batch(b, u, prev, prev2, nxt, group=None, g0=0, gu=0, turn=0, attend=True):
                for k in range(NU2):
                    if attend:
                        if k in (1, 3, 4):
                            val_copy(b, u, {1: 3, 3: 4, 4: 5}[k])
                        if k in (2, 4, 5):
                            qkT_copy(b, u, {2: 3, 4: 4, 5: 5}[k])
                    if nxt is not None:
                        if k in (5, 7, 8):
                            val_copy(nxt, 1 - u, {5: 0, 7: 1, 8: 2}[k])
                        if k in (6, 8, 9):
                            qkT_copy(nxt, 1 - u, {6: 0, 8: 1, 9: 2}[k])
                    if k == 0 and prev2 is not None:
                        put(prev2, u, gu, turn)
                        mT_copy(prev2)
                    if k == 1 and prev2 is not None:
                        logit_copy(prev2, u, g0)
                    if k == 2 and nxt is not None:
                        xrT_copy(nxt, 1 - u)
                    if k in (1, 3) and prev is not None:
                        oT_copy(prev, {1: 3, 3: 4}[k])
                    if k in (5, 7, 9) and attend:
                        oT_copy(b, {5: 0, 7: 1, 9: 2}[k])
                    if k < 2:
                        if prev is not None:
                            pT_copy(prev, 1 - u, NU2 - 2 + k)
                    elif attend:
                        pT_copy(b, u, k - 2)
                    if k == 5 and group is not None:
                        weight_exp(group)
                    if attend:
                        exponent(b, k)

            def logit_copy(b, u, g):
                act.wait_ge(s_logit, b + 1)
                if u == 0:
                    wait(act, s_logit_used, g)
                act.copy(logit[:, 2 * u:2 * u + 2, :], MISC[0:T, 0:2 * E].rearrange("p (h e) -> p h e", h=2)).then_inc(s_logit_in, 1)

            def pair(i, gu=0, turn=0, first=False, last=False):
                batch(2 * i, 0, None if first else 2 * i - 1, None if first else 2 * i - 2, 2 * i + 1, None, i - 1, gu, turn)
                batch(2 * i + 1, 1, 2 * i, None if first else 2 * i - 1, None if last else 2 * i + 2, None if first else i - 1,
                      0, gu, turn)

            pair(0, first=True)
            pair(1, 0, 0)
            pair(2, 1, 0)
            with act.Fori(1, NPAIR // 2 - 1) as i:
                pair(2 * i + 1, 0, i)
                pair(2 * i + 2, 1, i)
            pair(NPAIR - 1, 0, NPAIR // 2 - 1, last=True)
            batch(B, 0, B - 1, B - 2, None, None, NPAIR - 1, 1, NPAIR // 2 - 1, attend=False)
            put(B - 1, 1, 1, NPAIR // 2 - 1)
            mT_copy(B - 1)
            logit_copy(B - 1, 1, NPAIR - 1)
            weight_exp(NPAIR - 1)

            act.wait_ge(s_count, 1)
            for e in range(1, E, 2):
                end = act.value_load(cnt_i[0:1, e:e + 1], min_val=0, max_val=E * CAP - MT)
                act.dma_start(rows_d[bass.ds(end, MT), :], blank[:]).then_inc(s_fill_b, 16)

            def xgT_copy(k, u):
                act.wait_ge(s_xgTp, k + 1)
                act.copy(xgT[:, u], bank[0][0:C, 0:2 * MT].rearrange("p (c t) -> p c t", c=2)).then_inc(s_xgT, 1)

            def silu(k, u):
                act.wait_ge(s_gated, k + 1)
                act.activation(sg[:, u], GATE[u][:, 0:FF], ACT.Silu).then_inc(s_sg, 1)

            def hT_copy(k, u):
                act.wait_ge(s_hTp, k + 1)
                act.copy(hT[:, u], bank[1][:, 0:FF].rearrange("p (m t) -> p m t", m=3)).then_inc(s_hT, 1)

            def tile(k, u, last=0):
                if last < 2:
                    silu(k + 1, 1 - u)
                hT_copy(k, u)
                if last < 1:
                    xgT_copy(k + 2, u)

            xgT_copy(0, 0)
            xgT_copy(1, 1)
            silu(0, 0)
            for k in range(NX):
                tile(k, k % 2)
            with act.Fori(1, NMT // NX - 1) as i:
                for r in range(NX):
                    tile(NX * i + r, r % 2)
            for k in range(NMT - NX, NMT):
                tile(k, k % 2, max(0, k - (NMT - 3)))

        @block.vector
        def _(dve):
            ch = Chain(dve, s_dve)
            dve.wait_ge(s_tok_vec, 64)
            dve.tensor_tensor(gw[:], gamma[:], tokw[:], ALU.mult)
            ch.link(dve.tensor_tensor(bw[:], beta[:], tokw[:], ALU.mult))
            ch.link(dve.tensor_reduce(bsum[:], bw[:], AX, ALU.add))
            ch.link(dve.tensor_tensor(bsum[:], bsum[:], tokb[:], ALU.add))

            def means(g):
                lo, hi = GT * g, GT * (g + 1)
                dve.wait_ge(s_tok_in[g], 16)
                ch.link(dve.tensor_reduce(mu[:, lo:hi], X[:, lo:hi, :], AX, ALU.add))
                dve.tensor_scalar(minus_mu[:, lo:hi], mu[:, lo:hi], -1.0 / D, None, ALU.mult).then_inc(s_centered, 1)
                ch.link(dve.tensor_scalar(mu[:, lo:hi], mu[:, lo:hi], 1.0 / D, None, ALU.mult))
                for n in range(lo, hi):
                    ins = dve.scalar_tensor_tensor(junk_dot[:, g % 2, n - lo, :], X[:, n, :], mu[:, n:n + 1], gw[0:HALF, :],
                                                   ALU.subtract, ALU.mult, accum_out=dot[:, n:n + 1])
                ch.link(ins)

            def stats(g):
                grp = slice(GT * g, GT * (g + 1))
                dve.wait_ge(s_squared, g + 1)
                dve.tensor_scalar(var[:, grp], var[:, grp], 1.0 / D, LN_EPS, ALU.mult, ALU.add).then_inc(s_stats, 1)

            def scores(g):
                grp = slice(GT * g, GT * (g + 1))
                dve.wait_ge(s_rs0, g + 1)
                ch.link(dve.tensor_tensor(mu[:, grp], rs0[:, grp], rs0[:, grp], ALU.mult))
                ch.link(dve.tensor_tensor(mu[:, grp], mu[:, grp], var[:, grp], ALU.mult))
                ch.link(dve.tensor_scalar(mu[:, grp], mu[:, grp], -0.5, 1.5, ALU.mult, ALU.add))
                ch.link(dve.tensor_tensor(rs0[:, grp], rs0[:, grp], mu[:, grp], ALU.mult))
                ch.link(dve.tensor_tensor(dot[:, grp], dot[:, grp], rs0[:, grp], ALU.mult))
                dve.tensor_scalar(score[:, grp], dot[:, grp], bsum[0:HALF, :], None, ALU.add).then_inc(s_score, 1)

            def compare(g, k):
                if k == 0:
                    dve.wait_ge(s_score_in[g], 16)
                n = GT * g + k
                row = all_scores[:, GT * HALF * g + N0 * (k // 2):GT * HALF * g + N0 * (k // 2 + 1)]
                dve.tensor_scalar(junk_above[:, k], row, score[:, n:n + 1], None, ALU.is_gt, ALU.add, accum_out=above[:, n:n + 1])
                ins = dve.scalar_tensor_tensor(junk_tied[:, k], row, score[:, n:n + 1], earlier[:, k % 2, :], ALU.is_equal, ALU.mult,
                                               accum_out=tied[:, n:n + 1])
                if k % (GT // 2) == GT // 2 - 1:
                    grp = slice(n + 1 - GT // 2, n + 1)
                    ch.link(ins)
                    ch.link(dve.tensor_tensor(above[:, grp], above[:, grp], tied[:, grp], ALU.add))
                    dve.tensor_tensor(rank[:, grp], above[:, grp], rowbase[0:HALF, grp], ALU.add).then_inc(s_rank, 1)

            means(0)
            stats(0)
            means(1)
            scores(0)
            stats(1)
            means(2)
            scores(1)
            stats(2)
            dve.wait_ge(s_const, 48)
            for k in range(GT):
                compare(0, k)
            means(3)
            stats(3)
            scores(2)
            ch.settle()

            def norm_rows(b, u):
                for h in range(2):
                    ins = dve.bn_stats(st1[:, h, :], H[:, bass.ds(2 * b + h, 1), :])
                ch.link(ins, apart=True)
                for h in range(2):
                    ins = dve.bn_aggr(mv1[:, u, h, :], st1[:, h, :])
                ins.then_inc(s_mv1, 1)

            def normalise(b, u):
                if not isinstance(b, int) or b >= 2:
                    wait_apart(dve, s_hx1, b - 1)
                dve.wait_ge(s_rs1, b + 1)
                for h in range(2):
                    ins = dve.tensor_scalar(xn1[:, u, h, :], H[:, bass.ds(2 * b + h, 1), :], mv1[:, u, h, 0:1], rs1[:, u, h:h + 1],
                                            ALU.subtract, ALU.mult)
                ins.then_inc(s_xn1, 1)

            def decayed(b, u, k):
                tile, heads = UNITS1[k]
                dve.wait_ge(s_sc1, NU1 * b + k + 1)
                src = SC1[k % 2][0:T, 0:2 * S]
                if tile == 1:
                    o = p1[:, u].rearrange("p (m e) t -> p m e t", e=2)[:, :, heads[0] % 2, :]
                    dve.tensor_tensor(o, src.rearrange("p (m t) -> p m t", m=4), decay[:, 0:T].unsqueeze(1).broadcast_to([T, 4, T]),
                                      ALU.mult).then_inc(s_p1, 1)
                else:
                    o = p0[:, u].rearrange("p (m e) t -> p m e t", e=2)[:, heads[0] // 2:heads[0] // 2 + 2, heads[0] % 2, :]
                    dve.tensor_tensor(o, src.rearrange("p (m t) -> p m t", m=2), decay[:].unsqueeze(1).broadcast_to([T, 2, S]),
                                      ALU.mult).then_inc(s_p1, 1)

            def close1(b, u, src=O1):
                dve.wait_ge(s_o1, b + 1)
                dve.wait_ge(s_hx1, b + 1)
                dve.tensor_tensor(H[:, bass.ds(2 * b, 2), :], src[0:T, 0:2 * D].rearrange("p (h d) -> p h d", h=2), hx1[:, u],
                                  ALU.add).then_inc(s_h1, 1)

            dve.wait_ge(s_w1, 16 * 6)
            dve.wait_ge(s_h0[0], 32)
            norm_rows(0, 0)
            scores(3)
            normalise(0, 0)
            norm_rows(1, 1)
            for k in range(GT // 2):
                compare(1, k)
            normalise(1, 1)
            for k in range(GT // 2, GT):
                compare(1, k)
            dve.wait_ge(s_gate, 1)
            ch.link(dve.tensor_scalar(gate[:], gate[:], 1.0, None, ALU.add))
            ch.link(dve.reciprocal(gate[:], gate[:]))
            for h in range(2):
                ins = dve.tensor_tensor(vg[:, h], SC1[h][0:T, :].rearrange("p (e d) -> p e d", e=NH),
                                        gate[:, h, :].unsqueeze(2).broadcast_to([T, NH, DK]), ALU.mult)
            ins.then_inc(s_kv, 1)
            ch.settle()

            def stats2(b, u):
                wait_apart(dve, s_h1, b + 1)
                for h in range(2):
                    ins = dve.bn_stats(st2[:, h, :], H[:, bass.ds(2 * b + h, 1), :])
                ch.link(ins, apart=True)
                for h in range(2):
                    ins = dve.bn_aggr(mv2[:, u, h, :], st2[:, h, :])
                ins.then_inc(s_mv2, 1)

            def rows2(b, u):
                dve.wait_ge(s_rs2, b + 1)
                for h in range(2):
                    ins = dve.tensor_scalar(M[:, bass.ds(2 * b + h, 1), :], H[:, bass.ds(2 * b + h, 1), :], mv2[:, u, h, 0:1],
                                            rs2[:, u, h:h + 1], ALU.subtract, ALU.mult)
                ins.then_inc(s_x3, 1)

            def body(b, u, prev, prev2, nxt2, g=None, half=0):
                for k in range(NU1):
                    decayed(b, u, k)
                if nxt2 is not None:
                    norm_rows(nxt2, u)
                if prev is not None:
                    close1(prev, 1 - u)
                    stats2(prev, 1 - u)
                if prev2 is not None:
                    rows2(prev2, u)
                if g is not None:
                    for k in range(GT // 2 * half, GT // 2 * (half + 1)):
                        compare(g, k)
                if nxt2 is not None:
                    normalise(nxt2, u)

            dve.wait_ge(s_h0[1], 32)
            body(0, 0, None, None, 2, 2, 0)
            body(1, 1, 0, None, 3, 2, 1)
            dve.wait_ge(s_h0[2], 32)
            body(2, 0, 1, 0, 4, 3, 0)
            body(3, 1, 2, 1, 5, 3, 1)
            dve.wait_ge(s_h0[3], 32)
            body(4, 0, 3, 2, 6)
            body(5, 1, 4, 3, 7)
            for q in range(4, 2 * NG):
                dve.wait_ge(s_h0[q], 32)
            ch.settle()
            with dve.Fori(3, B // 2 - 1) as i:
                ch.enter(i - 3, 4)
                body(2 * i, 0, 2 * i - 1, 2 * i - 2, 2 * i + 2)
                body(2 * i + 1, 1, 2 * i, 2 * i - 1, 2 * i + 3)
            ch.leave(B // 2 - 4)
            def rms_rows(b):
                dve.wait_ge(s_x3, b + 1)
                wait(dve, s_xTp2, b)
                for h in range(2):
                    n = bass.ds(2 * b + h, 1)
                    ins = dve.scalar_tensor_tensor(xr[:, h, :], M[:, n, :], rr2[:, n], norm1w[:], ALU.mult, ALU.mult)
                ins.then_inc(s_xr, 1)

            body(B - 2, 0, B - 3, B - 4, None)
            dve.wait_ge(s_w2, 16 * 6)
            dve.wait_ge(s_const2, 16 * 8)
            rms_rows(0)
            dve.tensor_copy(causal_b[:], causal[:])
            dve.tensor_copy(before_b[:], before[:])
            dve.tensor_copy(ident_b[:], ident[0:T, 0:T]).then_inc(s_w2b, 1)
            dve.tensor_copy(run[:], region[:])
            body(B - 1, 1, B - 2, B - 3, None)

            def rope(b, c):
                j, g = c // NKV, c % NKV
                dve.wait_ge(s_proj, NCH * b + c + 1)
                wait(dve, s_rot, NCH * b + c - 1)
                hw = HD // 2
                n = QKW // HD
                src = proj[0:T, g, 0:QKW].rearrange("p (n d) -> p n d", d=HD)
                tab = lambda t, lo, hi: t[:, j, lo:hi].unsqueeze(1).broadcast_to([T, n, hi - lo])
                dst = lambda t: t[:, c % 2].rearrange("p (n d) -> p n d", d=HD)
                dve.tensor_tensor(dst(rope_c), src, tab(cos, 0, HD), ALU.mult)
                dve.tensor_tensor(dst(rope_s)[:, :, 0:hw], src[:, :, hw:HD], tab(sin, 0, hw), ALU.mult)
                dve.tensor_tensor(dst(rope_s)[:, :, hw:HD], src[:, :, 0:hw], tab(sin, hw, HD), ALU.mult).then_inc(s_rope, 1)

            def peak(b, k):
                tile, heads = UNITS2[k]
                nh, w = len(heads), (T, S)[tile]
                dve.wait_ge(s_sc2, NU2 * b + k + 1)
                src = SC2[k % 2][0:T, 0:nh * w].rearrange("p (n t) -> p n t", n=nh)
                ch.link(dve.tensor_reduce(mx[:, k % 2, 0:nh], src, AX, ALU.max))
                wait(dve, s_pr, NU2 * b + k - 1)
                dve.tensor_scalar(shift[:, k % 2, 0:nh], mx[:, k % 2, 0:nh], -HD ** -0.5, None, ALU.mult).then_inc(s_shift, 1)

            def share(b, k):
                tile, heads = UNITS2[k]
                nh, w = len(heads), (T, S)[tile]
                dve.wait_ge(s_pr, NU2 * b + k + 1)
                ch.link(dve.reciprocal(rden[:, k % 2, 0:nh], den[:, k % 2, 0:nh]))
                p = pr[:, k % 2, 0:nh * w].rearrange("p (n t) -> p n t", n=nh)
                dve.tensor_tensor(p, p, rden[:, k % 2, 0:nh].unsqueeze(2).broadcast_to([T, nh, w]), ALU.mult).then_inc(s_pn, 1)

            def close2(b, j):
                n = bass.ds(2 * b + j, 1)
                dve.wait_ge(s_wo, 2 * b + j + 1)
                ch.link(dve.tensor_tensor(M[:, n, :], MISC[0:T, 0:D], M[:, n, :], ALU.add))
                dve.sem_inc(s_h2, 1)
                ch.link(dve.scalar_tensor_tensor(sqj[:, j, :], M[:, n, :], 1.0 / D, M[:, n, :], ALU.mult, ALU.mult, accum_out=ms[:, n]))
                if j:
                    dve.sem_inc(s_ms, 1)

            def rows3(b):
                wait_apart(dve, s_rr3, b + 1)
                wait_apart(dve, s_hadd, 2 * b + 2)
                wait(dve, s_send, b)
                wait(dve, s_mTp, b)
                for j in range(2):
                    n = bass.ds(2 * b + j, 1)
                    ins = dve.scalar_tensor_tensor(mrow[:, j, :], M[:, n, :], rr3[:, n], norm2w[:], ALU.mult, ALU.mult)
                ins.then_inc(s_mrow, 1)

            EW = [T, GR, E]
            wide = lambda t: t[:].unsqueeze(2).broadcast_to(EW)
            ranks = erank[0:T, :].unsqueeze(1).broadcast_to(EW)

            def choose(src, top, c_, one):
                ch.link(dve.tensor_reduce(top[:], src, AX, ALU.max))
                ch.link(dve.tensor_tensor(hit[:], src, wide(top), ALU.is_equal))
                ch.link(dve.tensor_tensor(hit[:], hit[:], ranks, ALU.mult))
                ch.link(dve.tensor_reduce(c_[:], hit[:], AX, ALU.max))
                ch.link(dve.tensor_tensor(one[:], ranks, wide(c_), ALU.is_equal))

            def router(g, gu, part):
                rows = lambda col: send[:, gu, :, col:col + 1]
                if part == 0:
                    dve.wait_ge(s_logit_in, 2 * g + 2)
                    choose(logit[:], top1, cm, sel1)
                if part == 1:
                    ch.link(dve.scalar_tensor_tensor(pick[:], sel1[:], MASKED, logit[:], ALU.mult, ALU.add))
                    dve.sem_inc(s_logit_used, 1)
                    choose(pick[:], top2, cm2, sel2)
                if part == 2:
                    dve.tensor_tensor(sel_b[:], sel1[:], sel2[:], ALU.add).then_inc(s_sel, 1)
                    dve.tensor_tensor(top2[:], top2[:], top1[:], ALU.subtract).then_inc(s_gap, 1)
                if part == 3:
                    dve.wait_ge(s_exp, g + 1)
                    ch.link(dve.tensor_scalar(w1[:], ex2[:], 1.0, None, ALU.add))
                    ch.link(dve.reciprocal(w1[:], w1[:]))
                    ch.link(dve.tensor_tensor(w2[:], ex2[:], w1[:], ALU.mult))
                    dve.tensor_tensor(rows(D + 2), w1[:].unsqueeze(2), w2[:].unsqueeze(2), ALU.subtract)
                    dve.tensor_copy(rows(D + 3), w2[:].unsqueeze(2))
                    dve.tensor_copy(rows(D + 1), cm[:].unsqueeze(2))
                    dve.tensor_copy(rows(D), outrow[:, bass.ds(GR * g, GR)].unsqueeze(2))
                if part == 4:
                    dve.wait_ge(s_cum, g + 1)
                    ch.link(dve.tensor_tensor(pos[:], MISC[0:T, 0:GR * E].rearrange("p (n e) -> p n e", e=E),
                                              run[0:T, :].unsqueeze(1).broadcast_to(EW), ALU.add))
                    ch.link(dve.tensor_tensor(run[:], MISC[:, GR * E:(GR + 1) * E], run[:], ALU.add))
                    dve.sem_inc(s_cum_read, 1)
                    ch.link(dve.tensor_tensor(sel1[:], sel1[:], pos[:], ALU.mult))
                    ch.link(dve.tensor_tensor(sel2[:], sel2[:], pos[:], ALU.mult))
                if part == 5:
                    ch.link(dve.tensor_reduce(slot_f[:, 0], sel1[:], AX, ALU.add))
                    ch.link(dve.tensor_reduce(slot_f[:, 1], sel2[:], AX, ALU.add))
                    dve.tensor_copy(slot[:, gu], slot_f[:]).then_inc(s_slot, 1)

            rope(0, 0)
            rope(0, 1)
            rope(0, 2)
            close1(B - 1, 1, TX1)
            stats2(B - 1, 1)

            def batch(b, u, prev, nxt, group=None, gu=0):
                if prev is not None:
                    close2(prev, 0)
                for k in range(NU2):
                    peak(b, k)
                    if k:
                        share(b, k - 1)
                    elif prev is not None:
                        share(prev, NU2 - 1)
                    if k in (0, 2, 3):
                        rope(b, {0: 3, 2: 4, 3: 5}[k])
                    if k in (4, 6, 7) and nxt is not None:
                        rope(nxt, {4: 0, 6: 1, 7: 2}[k])
                    if k == 1 and nxt is not None:
                        rms_rows(nxt)
                    if k == 5 and prev is not None:
                        close2(prev, 1)
                    if k == 8 and prev is not None:
                        rows3(prev)
                    if group is not None and k in (2, 3, 4, 6, 7, 8):
                        router(group, gu, {2: 0, 3: 1, 4: 2, 6: 4, 7: 3, 8: 5}[k])

            def pair(i, gu=0, first=False, last=False):
                batch(2 * i, 0, None if first else 2 * i - 1, 2 * i + 1)
                if first:
                    rows2(B - 2, 0)
                    rows2(B - 1, 1)
                batch(2 * i + 1, 1, 2 * i, None if last else 2 * i + 2, None if first else i - 1, gu)

            pair(0, first=True)
            pair(1, 0)
            pair(2, 1)
            ch.settle()
            with dve.Fori(1, NPAIR // 2 - 1) as i:
                ch.enter(i - 1, 4 * (2 * NU2 + 4) + 2 * 20)
                pair(2 * i + 1, 0)
                pair(2 * i + 2, 1)
            ch.leave(NPAIR // 2 - 2)
            pair(NPAIR - 1, 0, last=True)
            close2(B - 1, 0)
            share(B - 1, NU2 - 1)
            close2(B - 1, 1)
            rows3(B - 1)
            for part in (0, 1, 2, 4, 3, 5):
                router(NPAIR - 1, 1, part)

            ch.link(dve.tensor_copy(cnt_i[:], run[:]))
            dve.sem_inc(s_count, 1)
            ch.link(dve.tensor_tensor(til[:], run[:], region[:], ALU.subtract))
            ch.link(dve.tensor_scalar(til_i[:], til[:], float(MT - 1), None, ALU.add))
            ch.link(dve.tensor_scalar(til_i[:], til_i[:], MT.bit_length() - 1, None, ALU.arith_shift_right))
            ch.link(dve.tensor_copy(til[:], til_i[:]))
            ends, spare, step = til, end_a, 1
            while step < E:
                dve.tensor_copy(spare[:, 0:step], ends[:, 0:step])
                ch.link(dve.tensor_tensor(spare[:, step:E], ends[:, step:E], ends[:, 0:E - step], ALU.add))
                ends, spare, step = spare, (end_b if spare is end_a else end_a), 2 * step
            TW = [MT, NMT, E]
            ch.link(dve.tensor_tensor(past[:], tileno[:].unsqueeze(2).broadcast_to(TW), ends[:].unsqueeze(1).broadcast_to(TW), ALU.is_ge))
            ch.link(dve.tensor_reduce(texp_f[:], past[:], AX, ALU.add))
            dve.tensor_scalar(rexp[:], texp_f[:], -1.0, float(E), ALU.mult, ALU.add)
            dve.tensor_scalar(texp[:], texp_f[0:1, :], float(E - 1), None, ALU.min)
            ch.link(dve.tensor_scalar(need_f[:], texp_f[0:1, 0:NX], NEARLY - 0.5, float(WE_ALL - WE_EARLY), ALU.is_ge, ALU.mult))
            dve.tensor_scalar(tneed[:], need_f[:], float(WE_EARLY), None, ALU.add)
            ch.link(dve.tensor_scalar(skip[:], til[:], -float(MT), float(CAP), ALU.mult, ALU.add))
            ch.link(dve.tensor_tensor(jump[:], past[:], skip[:].unsqueeze(1).broadcast_to(TW), ALU.mult))
            ch.link(dve.tensor_reduce(tstart_f[:], jump[:], AX, ALU.add))
            ch.link(dve.scalar_tensor_tensor(tstart_f[:], tileno[:], float(MT), tstart_f[:], ALU.mult, ALU.add))
            dve.tensor_scalar(tstart[:], tstart_f[0:1, :], float(E * CAP), None, ALU.min).then_inc(s_tables, 1)


            def hidden(k, u):
                dve.wait_ge(s_sg, k + 1)
                dve.wait_ge(s_up, k + 1)
                dve.tensor_tensor(hb[:, u], UP[u][:, 0:FF], sg[:, u], ALU.mult).then_inc(s_h, 1)

            def result(k, u, slot):
                row = xg[:, slot]
                ch.link(dve.tensor_scalar(wv_[:, u, 0:1], row[:, D + 1:D + 2], rexp[:, bass.ds(k, 1)], row[:, D + 2:D + 3],
                                          ALU.is_equal, ALU.mult))
                ch.link(dve.tensor_tensor(wv_[:, u, 1:2], wv_[:, u, 0:1], row[:, D + 3:D + 4], ALU.add))
                wait(dve, s_add, 16 * (k - 1))
                dve.wait_ge(s_dn, k + 1)
                dve.tensor_scalar(ys[:, u], bank[2][:, 0:D], wv_[:, u, 1:2], None, ALU.mult).then_inc(s_y, 1)

            def tile(k, u, slot, last=False):
                result(k, u, slot)
                if not last:
                    hidden(k + 1, 1 - u)

            hidden(0, 0)
            for k in range(NX):
                tile(k, k % 2, k)
            ch.settle()
            with dve.Fori(1, NMT // NX - 1) as i:
                ch.enter(i - 1, 2 * NX)
                for r in range(NX):
                    tile(NX * i + r, r % 2, r)
            ch.leave(NMT // NX - 2)
            for k in range(NMT - NX, NMT):
                tile(k, k % 2, k % NX, k == NMT - 1)

        @block.tensor
        def _(pe):
            pe.wait_ge(s_const, 48)
            for g in range(NG):
                pe.wait_ge(s_score, g + 1)
                pe.transpose(bank[g][0:GT, 0:HALF], score[:, GT * g:GT * (g + 1)],
                             ident[0:HALF, 0:HALF]).then_inc(s_score_tp, 1)
            pe.wait_ge(s_score_t, NG)
            pe.wait_ge(s_w1, 16 * 6)

            def transpose_x(b, u):
                pe.wait_ge(s_xn1, b + 1)
                wait(pe, s_xT1, b)
                for c in range(2):
                    for h in range(2):
                        ins = pe.transpose(TX1[0:C, c * S + h * T:c * S + h * T + T], xn1[:, u, h, c * C:(c + 1) * C], ident[0:T, 0:T])
                ins.then_inc(s_xTp1, 1)

            def project(w, x, dst, m0):
                for m in range(2):
                    for c in range(2):
                        ins = pe.matmul(dst[:, m * S:(m + 1) * S], w[:, c, 128 * (m0 + m):128 * (m0 + m + 1)], x[:, c, :],
                                        start=c == 0, stop=c == 1)
                return ins

            def queries(b, u, h):
                pe.wait_ge(s_xT1, b + 1)
                wait(pe, s_q1, 2 * b + h - 1 if isinstance(b, int) else 2 * (b - 1) + h + 1)
                if isinstance(b, int) and b == 0:
                    pe.wait_ge(s_kv, h + 1)
                project(wq, xT1[:, u], Q1[h], 2 * h).then_inc(s_qp1, 1)

            def scores(b, u, k):
                tile, heads = UNITS1[k]
                if k % 2 == 0 or True:
                    pe.wait_ge(s_q1, 2 * b + (2 if k < 2 or k >= 4 else 1))
                if isinstance(b, int) and b == 0 and k < 2:
                    pe.wait_ge(s_kv, 3)
                else:
                    pe.wait_ge(s_p1, NU1 * b + k - 1)
                w = S if tile == 0 else T
                for n, hd in enumerate(heads):
                    base = 64 * (hd % 2)
                    ins = pe.matmul(SC1[k % 2][0:T, n * w:(n + 1) * w], kT1[base:base + DK, hd // 2, tile * T:tile * T + T],
                                    qT1[base:base + DK, u, hd // 2, S - w:S], start=True, stop=True)
                ins.then_inc(s_sc1, 1)

            def retrieve(b, u, h):
                pe.wait_ge(s_p1, NU1 * b + (4 if h == 0 else 6))
                wait(pe, s_r1, 2 * b + h - 1 if isinstance(b, int) else 2 * (b - 1) + h + 1)
                for m in range(2):
                    o = [R1[h][DK * e:DK * e + DK, m * S:(m + 1) * S] for e in range(2)]
                    hd = 4 * h + 2 * m
                    for e in range(2):
                        pe.matmul(o[e], vg[:, 0, hd + e, :], p0[:, u, hd + e, :], start=True, stop=False, skip_group_check=True)
                    for e in range(2):
                        ins = pe.matmul(o[e][:, T:S], vg[:, 1, hd + e, :], p1[:, u, hd + e, :], start=False, stop=True,
                                        skip_group_check=True)
                ins.then_inc(s_rp1, 1)

            def output(b, u, dst=O1):
                pe.wait_ge(s_r1, 2 * b + 2)
                wait(pe, s_h1, b)
                for h in range(2):
                    for m in range(4):
                        ins = pe.matmul(dst[0:T, h * D:(h + 1) * D], rT1[:, u, m, h * T:(h + 1) * T], wo[:, m, :],
                                        start=m == 0, stop=m == 3)
                ins.then_inc(s_o1, 1)

            transpose_x(0, 0)
            pe.wait_ge(s_xT1, 1)
            for h in range(2):
                project(wk, xT1[:, 0], Q1[h], 2 * h).then_inc(s_kvg, 1)
            for h in range(2):
                for c in range(2):
                    pe.matmul(SC1[h][0:T, :], xT1[:, 0, c, h * T:(h + 1) * T], wv[:, c, :], start=c == 0, stop=c == 1)
            for h in range(2):
                for c in range(2):
                    ins = pe.matmul(O1[0:T, h * NH:(h + 1) * NH], xT1[:, 0, c, h * T:(h + 1) * T], wg[:, c, :], start=c == 0, stop=c == 1)
            ins.then_inc(s_kvg, 1)
            for h in range(2):
                queries(0, 0, h)

            def body(b, u, nxt):
                for k in range(4):
                    scores(b, u, k)
                if nxt is not None:
                    transpose_x(nxt, 1 - u)
                scores(b, u, 4)
                scores(b, u, 5)
                retrieve(b, u, 0)
                if nxt is not None:
                    queries(nxt, 1 - u, 0)
                retrieve(b, u, 1)
                if nxt is not None:
                    queries(nxt, 1 - u, 1)
                    output(b, u)

            body(0, 0, 1)
            with pe.Fori(0, B // 2 - 1) as i:
                body(2 * i + 1, 1, 2 * i + 2)
                body(2 * i + 2, 0, 2 * i + 3)


            def transpose_xr(b):
                pe.wait_ge(s_xr, b + 1)
                if not isinstance(b, int) or b >= 3:
                    pe.wait_ge(s_logit_in, b - 2)
                elif b == 2:
                    pe.wait_ge(s_h2, 1)
                for c in range(2):
                    for h in range(2):
                        ins = pe.transpose(MISC[0:C, c * S + h * T:c * S + h * T + T], xr[:, h, c * C:(c + 1) * C], ident[0:T, 0:T])
                ins.then_inc(s_xTp2, 1)

            def project2(b, u, c):
                j, g = c // NKV, c % NKV
                pe.wait_ge(s_xrT, b + 1)
                wait(pe, s_qkT, NCH * b + c - 2)
                for k in range(2):
                    ins = pe.matmul(proj[0:T, g, 0:GW], xrT[:, u, k, j * T:(j + 1) * T], wqkv[:, k, g, :], start=k == 0, stop=k == 1)
                ins.then_inc(s_proj, 1)

            def transpose_qk(b, c):
                pe.wait_ge(s_rot, NCH * b + c + 1)
                pe.wait_ge(s_val, NCH * b + c + 1)
                for k in range(3):
                    ins = pe.transpose(proj[:, c % NKV, k * T:(k + 1) * T], rot[:, c % 2, 128 * k:128 * (k + 1)], ident[0:T, 0:T])
                ins.then_inc(s_qkTp, 1)

            def scores2(b, u, k):
                tile, heads = UNITS2[k]
                nh, w = len(heads), (T, S)[tile]
                pe.wait_ge(s_qkT, NCH * b + NKV * tile + heads[-1] // 4 + 1)
                wait(pe, s_pr, NU2 * b + k - 1)
                dst = SC2[k % 2][0:T, 0:nh * w].rearrange("p (n t) -> p n t", n=nh)
                pe.matmul(dst[:, :, w - T:w], ident_b[:], causal_b[:].unsqueeze(1).broadcast_to([T, nh, T]),
                          start=True, stop=False, skip_group_check=True)
                for n, hd in enumerate(heads):
                    base, g, m = HD * (hd % 2), hd // 4, (hd % 4) // 2
                    ins = pe.matmul(dst[:, n, :], qkT[base:base + HD, u, g, m, tile * T:tile * T + T], qkT[base:base + HD, u, g, 2, 0:w],
                                    start=False, stop=n == nh - 1, skip_group_check=True)
                ins.then_inc(s_sc2, 1)

            def transpose_p(b, k):
                tile, heads = UNITS2[k]
                pe.wait_ge(s_pn, NU2 * b + k + 1)
                wait(pe, s_pT, NU2 * b + k)
                for n in range(len(heads) * (tile + 1)):
                    ins = pe.transpose(PT2[0:T, n * T:(n + 1) * T], pr[:, k % 2, n * T:(n + 1) * T], ident[0:T, 0:T])
                ins.then_inc(s_tp, 1)

            def weigh(b, u, p):
                tile, heads = UNITS2[2 * p]
                pe.wait_ge(s_pT, NU2 * b + 2 * p + 2)
                wait(pe, s_oT, NPU * b + p)
                for n, hd in enumerate(heads):
                    for blk in range(tile + 1):
                        q = n * (tile + 1) + blk
                        for e in range(2):
                            ins = pe.matmul(O2[HD * e:HD * e + HD, n * T:(n + 1) * T], val[:, u, blk, hd // 4, :],
                                            pT[:, buffer4(u, 2 * p + e), q * T:(q + 1) * T], start=blk == 0, stop=blk == tile,
                                            skip_group_check=True)
                ins.then_inc(s_pv, 1)

            def output2(b, j, group=None):
                pe.wait_ge(s_oT, NPU * b + (2, 5)[j])
                if group is not None:
                    pe.wait_ge(s_cum_read, group + 1)
                elif j == 0:
                    if not isinstance(b, int) or b:
                        pe.wait_ge(s_h2, 2 * b)
                    else:
                        pe.wait_ge(s_xrT, 2)
                elif isinstance(b, int) and b >= B - 2:
                    pe.wait_ge(s_logit_in, b)
                else:
                    pe.wait_ge(s_xrT, b + 3)
                for m in range(6):
                    ins = pe.matmul(MISC[0:T, 0:D], oT[:, j, m, :], wout[:, m, :], start=m == 0, stop=m == 5)
                ins.then_inc(s_wo, 1)

            def transpose_m(b):
                pe.wait_ge(s_mrow, b + 1)
                pe.wait_ge(s_h2, 2 * b + 3 if not isinstance(b, int) or b < B - 1 else 2 * B)
                wait(pe, s_mT, b)
                for c in range(2):
                    for h in range(2):
                        ins = pe.transpose(MISC[0:C, c * S + h * T:c * S + h * T + T], mrow[:, h, c * C:(c + 1) * C], ident[0:T, 0:T])
                ins.then_inc(s_mTp, 1)

            def route(b):
                pe.wait_ge(s_mT, b + 1)
                for h in range(2):
                    for c in range(2):
                        ins = pe.matmul(MISC[0:T, h * E:(h + 1) * E], mT[:, c, h * T:(h + 1) * T], wr[:, c, :], start=c == 0, stop=c == 1)
                ins.then_inc(s_logit, 1)

            def count(g):
                pe.wait_ge(s_sel, g + 1)
                pe.wait_ge(s_h2, 4 * g + 6 if not isinstance(g, int) or g < NPAIR - 1 else 2 * B)
                cum, tot, flat_sel = MISC[0:T, 0:GR * E], MISC[:, GR * E:(GR + 1) * E], sel_b[:].rearrange("p n e -> p (n e)")
                pe.matmul(cum, before_b[:], flat_sel, start=True, stop=False, skip_group_check=True)
                for j in range(1, GR):
                    pe.matmul(cum[:, j * E:GR * E], ones_b[:, 0:T], flat_sel[:, 0:(GR - j) * E], start=False, stop=j == GR - 1,
                              skip_group_check=True)
                for j in range(GR):
                    ins = pe.matmul(tot, ones_b[:], flat_sel[:, j * E:(j + 1) * E], start=j == 0, stop=j == GR - 1, skip_group_check=True)
                ins.then_inc(s_cum, 1)

            def batch(b, u, prev, prev2, nxt, group=None):
                for k in range(NU2):
                    scores2(b, u, k)
                    if k in (2, 4, 5):
                        transpose_qk(b, {2: 3, 4: 4, 5: 5}[k])
                    if k in (6, 8, 9) and nxt is not None:
                        transpose_qk(nxt, {6: 0, 8: 1, 9: 2}[k])
                    if k in (0, 2, 3):
                        project2(b, u, {0: 3, 2: 4, 3: 5}[k])
                    if k in (4, 6, 7) and nxt is not None:
                        project2(nxt, 1 - u, {4: 0, 6: 1, 7: 2}[k])
                    if k == 0 and prev2 is not None:
                        transpose_m(prev2)
                    if k == 1 and prev2 is not None:
                        route(prev2)
                    if k == 2 and nxt is not None:
                        transpose_xr(nxt)
                    if k == 5 and prev is not None:
                        output2(prev, 1)
                    if k == 6 and group is not None:
                        count(group)
                    if k == 9:
                        output2(b, 0, group)
                    if k < 2:
                        if prev is not None:
                            transpose_p(prev, NU2 - 2 + k)
                    else:
                        transpose_p(b, k - 2)
                    if k in (0, 2) and prev is not None:
                        weigh(prev, 1 - u, {0: 3, 2: 4}[k])
                    if k in (4, 6, 8):
                        weigh(b, u, k // 2 - 2)

            def pair(i, first=False, last=False):
                batch(2 * i, 0, None if first else 2 * i - 1, None if first else 2 * i - 2, 2 * i + 1)
                batch(2 * i + 1, 1, 2 * i, None if first else 2 * i - 1, None if last else 2 * i + 2, None if first else i - 1)

            body(B - 1, 1, None)
            pe.wait_ge(s_w2b, 2)
            pe.wait_ge(s_q1, 2 * B)
            transpose_xr(0)
            pe.wait_ge(s_r1, 2 * B)
            project2(0, 0, 0)
            project2(0, 0, 1)
            pe.wait_ge(s_h1, B - 1)
            project2(0, 0, 2)
            output(B - 1, 1, TX1)
            transpose_qk(0, 0)
            transpose_qk(0, 1)
            transpose_qk(0, 2)
            pair(0, first=True)
            pair(1)
            with pe.Fori(2, NPAIR - 1) as i:
                pair(i)
            pair(NPAIR - 1, last=True)
            transpose_m(B - 2)
            transpose_p(B - 1, NU2 - 2)
            weigh(B - 1, 1, NPU - 2)
            route(B - 2)
            transpose_p(B - 1, NU2 - 1)
            weigh(B - 1, 1, NPU - 1)
            output2(B - 1, 1)
            transpose_m(B - 1)
            route(B - 1)
            count(NPAIR - 1)

            def transpose_rows(k, u, slot, turn):
                pe.wait_ge(s_xg[slot], 16 * (turn + 1))
                wait(pe, s_xgT, k)
                for c in range(2):
                    ins = pe.transpose(bank[0][0:C, c * MT:(c + 1) * MT], xg[:, slot, c * C:(c + 1) * C], ident[:])
                ins.then_inc(s_xgTp, 1)

            def expert_of(k):
                return pe.value_load(texp[0:1, bass.ds(k, 1)], min_val=0, max_val=E - 1)

            def weights_of(k):
                return pe.value_load(tneed[0:1, k:k + 1], min_val=WE_EARLY, max_val=WE_ALL)

            def up(k, u, e, part, need=None):
                pe.wait_ge(s_xgT, k + 1)
                if need is not None:
                    pe.wait_ge(s_expert_w, need)
                dst = (GATE, UP)[part][u]
                for c in range(2):
                    ins = pe.matmul(dst[:, 0:FF], xgT[:, u, c, :], wgu[:, bass.ds(e * (4 * FF) + (2 * c + part) * FF, FF)],
                                    start=c == 0, stop=c == 1)
                ins.then_inc((s_gated, s_up)[part], 1)

            def transpose_h(k, u):
                pe.wait_ge(s_h, k + 1)
                for m in range(3):
                    ins = pe.transpose(bank[1][:, m * MT:(m + 1) * MT], hb[:, u, m * MT:(m + 1) * MT], ident[:])
                ins.then_inc(s_hTp, 1)

            def down(k, u, e):
                pe.wait_ge(s_hT, k + 1)
                wait(pe, s_y, k)
                for m in range(3):
                    ins = pe.matmul(bank[2][:, 0:D], hT[:, u, m, :], wdn[:, bass.ds(e * (3 * D) + m * D, D)], start=m == 0, stop=m == 2)
                ins.then_inc(s_dn, 1)

            def tile(k, u, slot, turn, last=0):
                if last < 2:
                    need = weights_of(k + 1) if isinstance(k, int) and k + 1 < NX else None
                    e_next = expert_of(k + 1)
                    up(k + 1, 1 - u, e_next, 0, need)
                transpose_h(k, u)
                if last < 2:
                    up(k + 1, 1 - u, e_next, 1)
                if last < 1:
                    transpose_rows(k + 2, u, slot, turn)
                down(k, u, expert_of(k))

            pe.wait_ge(s_tables, 1)
            pe.wait_ge(s_expert_w, WE_EARLY)
            transpose_rows(0, 0, 0, 0)
            transpose_rows(1, 1, 1, 0)
            need = weights_of(0)
            e0 = expert_of(0)
            up(0, 0, e0, 0, need)
            up(0, 0, e0, 1)
            for k in range(NX - 1):
                tile(k, k % 2, (k + 2) % NX, (k + 2) // NX)
            pe.wait_ge(s_expert_w, WE_ALL)
            tile(NX - 1, (NX - 1) % 2, 1, 1)
            with pe.Fori(1, NMT // NX - 1) as i:
                for r in range(NX):
                    tile(NX * i + r, r % 2, (r + 2) % NX, i + (r + 2) // NX)
            for k in range(NMT - NX, NMT):
                tile(k, k % 2, (k + 2) % NX, (k + 2) // NX, max(0, k - (NMT - 3)))


def host_layout(inputs):
    f = {k: np.asarray(v) for k, v in inputs.items()}
    rows = lambda v: np.ascontiguousarray(np.broadcast_to(v.reshape(1, -1), (128, v.size)))
    chunk = lambda w, k: np.ascontiguousarray(w.reshape(w.shape[0] // k, k, w.shape[1]).transpose(1, 0, 2))
    a = {"x": f["x"], "gamma": rows(f["L0_tok_gamma"]), "beta": rows(f["L0_tok_beta"]), "tokw": rows(f["L0_tok_w"]),
         "tokb": rows(f["L0_tok_b"]),
         "wq": chunk(f["L0_attn_w_query"].T, C), "wk": chunk(f["L0_attn_w_key"].T, C), "wv": chunk(f["L0_attn_w_value"].T, C),
         "wg": chunk(f["L0_attn_w_gate"].T, C), "wo": chunk(f["L0_attn_w_out"].T, 128)}
    w = f["L0_ffn_w_qkv"]
    split = lambda v: v.reshape(D, -1, HD // 2, 2).transpose(0, 1, 3, 2)
    q = split(w[:, :NQ * HD]).reshape(D, NKV, NQ // NKV * HD)
    k = split(w[:, NQ * HD:(NQ + NKV) * HD]).reshape(D, NKV, HD)
    v = w[:, (NQ + NKV) * HD:].reshape(D, NKV, HD)
    a["wqkv"] = chunk(np.concatenate([q, k, v], 2).reshape(D, NKV * GW), C).reshape(C, 2, NKV, GW)
    a["wout"] = chunk(f["L0_ffn_w_out"], 128)
    a["norm2w"] = rows(f["L0_ffn_norm2_w"])[:T]
    a["wr"] = chunk(f["L0_ffn_w_router"], C)
    a["wgu"] = f["L0_ffn_w_gate_up"].reshape(E, 2, C, 2 * FF).transpose(2, 0, 1, 3).reshape(C, E * 4 * FF)
    a["wdn"] = f["L0_ffn_w_down"].reshape(E, 3, FF // 3, D).transpose(2, 0, 1, 3).reshape(FF // 3, E * 3 * D)
    a["norm1w"] = rows(f["L0_ffn_norm1_w"])[:T]
    a.update(constants())
    return a


def kernel(**inputs):
    import concourse.bacc as _bacc
    from concourse import mybir as _mybir
    from concourse.bass_utils import run_bass_kernel_spmd as _run

    nc = _bacc.Bacc("TRN2", target_bir_lowering=False, num_devices=1)
    arrays, args = {}, {}
    for name, v in host_layout(inputs).items():
        v = np.ascontiguousarray(v)
        arrays[f"in_{name}"] = v
        args[name] = nc.dram_tensor(f"in_{name}", v.shape, _mybir.dt.from_np(v.dtype), kind="ExternalInput").ap()
    out = nc.dram_tensor("out_0", (B, KEEP, D), _mybir.dt.float32, kind="ExternalOutput").ap()
    build(nc, args, out)
    r = _run(nc, [arrays], core_ids=[0])
    return r.results[0]["out_0"]
```
